# Optimizing a Trainium2 kernel written in Bass

```python
import numpy as np
import jax
import jax.numpy as jnp

def _softmax(x, axis=-1):
    return jax.nn.softmax(x, axis=axis)
def _gelu(x):
    return jax.nn.gelu(x, approximate=True)
def _silu(x):
    return jax.nn.silu(x)
def _sigmoid(x):
    return jax.nn.sigmoid(x)
def _layernorm(x, axis=-1, eps=1e-5):
    m = jnp.mean(x, axis=axis, keepdims=True)
    v = jnp.var(x, axis=axis, keepdims=True)
    return (x - m) / jnp.sqrt(v + eps)
def _scatter_add(tgt, idx, src, axis=0):
    return tgt.at[idx].add(src)
def _segment_sum(src, seg, n):
    return jax.ops.segment_sum(src, seg, n)

kernel_name = 'mk_conv_seq_d2_conv_nchw256_11f38f'

def setup_inputs(seed: int = 0):
    np.random.seed(seed)
    _w = jnp.asarray
    def _rec_inputs():
        import jax
        import jax.numpy as jnp
        _gk = jax.random.key(seed)
        x = 0.0006394 + 0.9997 * jax.random.normal(jax.random.fold_in(_gk, 1), (8, 256, 32, 32), jnp.float32)
        return x
    x = _rec_inputs()
    def _L0_conv_setup():
        import jax, jax.numpy as jnp
        import numpy as np
        from jax import lax
        C = 256
        NH = 4
        KD = 32
        HD = 64
        SCALE = KD ** (-0.5)
        PS = 8
        BN_EPS = 1e-05
        LN_EPS = 1e-06

        def _conv1x1(x, w):
            return jnp.einsum('oi,bihw->bohw', w, x)

        def _dwconv3(x, w):
            return lax.conv_general_dilated(x, w, window_strides=(1, 1), padding=((1, 1), (1, 1)), feature_group_count=x.shape[1], dimension_numbers=('NCHW', 'OIHW', 'NCHW'))

        def _bn(x, g, b, m, v):
            s = g * lax.rsqrt(v + BN_EPS)
            return x * s[:, None, None] + (b - m * s)[:, None, None]

        def _ln(x, w, b):
            r = lax.rsqrt(jnp.mean(x * x, axis=1, keepdims=True) + LN_EPS)
            return x * r * w[:, None, None] + b[:, None, None]

        def _attention(x, qkv_w, qkv_g, qkv_b, qkv_m, qkv_v, pe_w, pe_g, pe_b, pe_m, pe_v, proj_w, proj_g, proj_b, proj_m, proj_v):
            B, Cc, H, W = x.shape
            N = H * W
            qkv = _bn(_conv1x1(x, qkv_w), qkv_g, qkv_b, qkv_m, qkv_v)
            qkv = qkv.reshape(B, NH, 2 * KD + HD, N)
            q, k, v = (qkv[:, :, :KD], qkv[:, :, KD:2 * KD], qkv[:, :, 2 * KD:])
            attn = jnp.einsum('bhkn,bhkm->bhnm', q, k) * SCALE
            attn = jax.nn.softmax(attn, axis=-1)
            out = jnp.einsum('bhdm,bhnm->bhdn', v, attn).reshape(B, Cc, H, W)
            v_img = v.reshape(B, Cc, H, W)
            pe = _bn(_dwconv3(v_img, pe_w), pe_g, pe_b, pe_m, pe_v)
            out = out + pe
            return _bn(_conv1x1(out, proj_w), proj_g, proj_b, proj_m, proj_v)

        def _edffn(x, pi_w, dw_w, fft_p, po_w):
            x = _conv1x1(x, pi_w)
            x = _dwconv3(x, dw_w)
            hid = x.shape[1] // 2
            x1, x2 = (x[:, :hid], x[:, hid:])
            x = jax.nn.gelu(x1, approximate=False) * x2
            x = _conv1x1(x, po_w)
            B, Cc, H, W = x.shape
            h_n = (PS - H % PS) % PS
            w_n = (PS - W % PS) % PS
            if h_n or w_n:
                x = jnp.pad(x, ((0, 0), (0, 0), (0, h_n), (0, w_n)), mode='reflect')
            Hp, Wp = (H + h_n, W + w_n)
            gh, gw = (Hp // PS, Wp // PS)
            xp = x.reshape(B, Cc, gh, PS, gw, PS).transpose(0, 1, 2, 4, 3, 5)
            xf = jnp.fft.rfft2(xp) * fft_p
            xp = jnp.fft.irfft2(xf, s=(PS, PS))
            x = xp.transpose(0, 1, 2, 4, 3, 5).reshape(B, Cc, Hp, Wp)
            return x[:, :, :H, :W]

        def _forward(x, norm1_w, norm1_b, norm2_w, norm2_b, gamma1, gamma2, qkv_w, qkv_g, qkv_b, qkv_m, qkv_v, pe_w, pe_g, pe_b, pe_m, pe_v, proj_w, proj_g, proj_b, proj_m, proj_v, pi_w, dw_w, fft_p, po_w):
            a = _attention(_ln(x, norm1_w, norm1_b), qkv_w, qkv_g, qkv_b, qkv_m, qkv_v, pe_w, pe_g, pe_b, pe_m, pe_v, proj_w, proj_g, proj_b, proj_m, proj_v)
            x = x + gamma1 * a
            f = _edffn(_ln(x, norm2_w, norm2_b), pi_w, dw_w, fft_p, po_w)
            return x + gamma2 * f
        key = jax.random.key(seed)
        ks = iter(jax.random.split(key, 32))
        B, H, W = (8, 32, 32)
        HID = 2 * C

        def rn(shape, scale=1.0):
            return jax.random.normal(next(ks), shape, dtype=jnp.float32) * scale

        def bn_params(c):
            g = 1.0 + rn((c,), 0.1)
            b = rn((c,), 0.1)
            m = rn((c,), 0.1)
            v = 0.5 + jax.random.uniform(next(ks), (c,), dtype=jnp.float32)
            return (g, b, m, v)
        qkv_g, qkv_b, qkv_m, qkv_v = bn_params(C + 2 * NH * KD)
        pe_g, pe_b, pe_m, pe_v = bn_params(C)
        proj_g, proj_b, proj_m, proj_v = bn_params(C)
        return dict(x=rn((B, C, H, W)), norm1_w=jnp.ones((C,), jnp.float32), norm1_b=jnp.zeros((C,), jnp.float32), norm2_w=jnp.ones((C,), jnp.float32), norm2_b=jnp.zeros((C,), jnp.float32), gamma1=jnp.full((C, 1, 1), 0.5, jnp.float32), gamma2=jnp.full((C, 1, 1), 0.5, jnp.float32), qkv_w=rn((C + 2 * NH * KD, C), C ** (-0.5)), qkv_g=qkv_g, qkv_b=qkv_b, qkv_m=qkv_m, qkv_v=qkv_v, pe_w=rn((C, 1, 3, 3), 1.0 / 3.0), pe_g=pe_g, pe_b=pe_b, pe_m=pe_m, pe_v=pe_v, proj_w=rn((C, C), C ** (-0.5)), proj_g=proj_g, proj_b=proj_b, proj_m=proj_m, proj_v=proj_v, pi_w=rn((2 * HID, C), C ** (-0.5)), dw_w=rn((2 * HID, 1, 3, 3), 1.0 / 3.0), fft_p=rn((C, 1, 1, PS, PS // 2 + 1), 0.02), po_w=rn((C, HID), HID ** (-0.5)))
    _L0_conv_all = _L0_conv_setup()
    _L0_conv_in = {k: v for k, v in _L0_conv_all.items() if k in ('norm1_w', 'norm1_b', 'norm2_w', 'norm2_b', 'gamma1', 'gamma2', 'qkv_w', 'qkv_g', 'qkv_b', 'qkv_m', 'qkv_v', 'pe_w', 'pe_g', 'pe_b', 'pe_m', 'pe_v', 'proj_w', 'proj_g', 'proj_b', 'proj_m', 'proj_v', 'pi_w', 'dw_w', 'fft_p', 'po_w', )}
    del _L0_conv_all

    def _L1_conv_setup():
        import jax, jax.numpy as jnp
        import numpy as np
        B_, C_, H_, W_ = (8, 256, 32, 32)
        NL, DS, DI, DTR, K = (4, 16, 512, 16, 4)

        def _mamba(xs, lw, lb, iw, cw, cb, xw, dw, db, alog, dp, ow):
            mu = xs.mean(-1, keepdims=True)
            var = ((xs - mu) ** 2).mean(-1, keepdims=True)
            xn = (xs - mu) * jax.lax.rsqrt(var + 1e-05) * lw + lb
            xin, z = jnp.split(xn @ iw.T, 2, axis=-1)
            xc = jnp.swapaxes(xin, 1, 2)
            xc = jax.lax.conv_general_dilated(xc, cw[:, None, :], (1,), [(K - 1, 0)], dimension_numbers=('NCH', 'OIH', 'NCH'), feature_group_count=DI) + cb[None, :, None]
            xin = jax.nn.silu(jnp.swapaxes(xc, 1, 2))
            proj = xin @ xw.T
            dt = jax.nn.softplus(proj[..., :DTR] @ dw.T + db)
            Bm = proj[..., DTR:DTR + DS]
            Cm = proj[..., DTR + DS:]
            A = -jnp.exp(alog)

            def step(h, t):
                dt_t, b_t, c_t, x_t = t
                h = h * jnp.exp(dt_t[..., None] * A) + (dt_t * x_t)[..., None] * b_t[:, None, :]
                return (h, jnp.einsum('bdn,bn->bd', h, c_t))
            h0 = jnp.zeros((xs.shape[0], DI, DS), xs.dtype)
            ts = tuple((jnp.swapaxes(a, 0, 1) for a in (dt, Bm, Cm, xin)))
            _, ys = jax.lax.scan(step, h0, ts)
            y = jnp.swapaxes(ys, 0, 1) + xin * dp
            return y * jax.nn.silu(z) @ ow.T

        def _forward(x, ln_w, ln_b, in_proj_w, conv_w, conv_b, x_proj_w, dt_proj_w, dt_proj_b, A_log, D, out_proj_w, se_w1, se_b1, se_w2, se_b2, bn_w, bn_b):
            Bsz, C, H, W = x.shape
            residual = x
            xs = jnp.swapaxes(x.reshape(Bsz, C, H * W), 1, 2)
            for i in range(NL):
                xs = xs + _mamba(xs, ln_w[i], ln_b[i], in_proj_w[i], conv_w[i], conv_b[i], x_proj_w[i], dt_proj_w[i], dt_proj_b[i], A_log[i], D[i], out_proj_w[i])
            xo = jnp.swapaxes(xs, 1, 2).reshape(Bsz, C, H, W)
            g = xo.mean((2, 3))
            g = jax.nn.relu(g @ se_w1.T + se_b1)
            g = jax.nn.sigmoid(g @ se_w2.T + se_b2)
            y = xo * g[:, :, None, None] + residual
            mu = y.mean((0, 2, 3))
            var = ((y - mu[None, :, None, None]) ** 2).mean((0, 2, 3))
            return (y - mu[None, :, None, None]) * jax.lax.rsqrt(var + 1e-05)[None, :, None, None] * bn_w[None, :, None, None] + bn_b[None, :, None, None]
        key = jax.random.key(seed)
        ks = jax.random.split(key, 10)

        def rn(k, shape, sc):
            return jax.random.normal(k, shape, jnp.float32) * sc
        return {'x': jax.random.normal(ks[0], (B_, C_, H_, W_), jnp.float32), 'ln_w': jnp.ones((NL, C_), jnp.float32), 'ln_b': jnp.zeros((NL, C_), jnp.float32), 'in_proj_w': rn(ks[1], (NL, 2 * DI, C_), 0.02), 'conv_w': rn(ks[2], (NL, DI, K), 0.1), 'conv_b': jnp.zeros((NL, DI), jnp.float32), 'x_proj_w': rn(ks[3], (NL, DTR + 2 * DS, DI), 0.02), 'dt_proj_w': rn(ks[4], (NL, DI, DTR), 0.1), 'dt_proj_b': jnp.full((NL, DI), -4.0, jnp.float32), 'A_log': jnp.tile(jnp.log(jnp.arange(1, DS + 1, dtype=jnp.float32)), (NL, DI, 1)), 'D': jnp.ones((NL, DI), jnp.float32), 'out_proj_w': rn(ks[5], (NL, C_, DI), 0.02), 'se_w1': rn(ks[6], (C_ // 4, C_), 0.05), 'se_b1': jnp.zeros((C_ // 4,), jnp.float32), 'se_w2': rn(ks[7], (C_, C_ // 4), 0.05), 'se_b2': jnp.zeros((C_,), jnp.float32), 'bn_w': jnp.ones((C_,), jnp.float32), 'bn_b': jnp.zeros((C_,), jnp.float32)}
    _L1_conv_all = _L1_conv_setup()
    _L1_conv_in = {k: v for k, v in _L1_conv_all.items() if k in ('ln_w', 'ln_b', 'in_proj_w', 'conv_w', 'conv_b', 'x_proj_w', 'dt_proj_w', 'dt_proj_b', 'A_log', 'D', 'out_proj_w', 'se_w1', 'se_b1', 'se_w2', 'se_b2', 'bn_w', 'bn_b', )}
    del _L1_conv_all

    return {
        "x": x,
        "L0_conv_norm1_w": _L0_conv_in["norm1_w"],
        "L0_conv_norm1_b": _L0_conv_in["norm1_b"],
        "L0_conv_norm2_w": _L0_conv_in["norm2_w"],
        "L0_conv_norm2_b": _L0_conv_in["norm2_b"],
        "L0_conv_gamma1": _L0_conv_in["gamma1"],
        "L0_conv_gamma2": _L0_conv_in["gamma2"],
        "L0_conv_qkv_w": _L0_conv_in["qkv_w"],
        "L0_conv_qkv_g": _L0_conv_in["qkv_g"],
        "L0_conv_qkv_b": _L0_conv_in["qkv_b"],
        "L0_conv_qkv_m": _L0_conv_in["qkv_m"],
        "L0_conv_qkv_v": _L0_conv_in["qkv_v"],
        "L0_conv_pe_w": _L0_conv_in["pe_w"],
        "L0_conv_pe_g": _L0_conv_in["pe_g"],
        "L0_conv_pe_b": _L0_conv_in["pe_b"],
        "L0_conv_pe_m": _L0_conv_in["pe_m"],
        "L0_conv_pe_v": _L0_conv_in["pe_v"],
        "L0_conv_proj_w": _L0_conv_in["proj_w"],
        "L0_conv_proj_g": _L0_conv_in["proj_g"],
        "L0_conv_proj_b": _L0_conv_in["proj_b"],
        "L0_conv_proj_m": _L0_conv_in["proj_m"],
        "L0_conv_proj_v": _L0_conv_in["proj_v"],
        "L0_conv_pi_w": _L0_conv_in["pi_w"],
        "L0_conv_dw_w": _L0_conv_in["dw_w"],
        "L0_conv_fft_p": _L0_conv_in["fft_p"],
        "L0_conv_po_w": _L0_conv_in["po_w"],
        "L1_conv_ln_w": _L1_conv_in["ln_w"],
        "L1_conv_ln_b": _L1_conv_in["ln_b"],
        "L1_conv_in_proj_w": _L1_conv_in["in_proj_w"],
        "L1_conv_conv_w": _L1_conv_in["conv_w"],
        "L1_conv_conv_b": _L1_conv_in["conv_b"],
        "L1_conv_x_proj_w": _L1_conv_in["x_proj_w"],
        "L1_conv_dt_proj_w": _L1_conv_in["dt_proj_w"],
        "L1_conv_dt_proj_b": _L1_conv_in["dt_proj_b"],
        "L1_conv_A_log": _L1_conv_in["A_log"],
        "L1_conv_D": _L1_conv_in["D"],
        "L1_conv_out_proj_w": _L1_conv_in["out_proj_w"],
        "L1_conv_se_w1": _L1_conv_in["se_w1"],
        "L1_conv_se_b1": _L1_conv_in["se_b1"],
        "L1_conv_se_w2": _L1_conv_in["se_w2"],
        "L1_conv_se_b2": _L1_conv_in["se_b2"],
        "L1_conv_bn_w": _L1_conv_in["bn_w"],
        "L1_conv_bn_b": _L1_conv_in["bn_b"],
    }

def reference(x, L0_conv_norm1_w, L0_conv_norm1_b, L0_conv_norm2_w, L0_conv_norm2_b, L0_conv_gamma1, L0_conv_gamma2, L0_conv_qkv_w, L0_conv_qkv_g, L0_conv_qkv_b, L0_conv_qkv_m, L0_conv_qkv_v, L0_conv_pe_w, L0_conv_pe_g, L0_conv_pe_b, L0_conv_pe_m, L0_conv_pe_v, L0_conv_proj_w, L0_conv_proj_g, L0_conv_proj_b, L0_conv_proj_m, L0_conv_proj_v, L0_conv_pi_w, L0_conv_dw_w, L0_conv_fft_p, L0_conv_po_w, L1_conv_ln_w, L1_conv_ln_b, L1_conv_in_proj_w, L1_conv_conv_w, L1_conv_conv_b, L1_conv_x_proj_w, L1_conv_dt_proj_w, L1_conv_dt_proj_b, L1_conv_A_log, L1_conv_D, L1_conv_out_proj_w, L1_conv_se_w1, L1_conv_se_b1, L1_conv_se_w2, L1_conv_se_b2, L1_conv_bn_w, L1_conv_bn_b):
    import jax
    import jax.numpy as jnp
    def _L0_conv_ref(x, norm1_w, norm1_b, norm2_w, norm2_b, gamma1, gamma2, qkv_w, qkv_g, qkv_b, qkv_m, qkv_v, pe_w, pe_g, pe_b, pe_m, pe_v, proj_w, proj_g, proj_b, proj_m, proj_v, pi_w, dw_w, fft_p, po_w):
        import jax, jax.numpy as jnp
        import numpy as np
        from jax import lax
        C = 256
        NH = 4
        KD = 32
        HD = 64
        SCALE = KD ** (-0.5)
        PS = 8
        BN_EPS = 1e-05
        LN_EPS = 1e-06

        def _conv1x1(x, w):
            return jnp.einsum('oi,bihw->bohw', w, x)

        def _dwconv3(x, w):
            return lax.conv_general_dilated(x, w, window_strides=(1, 1), padding=((1, 1), (1, 1)), feature_group_count=x.shape[1], dimension_numbers=('NCHW', 'OIHW', 'NCHW'))

        def _bn(x, g, b, m, v):
            s = g * lax.rsqrt(v + BN_EPS)
            return x * s[:, None, None] + (b - m * s)[:, None, None]

        def _ln(x, w, b):
            r = lax.rsqrt(jnp.mean(x * x, axis=1, keepdims=True) + LN_EPS)
            return x * r * w[:, None, None] + b[:, None, None]

        def _attention(x, qkv_w, qkv_g, qkv_b, qkv_m, qkv_v, pe_w, pe_g, pe_b, pe_m, pe_v, proj_w, proj_g, proj_b, proj_m, proj_v):
            B, Cc, H, W = x.shape
            N = H * W
            qkv = _bn(_conv1x1(x, qkv_w), qkv_g, qkv_b, qkv_m, qkv_v)
            qkv = qkv.reshape(B, NH, 2 * KD + HD, N)
            q, k, v = (qkv[:, :, :KD], qkv[:, :, KD:2 * KD], qkv[:, :, 2 * KD:])
            attn = jnp.einsum('bhkn,bhkm->bhnm', q, k) * SCALE
            attn = jax.nn.softmax(attn, axis=-1)
            out = jnp.einsum('bhdm,bhnm->bhdn', v, attn).reshape(B, Cc, H, W)
            v_img = v.reshape(B, Cc, H, W)
            pe = _bn(_dwconv3(v_img, pe_w), pe_g, pe_b, pe_m, pe_v)
            out = out + pe
            return _bn(_conv1x1(out, proj_w), proj_g, proj_b, proj_m, proj_v)

        def _edffn(x, pi_w, dw_w, fft_p, po_w):
            x = _conv1x1(x, pi_w)
            x = _dwconv3(x, dw_w)
            hid = x.shape[1] // 2
            x1, x2 = (x[:, :hid], x[:, hid:])
            x = jax.nn.gelu(x1, approximate=False) * x2
            x = _conv1x1(x, po_w)
            B, Cc, H, W = x.shape
            h_n = (PS - H % PS) % PS
            w_n = (PS - W % PS) % PS
            if h_n or w_n:
                x = jnp.pad(x, ((0, 0), (0, 0), (0, h_n), (0, w_n)), mode='reflect')
            Hp, Wp = (H + h_n, W + w_n)
            gh, gw = (Hp // PS, Wp // PS)
            xp = x.reshape(B, Cc, gh, PS, gw, PS).transpose(0, 1, 2, 4, 3, 5)
            xf = jnp.fft.rfft2(xp) * fft_p
            xp = jnp.fft.irfft2(xf, s=(PS, PS))
            x = xp.transpose(0, 1, 2, 4, 3, 5).reshape(B, Cc, Hp, Wp)
            return x[:, :, :H, :W]

        def _forward(x, norm1_w, norm1_b, norm2_w, norm2_b, gamma1, gamma2, qkv_w, qkv_g, qkv_b, qkv_m, qkv_v, pe_w, pe_g, pe_b, pe_m, pe_v, proj_w, proj_g, proj_b, proj_m, proj_v, pi_w, dw_w, fft_p, po_w):
            a = _attention(_ln(x, norm1_w, norm1_b), qkv_w, qkv_g, qkv_b, qkv_m, qkv_v, pe_w, pe_g, pe_b, pe_m, pe_v, proj_w, proj_g, proj_b, proj_m, proj_v)
            x = x + gamma1 * a
            f = _edffn(_ln(x, norm2_w, norm2_b), pi_w, dw_w, fft_p, po_w)
            return x + gamma2 * f
        return _forward(x, norm1_w, norm1_b, norm2_w, norm2_b, gamma1, gamma2, qkv_w, qkv_g, qkv_b, qkv_m, qkv_v, pe_w, pe_g, pe_b, pe_m, pe_v, proj_w, proj_g, proj_b, proj_m, proj_v, pi_w, dw_w, fft_p, po_w)

    def _L1_conv_ref(x, ln_w, ln_b, in_proj_w, conv_w, conv_b, x_proj_w, dt_proj_w, dt_proj_b, A_log, D, out_proj_w, se_w1, se_b1, se_w2, se_b2, bn_w, bn_b):
        import jax, jax.numpy as jnp
        import numpy as np
        B_, C_, H_, W_ = (8, 256, 32, 32)
        NL, DS, DI, DTR, K = (4, 16, 512, 16, 4)

        def _mamba(xs, lw, lb, iw, cw, cb, xw, dw, db, alog, dp, ow):
            mu = xs.mean(-1, keepdims=True)
            var = ((xs - mu) ** 2).mean(-1, keepdims=True)
            xn = (xs - mu) * jax.lax.rsqrt(var + 1e-05) * lw + lb
            xin, z = jnp.split(xn @ iw.T, 2, axis=-1)
            xc = jnp.swapaxes(xin, 1, 2)
            xc = jax.lax.conv_general_dilated(xc, cw[:, None, :], (1,), [(K - 1, 0)], dimension_numbers=('NCH', 'OIH', 'NCH'), feature_group_count=DI) + cb[None, :, None]
            xin = jax.nn.silu(jnp.swapaxes(xc, 1, 2))
            proj = xin @ xw.T
            dt = jax.nn.softplus(proj[..., :DTR] @ dw.T + db)
            Bm = proj[..., DTR:DTR + DS]
            Cm = proj[..., DTR + DS:]
            A = -jnp.exp(alog)

            def step(h, t):
                dt_t, b_t, c_t, x_t = t
                h = h * jnp.exp(dt_t[..., None] * A) + (dt_t * x_t)[..., None] * b_t[:, None, :]
                return (h, jnp.einsum('bdn,bn->bd', h, c_t))
            h0 = jnp.zeros((xs.shape[0], DI, DS), xs.dtype)
            ts = tuple((jnp.swapaxes(a, 0, 1) for a in (dt, Bm, Cm, xin)))
            _, ys = jax.lax.scan(step, h0, ts)
            y = jnp.swapaxes(ys, 0, 1) + xin * dp
            return y * jax.nn.silu(z) @ ow.T

        def _forward(x, ln_w, ln_b, in_proj_w, conv_w, conv_b, x_proj_w, dt_proj_w, dt_proj_b, A_log, D, out_proj_w, se_w1, se_b1, se_w2, se_b2, bn_w, bn_b):
            Bsz, C, H, W = x.shape
            residual = x
            xs = jnp.swapaxes(x.reshape(Bsz, C, H * W), 1, 2)
            for i in range(NL):
                xs = xs + _mamba(xs, ln_w[i], ln_b[i], in_proj_w[i], conv_w[i], conv_b[i], x_proj_w[i], dt_proj_w[i], dt_proj_b[i], A_log[i], D[i], out_proj_w[i])
            xo = jnp.swapaxes(xs, 1, 2).reshape(Bsz, C, H, W)
            g = xo.mean((2, 3))
            g = jax.nn.relu(g @ se_w1.T + se_b1)
            g = jax.nn.sigmoid(g @ se_w2.T + se_b2)
            y = xo * g[:, :, None, None] + residual
            mu = y.mean((0, 2, 3))
            var = ((y - mu[None, :, None, None]) ** 2).mean((0, 2, 3))
            return (y - mu[None, :, None, None]) * jax.lax.rsqrt(var + 1e-05)[None, :, None, None] * bn_w[None, :, None, None] + bn_b[None, :, None, None]
        return _forward(x, ln_w, ln_b, in_proj_w, conv_w, conv_b, x_proj_w, dt_proj_w, dt_proj_b, A_log, D, out_proj_w, se_w1, se_b1, se_w2, se_b2, bn_w, bn_b)

    def _gn(v, G=32, eps=1e-5):
        B_, C_, H_, W_ = v.shape
        g = v.reshape(B_, G, C_ // G, H_, W_)
        m = jnp.mean(g, axis=(2, 3, 4), keepdims=True)
        s = jnp.var(g, axis=(2, 3, 4), keepdims=True)
        return ((g - m) / jnp.sqrt(s + eps)).reshape(v.shape)

    def _ln_c(v, eps=1e-6):
        m = jnp.mean(v, axis=1, keepdims=True)
        s = jnp.var(v, axis=1, keepdims=True)
        return (v - m) / jnp.sqrt(s + eps)

    def _ln_t(v, eps=1e-5):
        m = jnp.mean(v, axis=-1, keepdims=True)
        s = jnp.var(v, axis=-1, keepdims=True)
        return (v - m) / jnp.sqrt(s + eps)

    def _to_tokens(v):
        B_, C_, H_, W_ = v.shape
        return v.reshape(B_, C_, H_ * W_).transpose(0, 2, 1)
    def _from_tokens(t, like):
        B_, C_, H_, W_ = like.shape
        return t.transpose(0, 2, 1).reshape(B_, C_, H_, W_)

    x = _L0_conv_ref(x, L0_conv_norm1_w, L0_conv_norm1_b, L0_conv_norm2_w, L0_conv_norm2_b, L0_conv_gamma1, L0_conv_gamma2, L0_conv_qkv_w, L0_conv_qkv_g, L0_conv_qkv_b, L0_conv_qkv_m, L0_conv_qkv_v, L0_conv_pe_w, L0_conv_pe_g, L0_conv_pe_b, L0_conv_pe_m, L0_conv_pe_v, L0_conv_proj_w, L0_conv_proj_g, L0_conv_proj_b, L0_conv_proj_m, L0_conv_proj_v, L0_conv_pi_w, L0_conv_dw_w, L0_conv_fft_p, L0_conv_po_w)
    x = _L1_conv_ref(x, L1_conv_ln_w, L1_conv_ln_b, L1_conv_in_proj_w, L1_conv_conv_w, L1_conv_conv_b, L1_conv_x_proj_w, L1_conv_dt_proj_w, L1_conv_dt_proj_b, L1_conv_A_log, L1_conv_D, L1_conv_out_proj_w, L1_conv_se_w1, L1_conv_se_b1, L1_conv_se_w2, L1_conv_se_b2, L1_conv_bn_w, L1_conv_bn_b)
    return x


_drawn_inputs = setup_inputs


def setup_inputs(seed=0):
    import zlib

    import numpy as np

    out = dict(_drawn_inputs(seed))
    spreads = {'L0_conv_norm1_w': (1.0, 0.2),
     'L0_conv_norm1_b': (0.0, 0.775),
     'L0_conv_norm2_w': (1.0, 0.6),
     'L0_conv_norm2_b': (0.0, 0.8),
     'L0_conv_gamma1': (0.5, 0.2),
     'L0_conv_gamma2': (0.5, 0.6),
     'L1_conv_ln_w': (1.0, 0.6),
     'L1_conv_ln_b': (0.0, 0.8),
     'L1_conv_conv_b': (0.0, 0.8),
     'L1_conv_dt_proj_b': (-4.0, 0.6),
     'L1_conv_D': (1.0, 0.6),
     'L1_conv_se_b1': (0.0, 0.8),
     'L1_conv_se_b2': (0.0, 0.8),
     'L1_conv_bn_w': (1.0, 0.2),
     'L1_conv_bn_b': (0.0, 0.1)}
    factors = {'L0_conv_qkv_b': 5.348,
     'L0_conv_qkv_m': 5.334,
     'L0_conv_pe_b': 8.0,
     'L0_conv_pe_m': 8.0,
     'L0_conv_proj_b': 8.0,
     'L0_conv_proj_m': 8.0,
     'L0_conv_pi_w': 8.0,
     'L0_conv_dw_w': 8.0,
     'L0_conv_fft_p': 8.0,
     'L0_conv_po_w': 8.0,
     'L1_conv_in_proj_w': 8.0,
     'L1_conv_conv_w': 8.0,
     'L1_conv_x_proj_w': 8.0,
     'L1_conv_dt_proj_w': 8.0,
     'L1_conv_A_log': 8.0,
     'L1_conv_out_proj_w': 8.0,
     'L1_conv_se_w1': 8.0,
     'L1_conv_se_w2': 8.0}
    for name, (base, spread) in spreads.items():
        noise = np.random.default_rng([zlib.crc32(name.encode()), seed]).standard_normal(out[name].shape)
        drawn = base * np.exp(spread * noise) if base else spread * noise
        out[name] = jnp.asarray(drawn.astype(out[name].dtype))
    for name, factor in factors.items():
        out[name] = (out[name] * factor).astype(out[name].dtype)
    return out
```

```python
from contextlib import ExitStack

import numpy as np
import concourse.bass as bass
from concourse import mybir

P = 128
F32 = mybir.dt.float32
ALU = mybir.AluOpType
ACT = mybir.ActivationFunctionType

B, C, H, W = 8, 256, 32, 32
N = H * W
KT = C // P
NL, DS, DI, DTR, TAPS = 4, 16, 512, 16, 4
DT = DI // P
T = 512
TT = T // P
HALVES = N // T
IMAGES = NL * B
CHUNKS = IMAGES * HALVES
BROW = 32
SMALL = DT * TAPS + DT + DT * DS + 2 * KT
O_CW, O_CB = 0, DT * TAPS
O_AL = O_CB + DT
O_LW = O_AL + DT * DS
O_LB = O_LW + KT
LN_EPS = 1e-5


def need(eng, sem, per, k, n):
    v = per * k + n
    if isinstance(v, int) and v <= 0:
        return
    eng.wait_ge(sem, v)


NH, KD, HD = 4, 32, 64
SCALE = KD ** -0.5
HID = 2 * C
HT = HID // P
NT = N // P
PW = W + 2
PS_ = 8
RMS_EPS = 1e-6
BN_EPS = 1e-5
UNITS = NT * NH


def conv_block(nc, x_in, state, w, consts):
    ctx = ExitStack()
    with ctx:
        def sb(n, s):
            return ctx.enter_context(nc.sbuf_tensor("a_" + n, s, F32))

        def sem(n):
            return ctx.enter_context(nc.semaphore("a_" + n))

        ident = sb("ident", [P, P])
        ones_c = sb("ones_c", [P, P])
        ones = sb("ones", [P, P])
        dft = sb("dft", [P, P])
        idft = sb("idft", [P, P])
        fsel = sb("fsel", [40, P])
        fftp = sb("fftp", [40, C])
        filt = sb("filt", [P, C])
        wqkv = sb("wqkv", [P, KT, 4 * P])
        wproj = sb("wproj", [P, KT, C])
        wpi = sb("wpi", [P, KT, 2 * HID])
        wpo = sb("wpo", [P, HT, C])
        bn = sb("bn", [P, 4, 8])
        bns = sb("bns", [P, 6, 8])
        vec = sb("vec", [P, 6, KT])
        pew = sb("pew", [P, KT, 9])
        dww = sb("dww", [P, 2 * HT, 9])
        x = sb("x", [P, KT, N])
        xn = sb("xn", [P, KT, N])
        sq = sb("sq", [P, KT, N])
        lnv = sb("lnv", [P, 5, NT])
        dg = sb("dg", [P, NT, P])
        qk = sb("qk", [P, 2, N])
        vpad = sb("vpad", [P, KT, PW, PW])
        vt = sb("vt", [P, NT, C])
        cv = sb("cv", [P, KT, N])
        prob = sb("prob", [P, 2, N])
        probt = sb("probt", [P, 2, N])
        nmx = sb("nmx", [P, 2, UNITS])
        rsum = sb("rsum", [P, 2, UNITS])
        otok = sb("otok", [P, 2, C])
        x1 = sb("x1", [P, KT, N])
        hpad = sb("hpad", [P, 2, PW, PW])
        hcv = sb("hcv", [P, 2, N])
        gl = sb("gl", [P, N])
        g = sb("g", [P, HT, N])
        pt = sb("pt", [P, 4, C])
        zf = sb("zf", [P, 4, C])

        def pair(n):
            return ctx.enter_context(nc.psum_tensor("a_" + n, [P, N], F32))
        PP = [pair("p0"), pair("p1"), pair("p2"), pair("p3")]

        s_w, s_x, s_st = sem("weights"), sem("x_loaded"), sem("store_done")
        p_var, p_bc, p_qkv, p_vt, p_s, p_t, p_av, p_ot, p_pj, p_pi, p_po, p_dft, p_idft, p_filt = (sem("pe_" + n) for n in (
            "var", "bc", "qkv", "vt", "s", "t", "av", "ot", "pj", "pi", "po", "dft", "idft", "filt"))
        a_sq, a_rs, a_qkv, a_cv0, a_exp, a_pt, a_pj, a_pad, a_h0, a_gl, a_po, a_bn, a_vt, a_vc = (sem("act_" + n) for n in (
            "sq", "rs", "qkv", "cv0", "exp", "probt", "pj", "pad", "h0", "gelu", "po", "bn", "vt", "vc"))
        v_rs, v_dg, v_xh, v_xn, v_max, v_pt, v_on, v_o, v_cv, v_x1, v_h, v_g, v_zf, v_x2, v_bn, v_filt, v_zero, v_rc = (
            sem("dve_" + n) for n in (
                "rs", "dg", "xh", "xn", "max", "probt", "otok", "o", "cv", "x1", "h", "g", "zf", "x2", "bn", "filt", "zero", "rsum"))

        N_W = 17
        x_v = x_in.rearrange("b (k p) n -> b p k n", p=P)
        st_v = state.rearrange("i (k p) n -> i p k n", p=P)

        def inner(pad, t):
            return pad[:, t, 1:1 + H, 1:1 + W]

        def image(a):
            return a.rearrange("p (r c) -> p r c", c=W)

        block = ctx.enter_context(nc.Block())

        @block.sync
        def _(sp):
            for dst, name in ((ident[:], "ident"), (ones_c[:], "ones_c"), (ones[:], "ones"), (dft[:], "dft"), (idft[:], "idft"),
                              (fsel[:], "fsel")):
                sp.dma_start(dst, consts[name]).then_inc(s_w, 16)
            for dst, name in ((fftp[:], "fftp"), (wqkv[:], "qkv"), (wproj[:], "proj"), (wpi[:], "pi"), (wpo[:], "po"),
                              (bn[:], "bn"), (vec[:], "vec"), (pew[:], "pe"), (dww[:], "dw")):
                sp.dma_start(dst, w[name]).then_inc(s_w, 16)

            def image_io(b):
                need(sp, s_st, 16, b, 0)
                need(sp, v_x1, KT, b - 1, KT)
                sp.dma_start(x[:], x_v[b]).then_inc(s_x, 16)
                need(sp, v_x2, 4, b, 4)
                sp.dma_start(st_v[b], x1[:]).then_inc(s_st, 16)

            image_io(0)
            with sp.Fori(1, B) as b:
                image_io(b)
            sp.wait_ge(s_st, 16 * B)

        def norm_pe(pe, b, src, which, free0, free1):
            need(pe, a_sq, 2, b, which + 1)
            free0()
            for t in range(NT):
                for c in range(KT):
                    i = nc.tensor.matmul(PP[0][:, t:t + 1], sq[:, c, t * P:(t + 1) * P], ones_c[:, 0:1],
                                         start=(c == 0), stop=(c == KT - 1))
            i.then_inc(p_var, 1)
            need(pe, v_dg, 2, b, which + 1)
            free1()
            for hf in range(2):
                i = nc.tensor.matmul(PP[1][:, hf * 512:(hf + 1) * 512], ones[:],
                                     dg[:, hf * 4:(hf + 1) * 4, :].rearrange("p a b -> p (a b)"), start=True, stop=True)
            i.then_inc(p_bc, 1)

        @block.tensor
        def _(pe):
            mm = nc.tensor.matmul
            tr = nc.tensor.transpose
            pe.wait_ge(s_w, 16 * (N_W - 2))
            mm(PP[3][:, 0:C], fsel[:], fftp[:], start=True, stop=True).then_inc(p_filt, 1)

            def dense(dst, wt, src, o, tiles=KT):
                for hf in range(2):
                    for c in range(tiles):
                        i = mm(dst[:, hf * 512:(hf + 1) * 512], wt[:, c, o:o + P], src[:, c, hf * 512:(hf + 1) * 512],
                               start=(c == 0), stop=(c == tiles - 1))
                return i

            def one(b):
                norm_pe(pe, b, x, 0, lambda: need(pe, a_po, 2, b - 1, 2), lambda: need(pe, v_zf, 2, b - 1, 2))
                need(pe, v_xn, 2, b, 1)
                for i in range(4):
                    if i >= 2:
                        need(pe, a_qkv, 4, b, i - 1)
                    dense(PP[i % 2], wqkv, xn, i * P).then_inc(p_qkv, 1)
                need(pe, a_qkv, 4, b, 4)
                need(pe, a_vc, 2, b, 2)
                for hf in range(2):
                    for m in range(4):
                        mt = hf * 4 + m
                        for c in range(KT):
                            i = tr(PP[hf][:, m * C + c * P:m * C + (c + 1) * P], sq[:, c, mt * P:(mt + 1) * P], ident[:])
                    i.then_inc(p_vt, 1)

                def scores(u):
                    nt, h = u // NH, u % NH
                    if u >= 2:
                        need(pe, a_exp, UNITS, b, u - 1)
                    else:
                        need(pe, a_vt, 2, b, u + 1)
                    r = slice(h * KD, (h + 1) * KD)
                    for hf in range(2):
                        i = mm(PP[u % 2][:, hf * 512:(hf + 1) * 512], qk[r, 0, nt * P:(nt + 1) * P],
                               qk[r, 1, hf * 512:(hf + 1) * 512], start=True, stop=True, tile_position=(h * KD, 0))
                    i.then_inc(p_s, 1)

                def turn(u):
                    need(pe, a_exp, UNITS, b, u + 1)
                    if u == 0:
                        need(pe, a_pad, 2 * HT, b - 1, 0)
                    need(pe, a_pt, UNITS, b, u)
                    need(pe, v_pt, UNITS, b, u)
                    for m in range(NT):
                        i = tr(PP[2][:, m * P:(m + 1) * P], prob[:, u % 2, m * P:(m + 1) * P], ident[:])
                    i.then_inc(p_t, 1)

                def values(u):
                    nt, h = u // NH, u % NH
                    bank = PP[3][:, (nt % 2) * 512:(nt % 2) * 512 + 512]
                    need(pe, a_pt, UNITS, b, u + 1)
                    need(pe, v_pt, UNITS, b, u + 1)
                    if h == 0:
                        need(pe, v_o, NT, b, nt - 1)
                        if nt < 2:
                            need(pe, v_x2, 4, b - 1, 4)
                            if isinstance(b, int) and b == 0:
                                need(pe, v_filt, 1, 0, 1)
                    for m in range(NT):
                        i = mm(bank[:, h * HD:(h + 1) * HD], probt[:, u % 2, m * P:(m + 1) * P],
                               vt[:, m, h * HD:(h + 1) * HD], start=(m == 0), stop=(m == NT - 1))
                    i.then_inc(p_av, 1)

                def back(nt):
                    need(pe, v_on, NT, b, nt + 1)
                    bank = PP[3][:, (nt % 2) * 512:(nt % 2) * 512 + 512]
                    for c in range(KT):
                        i = tr(bank[:, C + c * P:C + (c + 1) * P], otok[:, nt % 2, c * P:(c + 1) * P], ident[:])
                    i.then_inc(p_ot, 1)

                for u in range(UNITS + 3):
                    if u < UNITS:
                        scores(u)
                    if 0 <= u - 1 < UNITS:
                        turn(u - 1)
                    if 0 <= u - 2 < UNITS:
                        values(u - 2)
                    if u >= 6 and (u - 6) % NH == 0 and (u - 6) // NH < NT - 1:
                        back((u - 6) // NH)
                back(NT - 1)
                need(pe, v_o, NT, b, NT)
                need(pe, a_exp, UNITS, b, UNITS)
                for c in range(KT):
                    dense(PP[c], wproj, cv, c * P).then_inc(p_pj, 1)
                norm_pe(pe, b, x1, 1, lambda: need(pe, a_pj, KT, b, KT), lambda: None)
                need(pe, v_xn, 2, b, 2)
                for j in range(HT):
                    for q in range(2):
                        if j:
                            need(pe, a_pad, 2 * HT, b, 2 * (j - 1) + q + 1)
                        dense(PP[q], wpi, xn, (q * HT + j) * P).then_inc(p_pi, 1)
                need(pe, v_g, HT, b, HT)
                for i2 in range(2):
                    need(pe, a_pad, 2 * HT, b, 2 * HT)
                    if i2:
                        need(pe, a_po, 2, b, 1)
                    for t in range(4):
                        for j in range(HT):
                            tile = i2 * 4 + t
                            i = mm(PP[0][:, t * C:(t + 1) * C], g[:, j, tile * P:(tile + 1) * P], wpo[:, j, :], start=(j == 0), stop=(j == HT - 1))
                    i.then_inc(p_po, 1)
                    need(pe, a_po, 2, b, i2 + 1)
                    if i2:
                        need(pe, v_zf, 2, b, 1)
                    for hf in range(2):
                        i = mm(PP[1][:, hf * 512:(hf + 1) * 512], dft[:], pt[:, hf * 2:hf * 2 + 2, :].rearrange("p a b -> p (a b)"),
                               start=True, stop=True)
                    i.then_inc(p_dft, 1)
                    need(pe, v_zf, 2, b, i2 + 1)
                    if i2:
                        need(pe, v_x2, 4, b, 2)
                    for c in range(KT):
                        bank = image(PP[3][:, c * 512:(c + 1) * 512])
                        for t in range(4):
                            r0 = (t // 2) * PS_
                            i = mm(bank[:, r0:r0 + PS_, (t % 2) * 16:(t % 2) * 16 + 16], zf[:, t, c * P:(c + 1) * P], idft[:],
                                   start=True, stop=True)
                    i.then_inc(p_idft, 1)

            one(0)
            with pe.Fori(1, B) as b:
                one(b)

        def norm_act(act, b, src, which):
            av = nc.scalar.activation
            need(act, p_var, 2, b, which)
            av(sq[:], src[:], ACT.Square).then_inc(a_sq, 1)
            need(act, v_rs, 8, b, 4 * which + 1)
            av(lnv[:, 1, :], lnv[:, 0, :], ACT.Ln).then_inc(a_rs, 1)
            need(act, a_rs, 4, b, 2 * which + 1)
            av(lnv[:, 2, :], lnv[:, 1, :], ACT.Exp, scale=-0.5).then_inc(a_rs, 1)

        @block.scalar
        def _(act):
            av = nc.scalar.activation
            act.wait_ge(v_bn, 1)
            av(bns[:, 1, :], bns[:, 0, :], ACT.Ln).then_inc(a_bn, 1)
            act.wait_ge(a_bn, 1)
            av(bns[:, 2, :], bns[:, 1, :], ACT.Exp, scale=-0.5).then_inc(a_bn, 1)

            def one(b):
                need(act, s_x, 16, b, 16)
                norm_act(act, b, x, 0)
                need(act, v_bn, 8, 0, 8) if isinstance(b, int) and b == 0 else None
                need(act, p_av, UNITS, b - 1, UNITS)
                for i in range(4):
                    need(act, p_qkv, 4, b, i + 1)
                    src = PP[i % 2][:]
                    if i < 2:
                        av(qk[:, i, :], src, ACT.Identity, scale=bns[:, 4, i:i + 1], bias=bns[:, 5, i:i + 1]).then_inc(a_qkv, 1)
                    else:
                        if i == 2:
                            need(act, v_cv, 16, b - 1, 16)
                            need(act, v_zero, 1, 0, 1)
                        av(sq[:, i - 2, :], src, ACT.Identity, scale=bns[:, 4, i:i + 1], bias=bns[:, 5, i:i + 1]).then_inc(a_vc, 1)
                        av(inner(vpad, i - 2), image(src), ACT.Identity, scale=bns[:, 4, i:i + 1], bias=bns[:, 5, i:i + 1]).then_inc(a_qkv, 1)
                need(act, p_pj, KT, b - 1, KT)
                for c in range(KT):
                    need(act, a_qkv, 4, b, c + 3)
                    av(image(cv[:, c, :]), vpad[:, c, 0:H, 0:W], ACT.Identity, scale=pew[:, c, 0:1],
                       bias=bns[:, 5, 4 + c:5 + c]).then_inc(a_cv0, 1)
                for hf in range(2):
                    need(act, p_vt, 2, b, hf + 1)
                    av(vt[:, hf * 4:(hf + 1) * 4, :], PP[hf][:].rearrange("p (a b) -> p a b", b=C), ACT.Copy).then_inc(a_vt, 1)
                for u in range(UNITS + 1):
                    if u < UNITS:
                        need(act, v_max, 2 * UNITS, b, 2 * u + 2)
                        need(act, p_t, UNITS, b, u - 1)
                        av(prob[:, u % 2, :], PP[u % 2][:], ACT.Exp, scale=SCALE, bias=nmx[:, 1, u:u + 1],
                           accum_out=rsum[:, 0, u:u + 1]).then_inc(a_exp, 1)
                    if u >= 1:
                        need(act, p_t, UNITS, b, u)
                        need(act, p_av, UNITS, b, u - 2)
                        av(probt[:, (u - 1) % 2, 0:512], PP[2][:, 0:512], ACT.Copy).then_inc(a_pt, 1)
                for c in range(KT):
                    need(act, p_pj, KT, b, c + 1)
                    need(act, s_st, 16, b, 0)
                    av(x1[:, c, :], PP[c][:], ACT.Identity, scale=bns[:, 4, 6 + c:7 + c], bias=bns[:, 5, 6 + c:7 + c]).then_inc(a_pj, 1)
                need(act, v_x1, KT, b, KT)
                norm_act(act, b, x1, 1)
                for j in range(HT + 1):
                    if j < HT:
                        for q in range(2):
                            need(act, p_pi, 2 * HT, b, 2 * j + q + 1)
                            need(act, v_h, 16 * HT, b, 16 * (j - 1) + 8 * (q + 1))
                            if j == 0 and q == 0:
                                need(act, v_zero, 1, 0, 2)
                            av(inner(hpad, q), image(PP[q][:]), ACT.Copy).then_inc(a_pad, 1)
                            need(act, a_pad, 2 * HT, b, 2 * j + q + 1)
                            need(act, v_g, HT, b, j)
                            if q == 0:
                                need(act, a_gl, HT, b, j)
                            av(image(hcv[:, q, :]), hpad[:, q, 0:H, 0:W], ACT.Copy, scale=dww[:, q * HT + j, 0:1]).then_inc(a_h0, 1)
                        need(act, v_h, 16 * HT, b, 16 * j + 8)
                        need(act, v_g, HT, b, j)
                        av(gl[:], hcv[:, 0, :], ACT.Gelu).then_inc(a_gl, 1)
                for i2 in range(2):
                    need(act, p_po, 2, b, i2 + 1)
                    need(act, p_dft, 2, b, i2)
                    av(pt[:], PP[0][:].rearrange("p (a b) -> p a b", b=C), ACT.Copy).then_inc(a_po, 1)

            one(0)
            with act.Fori(1, B) as b:
                one(b)

        def norm_dve(dve, b, src, which):
            v = nc.vector
            r = 8
            o = 4 * which
            need(dve, p_var, 2, b, which + 1)
            need(dve, v_dg, 2, b, which)
            v.tensor_scalar(lnv[:, 0, :], PP[0][:, 0:NT], RMS_EPS, None, ALU.add).then_inc(v_rs, 1)
            need(dve, a_rs, 4, b, 2 * which + 2)
            v.tensor_tensor(lnv[:, 3, :], lnv[:, 2, :], lnv[:, 2, :], ALU.mult).then_inc(v_rs, 1)
            need(dve, v_rs, r, b, o + 2)
            v.scalar_tensor_tensor(lnv[:, 4, :], lnv[:, 3, :], -0.5, lnv[:, 0, :], ALU.mult, ALU.mult).then_inc(v_rs, 1)
            need(dve, v_rs, r, b, o + 3)
            v.scalar_tensor_tensor(lnv[:, 1, :], lnv[:, 4, :], 1.5, lnv[:, 2, :], ALU.add, ALU.mult).then_inc(v_rs, 1)
            need(dve, v_rs, r, b, o + 4)
            need(dve, p_bc, 2, b, which)
            for t in range(NT):
                i = v.tensor_scalar(dg[:, t, :], ident[:], lnv[:, 1, t:t + 1], None, ALU.mult)
            i.then_inc(v_dg, 1)
            need(dve, p_bc, 2, b, which + 1)
            if which == 0:
                need(dve, p_pi, 2 * HT, b - 1, 2 * HT)
            else:
                need(dve, p_qkv, 4, b, 4)
            for c in range(KT):
                v.tensor_tensor(xn[:, c, :], src[:, c, :], PP[1][:], ALU.mult).then_inc(v_xh, 1)
            for c in range(KT):
                need(dve, v_xh, 4, b, 2 * which + c + 1)
                i = v.tensor_scalar(xn[:, c, :], xn[:, c, :], vec[:, 2 * which, c:c + 1], vec[:, 2 * which + 1, c:c + 1],
                                    ALU.mult, ALU.add)
            i.then_inc(v_xn, 1)

        @block.vector
        def _(dve):
            v = nc.vector
            v.memset(vpad[:], 0.0).then_inc(v_zero, 1)
            v.memset(hpad[:], 0.0).then_inc(v_zero, 1)
            dve.wait_ge(s_w, 16 * (N_W - 2))
            n_bn = [0]

            def link(i):
                n_bn[0] += 1
                i.then_inc(v_bn, 1)
                dve.wait_ge(v_bn, n_bn[0])
            link(v.tensor_scalar(bns[:, 0, :], bn[:, 3, :], BN_EPS, None, ALU.add))
            dve.wait_ge(a_bn, 2)
            link(v.tensor_tensor(bns[:, 3, :], bns[:, 2, :], bns[:, 2, :], ALU.mult))
            link(v.scalar_tensor_tensor(bns[:, 1, :], bns[:, 3, :], -0.5, bns[:, 0, :], ALU.mult, ALU.mult))
            link(v.scalar_tensor_tensor(bns[:, 3, :], bns[:, 1, :], 1.5, bns[:, 2, :], ALU.add, ALU.mult))
            link(v.tensor_tensor(bns[:, 4, :], bns[:, 3, :], bn[:, 0, :], ALU.mult))
            link(v.tensor_tensor(bns[:, 5, :], bns[:, 4, :], bn[:, 2, :], ALU.mult))
            link(v.tensor_tensor(bns[:, 5, :], bn[:, 1, :], bns[:, 5, :], ALU.subtract))
            for c in range(KT):
                v.tensor_scalar(pew[:, c, :], pew[:, c, :], bns[:, 4, 4 + c:5 + c], None, ALU.mult)
            for r in (4, 5):
                v.tensor_tensor(bns[:, r, 6:8], bns[:, r, 6:8], vec[:, 4, :], ALU.mult)
            link(v.memset(nmx[:], 0.0))
            dve.wait_ge(p_filt, 1)
            v.tensor_copy(filt[:], PP[3][:, 0:C]).then_inc(v_filt, 1)
            dve.wait_ge(v_filt, 1)

            def pe_tap(b, k):
                c, tap = k % 2, k // 2 + 1
                if tap == 1:
                    need(dve, a_cv0, KT, b, c + 1)
                else:
                    need(dve, v_cv, 16, b, k - 1)
                dy, dx = tap // 3, tap % 3
                v.scalar_tensor_tensor(image(cv[:, c, :]), vpad[:, c, dy:dy + H, dx:dx + W], pew[:, c, tap:tap + 1],
                                       image(cv[:, c, :]), ALU.mult, ALU.add).then_inc(v_cv, 1)

            def one(b):
                need(dve, s_x, 16, b, 16)
                norm_dve(dve, b, x, 0)
                for u in range(UNITS + 3):
                    if u < UNITS:
                        need(dve, p_s, UNITS, b, u + 1)
                        v.tensor_reduce(nmx[:, 0, u:u + 1], PP[u % 2][:], mybir.AxisListType.X, ALU.max, negate=True).then_inc(v_max, 1)
                        need(dve, v_max, 2 * UNITS, b, 2 * u + 1)
                        v.tensor_scalar(nmx[:, 1, u:u + 1], nmx[:, 0, u:u + 1], SCALE, None, ALU.mult).then_inc(v_max, 1)
                    if 1 <= u <= UNITS:
                        need(dve, p_t, UNITS, b, u)
                        need(dve, p_av, UNITS, b, u - 2)
                        v.tensor_copy(probt[:, (u - 1) % 2, 512:1024], PP[2][:, 512:1024]).then_inc(v_pt, 1)
                    if u < 8:
                        pe_tap(b, 2 * u)
                        pe_tap(b, 2 * u + 1)
                    if u >= 5 and (u - 5) % NH == 0 and (u - 5) // NH < NT:
                        onorm(b, (u - 5) // NH)
                    if u >= 7 and (u - 7) % NH == 0 and (u - 7) // NH < NT - 1:
                        oadd(b, (u - 7) // NH)
                oadd(b, NT - 1)
                for c in range(KT):
                    need(dve, a_pj, KT, b, c + 1)
                    v.tensor_tensor(x1[:, c, :], x1[:, c, :], x[:, c, :], ALU.add).then_inc(v_x1, 1)
                need(dve, v_x1, KT, b, KT)
                norm_dve(dve, b, x1, 1)
                for j in range(HT):
                    for q in range(2):
                        for tap in range(1, 9):
                            if tap == 1:
                                need(dve, a_h0, 2 * HT, b, 2 * j + q + 1)
                            else:
                                need(dve, v_h, 16 * HT, b, 16 * j + 8 * q + tap - 1)
                            dy, dx = tap // 3, tap % 3
                            v.scalar_tensor_tensor(image(hcv[:, q, :]), hpad[:, q, dy:dy + H, dx:dx + W],
                                                   dww[:, q * HT + j, tap:tap + 1], image(hcv[:, q, :]),
                                                   ALU.mult, ALU.add).then_inc(v_h, 1)
                    need(dve, a_gl, HT, b, j + 1)
                    need(dve, v_h, 16 * HT, b, 16 * j + 16)
                    need(dve, p_po, 2, b - 1, 2)
                    for cb in range(2):
                        gv = g[:, j, :].rearrange("p (rb cb r c) -> p cb rb r c", rb=4, cb=2, r=PS_)[:, cb]
                        tok = lambda a: a.rearrange("p (rb r cb c) -> p cb rb r c", rb=4, r=PS_, cb=2)[:, cb]
                        i = v.tensor_tensor(gv, tok(gl[:]), tok(hcv[:, 1, :]), ALU.mult)
                    i.then_inc(v_g, 1)
                for i2 in range(2):
                    need(dve, p_dft, 2, b, i2 + 1)
                    need(dve, p_idft, 2, b, i2)
                    v.tensor_tensor(zf[:], PP[1][:].rearrange("p (a b) -> p a b", b=C),
                                    filt[:, None, :].to_broadcast([P, 4, C]), ALU.mult).then_inc(v_zf, 1)
                    need(dve, p_idft, 2, b, i2 + 1)
                    for c in range(KT):
                        o = i2 * 512
                        v.scalar_tensor_tensor(x1[:, c, o:o + 512], PP[3][:, c * 512:(c + 1) * 512], vec[:, 5, c:c + 1],
                                               x1[:, c, o:o + 512], ALU.mult, ALU.add).then_inc(v_x2, 1)

            def onorm(b, nt):
                need(dve, p_av, UNITS, b, NH * (nt + 1))
                need(dve, a_exp, UNITS, b, NH * (nt + 1))
                need(dve, p_ot, NT, b, nt - 1)
                us = slice(NH * nt, NH * (nt + 1))
                v.reciprocal(rsum[:, 1, us], rsum[:, 0, us]).then_inc(v_rc, 1)
                need(dve, v_rc, NT, b, nt + 1)
                bank = PP[3][:, (nt % 2) * 512:(nt % 2) * 512 + C].rearrange("p (h d) -> p h d", d=HD)
                v.tensor_tensor(otok[:, nt % 2, :].rearrange("p (h d) -> p h d", d=HD), bank,
                                rsum[:, 1, us, None].to_broadcast([P, NH, HD]), ALU.mult).then_inc(v_on, 1)

            def oadd(b, nt):
                need(dve, p_ot, NT, b, nt + 1)
                if nt == 0:
                    need(dve, v_cv, 16, b, 16)
                o = (nt % 2) * 512 + C
                v.tensor_tensor(cv[:, :, nt * P:(nt + 1) * P], PP[3][:, o:o + C].rearrange("p (a b) -> p a b", b=P),
                                cv[:, :, nt * P:(nt + 1) * P], ALU.add).then_inc(v_o, 1)

            one(0)
            with dve.Fori(1, B) as b:
                one(b)
def mamba_layers(nc, state, w, consts):
    ctx = ExitStack()
    with ctx:
        def sb(n, s):
            return ctx.enter_context(nc.sbuf_tensor("m_" + n, s, F32))

        def sem(n):
            return ctx.enter_context(nc.semaphore("m_" + n))

        ident = sb("ident", [P, P])
        ones_c = sb("ones_c", [P, P])
        ones = sb("ones", [P, P])
        rows_w = sb("rows_w", [P, 16 * P])
        iw = sb("iw", [P, KT, 2 * DI])
        xw = sb("xw", [P, DT, BROW + DS])
        xwc = sb("xwc", [P, DT, DS])
        ow = sb("ow", [P, DT, C])
        dskip = sb("dskip", [P, DT])
        small = sb("small", [P, SMALL])
        aexp = sb("aexp", [P, DT * DS])
        amat = sb("amat", [P, DT * DS])
        x_sb = sb("x_sb", [P, KT, T])
        xo = sb("xo", [P, KT, T])
        xc = sb("xc", [P, KT, T])
        sq = sb("sq", [P, KT, T])
        lnv = sb("lnv", [P, 5, TT])
        dg = sb("dg", [P, TT, P])
        xpre = sb("xpre", [P, DT, TAPS - 1 + T])
        cacc = sb("cacc", [P, DT, T])
        xin = sb("xin", [P, 2, DT, T])
        sz = sb("sz", [P, 2, DT, T])
        dtb = sb("dtb", [P, 2, DT, T])
        ub = sb("ub", [P, 2, DT, T])
        spa = sb("spa", [P, 2, T])
        spl = sb("spl", [P, 2, T])
        spw = sb("spw", [P, DT, T])
        yb = sb("yb", [P, DT, T])
        acc = sb("acc", [P, 2, TT, DI])
        hbuf = sb("hbuf", [P, 2, DT, T])
        dbu = sb("dbu", [P, 2, DT, T])
        bbc = sb("bbc", [P, 2, T])
        pr = sb("pr", [P, 2, T])
        ctok = sb("ctok", [P, 2, TT, DS])
        carry = sb("carry", [P, DS, DT])
        ln_one = sb("ln_one", [P, 1])

        def bank(n):
            return ctx.enter_context(nc.psum_tensor("m_" + n, [P, 512], F32))
        F = [bank("f0"), bank("f1")]
        TP = [bank("t0"), bank("t1")]
        DA = [bank("d0"), bank("d1")]
        BP = [bank("b0"), bank("b1")]

        s_const, s_x, s_win, s_wout, s_xres, s_store = (sem(n) for n in (
            "const", "x_loaded", "win_loaded", "wout_loaded", "xres_loaded", "store_done"))
        s_init = sem("init")
        p_mean, p_var, p_rb, p_ix, p_iz, p_proj, p_ctok, p_dt, p_bb, p_ht, p_y, p_out = (sem("pe_" + n) for n in (
            "mean", "var", "rstd", "ix", "iz", "proj", "ctok", "dt", "bb", "ht", "y", "out"))
        a_sq, a_rs, a_pre, a_tap, a_xin, a_sz, a_proj, a_abs, a_e, a_l, a_da, a_bbc, a_amat = (sem("act_" + n) for n in (
            "sq", "rs", "pre", "tap", "xin", "sz", "proj", "abs", "e", "ln", "da", "bbc", "amat"))
        v_xc, v_rs, v_dg, v_xh, v_xn, v_conv, v_tail, v_ctok, v_q, v_w1, v_scan, v_stt, v_carry, v_yb, v_xo, v_u = (
            sem("dve_" + n) for n in (
                "xc", "rs", "dg", "xh", "xn", "conv", "tail", "ctok", "q", "w1", "scan", "stt", "carry", "yb", "xo", "u"))
        g_s, g_bu, g_g = sem("pool_s"), sem("pool_bu"), sem("pool_gate")

        state_v = state.rearrange("i (k p) n -> i p k n", p=P)
        N_WIN = 5
        N_CONST = 4

        def half(par):
            return slice(par * T, (par + 1) * T)

        block = ctx.enter_context(nc.Block())

        @block.sync
        def _(sp):
            sp.dma_start(ident[:], consts["ident"]).then_inc(s_const, 16)
            sp.dma_start(ones_c[:], consts["ones_c"]).then_inc(s_const, 16)
            sp.dma_start(ones[:], consts["ones"]).then_inc(s_const, 16)
            sp.dma_start(rows_w[BROW:BROW + DS, :], consts["select"]).then_inc(s_const, 16)
            sp.wait_ge(s_init, 2)

            def load_in_weights(kk, im):
                need(sp, p_dt, DT, kk - 1, DT)
                need(sp, v_conv, 12, kk - 1, 12)
                need(sp, v_q, DT, kk - 1, DT)
                lay = im // B
                for dst, src in ((iw[:], w["iw"]), (xw[:, :, 0:DTR], w["xw_dt"]), (xw[:, :, BROW:BROW + DS], w["xw_b"]),
                                 (xwc[:], w["xw_c"]), (small[:], w["small"])):
                    sp.dma_start(dst, src[lay]).then_inc(s_win, 16)
                sp.dma_start(rows_w[0:DTR + 1, 0:DI], w["dw"][lay]).then_inc(s_win, 16)

            def load_x(kk, im, par):
                need(sp, v_xc, KT, kk - 1, KT)
                sp.dma_start(x_sb[:], state_v[im][:, :, half(par)]).then_inc(s_x, 16)

            def load_out_weights(kk, im):
                need(sp, p_out, KT, kk - 1, KT)
                need(sp, v_yb, DT, kk - 1, DT)
                lay = im // B
                sp.dma_start(ow[:], w["ow"][lay]).then_inc(s_wout, 16)
                sp.dma_start(dskip[:], w["dskip"][lay]).then_inc(s_wout, 16)

            def residual(kk, im, par):
                need(sp, s_store, 16, kk - 1, 16)
                sp.dma_start(xo[:], state_v[im][:, :, half(par)]).then_inc(s_xres, 16)

            def store(kk, im, par):
                need(sp, v_xo, KT, kk, KT)
                sp.dma_start(state_v[im + B][:, :, half(par)], xo[:]).then_inc(s_store, 16)

            load_in_weights(0, 0)
            load_x(0, 0, 0)

            def step(k, im, par, first=False, last=False):
                if not last:
                    if par == 1:
                        load_in_weights(k + 1, im + 1)
                        load_x(k + 1, im + 1, 0)
                    else:
                        load_x(k + 1, im, 1)
                if not first:
                    if par == 1:
                        load_out_weights(k - 1, im)
                        residual(k - 1, im, 0)
                        store(k - 1, im, 0)
                    else:
                        residual(k - 1, im - 1, 1)
                        store(k - 1, im - 1, 1)

            step(0, 0, 0, first=True)
            with sp.Fori(0, IMAGES - 1) as j:
                step(2 * j + 1, j, 1)
                step(2 * j + 2, j + 1, 0)
            step(CHUNKS - 1, IMAGES - 1, 1, last=True)
            residual(CHUNKS - 1, IMAGES - 1, 1)
            store(CHUNKS - 1, IMAGES - 1, 1)
            sp.wait_ge(s_store, 16 * CHUNKS)

        @block.tensor
        def _(pe):
            mm = nc.tensor.matmul
            pe.wait_ge(s_const, 16 * N_CONST)

            def f_mean(kk, par, after_back):
                need(pe, s_x, 16, kk, 16)
                if after_back:
                    need(pe, v_xo, KT, kk - 2, 1)
                else:
                    need(pe, v_q, DT, kk - 1, 4)
                for c in range(KT):
                    i = mm(F[0][:], ones_c[:], x_sb[:, c, :], start=(c == 0), stop=(c == KT - 1))
                i.then_inc(p_mean, 1)

            def f_var(kk, par, after_back):
                need(pe, a_sq, 1, kk, 1)
                if after_back:
                    need(pe, v_xo, KT, kk - 2, 2)
                else:
                    need(pe, v_q, DT, kk - 1, 3)
                for t in range(TT):
                    for c in range(KT):
                        i = mm(F[1][:, t:t + 1], sq[:, c, t * P:(t + 1) * P], ones_c[:, 0:1],
                               start=(c == 0), stop=(c == KT - 1))
                i.then_inc(p_var, 1)

            def f_rstd(kk, par):
                need(pe, v_dg, 1, kk, 1)
                mm(F[0][:], ones[:], dg[:].rearrange("p a b -> p (a b)"), start=True, stop=True).then_inc(p_rb, 1)

            def f_in(kk, par, which):
                psem = p_ix if which == 0 else p_iz
                if which == 0:
                    need(pe, v_xn, 1, kk, 1)
                    need(pe, s_win, 48, kk, 96 if par == 0 else 48)
                for d in range(DT):
                    if which == 0 and d >= 2:
                        need(pe, a_tap, DT, kk, d - 1)
                    if which == 1:
                        if d < 2:
                            need(pe, a_tap, DT, kk, d + 3)
                        else:
                            need(pe, a_sz, DT, kk, d - 1)
                    o = which * DI + d * P
                    for c in range(KT):
                        i = mm(F[(d + 1) % 2][:], iw[:, c, o:o + P], xc[:, c, :], start=(c == 0), stop=(c == KT - 1))
                    i.then_inc(psem, 1)

            def f_proj(kk, par):
                need(pe, a_xin, 1, kk, 1)
                need(pe, a_sz, DT, kk, 3)
                for d in range(DT):
                    i = mm(F[1][0:BROW + DS, :], xw[:, d, :], xin[:, par, d, :], start=(d == 0), stop=(d == DT - 1))
                i.then_inc(p_proj, 1)
                need(pe, a_sz, DT, kk, 4)
                for t in range(TT):
                    for d in range(DT):
                        i = mm(F[0][:, t * DS:(t + 1) * DS], xin[:, par, d, t * P:(t + 1) * P], xwc[:, d, :],
                               start=(d == 0), stop=(d == DT - 1))
                i.then_inc(p_ctok, 1)

            def f_dt(kk, par):
                need(pe, a_proj, 2, kk, 2)
                for d in range(DT):
                    if d == 1:
                        need(pe, v_ctok, 1, kk, 1)
                    if d >= 2:
                        need(pe, v_q, DT, kk, d - 1)
                    mm(F[(d + 1) % 2][:], rows_w[0:DTR + 1, d * P:(d + 1) * P], pr[0:DTR + 1, par, :],
                       start=True, stop=True).then_inc(p_dt, 1)

            def bb(k, par, n):
                if n == 0:
                    need(pe, a_proj, 2, k, 2)
                need(pe, a_bbc, DS, k, n - 1)
                mm(BP[n % 2][:], rows_w[BROW:BROW + DS, n * P:(n + 1) * P], pr[BROW:BROW + DS, par, :],
                   start=True, stop=True).then_inc(p_bb, 1)

            def ht(k, n):
                need(pe, v_scan, DT * DS, k, DT * n + DT)
                for t in range(TT):
                    need(pe, v_stt, DT * DS, k, TT * n + t - 1)
                    for d in range(DT):
                        i = nc.tensor.transpose(TP[t % 2][:, d * P:(d + 1) * P], hbuf[:, n % 2, d, t * P:(t + 1) * P], ident[:])
                    i.then_inc(p_ht, 1)

            def b_y(kk, par):
                need(pe, v_stt, DT * DS, kk, DT * DS)
                for d in range(DT):
                    if d == 0:
                        if isinstance(kk, int) and kk + 1 == CHUNKS:
                            need(pe, v_xo, KT, kk - 1, KT)
                        else:
                            need(pe, v_q, DT, kk + 1, DT)
                    elif d >= 2:
                        need(pe, v_yb, DT, kk, d - 1)
                    for t in range(TT):
                        i = nc.tensor.transpose(F[d % 2][:, t * P:(t + 1) * P], acc[:, par, t, d * P:(d + 1) * P], ident[:])
                    i.then_inc(p_y, 1)

            def b_out(kk, par):
                need(pe, g_g, 1, kk, 1)
                need(pe, s_wout, 16, kk, 32 if par == 0 else 16)
                for c in range(KT):
                    for d in range(DT):
                        i = mm(F[c][:], ow[:, d, c * P:(c + 1) * P], yb[:, d, :], start=(d == 0), stop=(d == DT - 1))
                    i.then_inc(p_out, 1)

            def front(slot, kk, par, after_back):
                if slot == 5: f_mean(kk, par, after_back)
                if slot == 6: f_var(kk, par, after_back)
                if slot == 8: f_rstd(kk, par)
                if slot == 9: f_in(kk, par, 0)
                if slot == 10: f_in(kk, par, 1)
                if slot == 12: f_proj(kk, par)
                if slot == 13: f_dt(kk, par)

            def step(k, par, first=False, last=False):
                for n in range(DS):
                    if not first and n == 0:
                        ht(k - 1, DS - 1)
                    if n >= 1:
                        ht(k, n - 1)
                    if n + 1 < DS:
                        bb(k, par, n + 1)
                    elif not last:
                        bb(k + 1, 1 - par, 0)
                    if not first:
                        if n == 1: b_y(k - 1, 1 - par)
                        if n == 3: b_out(k - 1, 1 - par)
                    if not last:
                        front(n, k + 1, 1 - par, not first)

            for s in range(DS):
                front(s, 0, 0, False)
            bb(0, 0, 0)
            step(0, 0, first=True)
            with pe.Fori(0, IMAGES - 1) as j:
                step(2 * j + 1, 1)
                step(2 * j + 2, 0)
            step(CHUNKS - 1, 1, last=True)
            ht(CHUNKS - 1, DS - 1)
            b_y(CHUNKS - 1, 1)
            b_out(CHUNKS - 1, 1)

        @block.scalar
        def _(act):
            av = nc.scalar.activation

            def front(slot, kk, par):
                if slot == 6:
                    need(act, v_xc, KT, kk, KT)
                    av(sq[:], xc[:], ACT.Square).then_inc(a_sq, 1)
                if slot == 7:
                    need(act, v_rs, 4, kk, 1)
                    av(lnv[:, 1, :], lnv[:, 0, :], ACT.Ln).then_inc(a_rs, 1)
                    need(act, a_rs, 2, kk, 1)
                    av(lnv[:, 2, :], lnv[:, 1, :], ACT.Exp, scale=-0.5).then_inc(a_rs, 1)
                if slot == 9:
                    need(act, v_tail, 1, kk, 1)
                    for d in range(DT):
                        need(act, p_ix, DT, kk, d + 1)
                        av(xpre[:, d, TAPS - 1:], F[(d + 1) % 2][:], ACT.Copy).then_inc(a_pre, 1)
                        if d == 0:
                            need(act, g_s, 1, kk - 1, 1)
                        cw = O_CW + d * TAPS + TAPS - 1
                        av(cacc[:, d, :], F[(d + 1) % 2][:], ACT.Identity, scale=small[:, cw:cw + 1],
                           bias=small[:, O_CB + d:O_CB + d + 1]).then_inc(a_tap, 1)
                if slot == 10:
                    need(act, g_g, 1, kk - 2, 1)
                    for d in range(DT):
                        need(act, p_iz, DT, kk, d + 1)
                        av(sz[:, par, d, :], F[(d + 1) % 2][:], ACT.Silu).then_inc(a_sz, 1)
                    need(act, v_conv, 12, kk, 12)
                    need(act, v_yb, DT, kk - 2, DT)
                    av(xin[:, par, :, :], cacc[:], ACT.Silu).then_inc(a_xin, 1)
                if slot == 12:
                    need(act, p_proj, 1, kk, 1)
                    av(pr[0:DTR, par, :], F[1][0:DTR, :], ACT.Copy).then_inc(a_proj, 1)
                    av(pr[BROW:BROW + DS, par, :], F[1][BROW:BROW + DS, :], ACT.Copy).then_inc(a_proj, 1)
                if slot == 13:
                    for d in range(DT):
                        need(act, p_dt, DT, kk, d + 1)
                        need(act, a_e, DT, kk, d - 1)
                        av(spa[:, d % 2, :], F[(d + 1) % 2][:], ACT.Abs).then_inc(a_abs, 1)
                        need(act, a_abs, DT, kk, d + 1)
                        av(cacc[:, d, :], spa[:, d % 2, :], ACT.Exp, scale=-1.0).then_inc(a_e, 1)
                        need(act, a_e, DT, kk, d + 1)
                        need(act, v_q, DT, kk, d - 1)
                        av(spl[:, d % 2, :], cacc[:, d, :], ACT.Ln, bias=1.0).then_inc(a_l, 1)
                    if par == 0:
                        need(act, s_win, 48, kk, 96)
                        av(aexp[:], small[:, O_AL:O_AL + DT * DS], ACT.Exp).then_inc(a_amat, 1)

            def bbcopy(k, n):
                need(act, p_bb, DS, k, n + 1)
                need(act, g_bu, DS, k, n - 1)
                av(bbc[:, n % 2, :], BP[n % 2][:], ACT.Copy).then_inc(a_bbc, 1)

            def decay(k, par, n):
                if n == 0:
                    if par == 0:
                        need(act, a_amat, 1, k, 1)
                        need(act, a_da, DT * DS, k - 1, DT * DS)
                        av(amat[:], aexp[:], ACT.Copy, scale=-1.0).then_inc(a_amat, 1)
                        need(act, a_amat, 1, k, 2)
                    need(act, v_u, 2, k, 1)
                for d in range(DT):
                    need(act, v_scan, DT * DS, k, DT * n + d - 1)
                    av(DA[d % 2][:], dtb[:, par, d, :], ACT.Exp, scale=amat[:, d * DS + n:d * DS + n + 1]).then_inc(a_da, 1)

            def step(k, par, first=False, last=False):
                for n in range(DS):
                    decay(k, par, n)
                    if n + 1 < DS:
                        bbcopy(k, n + 1)
                    if not last:
                        front(n, k + 1, 1 - par)
                if not last:
                    bbcopy(k + 1, 0)

            act.wait_ge(s_init, 3)
            av(ln_one[:], ln_one[:], ACT.Ln, bias=1.0).then_inc(s_init, 1)
            for s in range(DS):
                front(s, 0, 0)
            bbcopy(0, 0)
            step(0, 0, first=True)
            with act.Fori(0, IMAGES - 1) as j:
                step(2 * j + 1, 1)
                step(2 * j + 2, 0)
            step(CHUNKS - 1, 1, last=True)

        @block.vector
        def _(dve):
            v = nc.vector
            v.memset(xw[:], 0.0).then_inc(s_init, 1)
            v.memset(pr[:], 1.0).then_inc(s_init, 1)
            v.memset(ln_one[:], 0.0).then_inc(s_init, 1)
            v.memset(xpre[:, :, 0:TAPS - 1], 0.0).then_inc(v_tail, 1)
            dve.wait_ge(s_const, 16 * N_CONST)

            def front(slot, kk, par):
                if slot == 5:
                    need(dve, p_mean, 1, kk, 1)
                    need(dve, p_iz, DT, kk - 1, DT)
                    for c in range(KT):
                        v.tensor_tensor(xc[:, c, :], x_sb[:, c, :], F[0][:], ALU.subtract).then_inc(v_xc, 1)
                if slot == 7:
                    need(dve, p_var, 1, kk, 1)
                    need(dve, v_dg, 1, kk - 1, 1)
                    v.tensor_scalar(lnv[:, 0, :], F[1][:, 0:TT], LN_EPS, None, ALU.add).then_inc(v_rs, 1)
                    need(dve, a_rs, 2, kk, 2)
                    v.tensor_tensor(lnv[:, 3, :], lnv[:, 2, :], lnv[:, 2, :], ALU.mult).then_inc(v_rs, 1)
                    need(dve, v_rs, 4, kk, 2)
                    v.scalar_tensor_tensor(lnv[:, 4, :], lnv[:, 3, :], -0.5, lnv[:, 0, :], ALU.mult, ALU.mult).then_inc(v_rs, 1)
                    need(dve, v_rs, 4, kk, 3)
                    v.scalar_tensor_tensor(lnv[:, 1, :], lnv[:, 4, :], 1.5, lnv[:, 2, :], ALU.add, ALU.mult).then_inc(v_rs, 1)
                    need(dve, v_rs, 4, kk, 4)
                    need(dve, p_rb, 1, kk - 1, 1)
                    for t in range(TT):
                        i = v.tensor_scalar(dg[:, t, :], ident[:], lnv[:, 1, t:t + 1], None, ALU.mult)
                    i.then_inc(v_dg, 1)
                if slot == 8:
                    need(dve, p_rb, 1, kk, 1)
                    for c in range(KT):
                        v.tensor_tensor(xc[:, c, :], xc[:, c, :], F[0][:], ALU.mult).then_inc(v_xh, 1)
                    need(dve, s_win, 48, kk, 96 if par == 0 else 48)
                    for c in range(KT):
                        need(dve, v_xh, KT, kk, c + 1)
                        i = v.tensor_scalar(xc[:, c, :], xc[:, c, :], small[:, O_LW + c:O_LW + c + 1],
                                            small[:, O_LB + c:O_LB + c + 1], ALU.mult, ALU.add)
                    i.then_inc(v_xn, 1)
                if slot == 10:
                    need(dve, v_tail, 1, kk, 1)
                    for tap in range(TAPS - 1):
                        for d in range(DT):
                            if tap == 0:
                                need(dve, a_tap, DT, kk, d + 1)
                            else:
                                need(dve, v_conv, 12, kk, (tap - 1) * DT + d + 1)
                            s = TAPS - 2 - tap
                            cw = O_CW + d * TAPS + s
                            v.scalar_tensor_tensor(cacc[:, d, :], xpre[:, d, s:s + T], small[:, cw:cw + 1], cacc[:, d, :],
                                                   ALU.mult, ALU.add).then_inc(v_conv, 1)
                    need(dve, v_conv, 12, kk, 12)
                    if par == 0:
                        v.tensor_copy(xpre[:, :, 0:TAPS - 1], xpre[:, :, T:T + TAPS - 1]).then_inc(v_tail, 1)
                    else:
                        v.memset(xpre[:, :, 0:TAPS - 1], 0.0).then_inc(v_tail, 1)
                if slot == 12:
                    need(dve, p_ctok, 1, kk, 1)
                    v.tensor_copy(ctok[:, par, :, :], F[0][:, 0:TT * DS].rearrange("p (a b) -> p a b", b=DS)).then_inc(v_ctok, 1)
                if slot == 13:
                    for d in range(DT):
                        need(dve, a_l, DT, kk, d + 1)
                        v.scalar_tensor_tensor(dtb[:, par, d, :], F[(d + 1) % 2][:], 0.0, spl[:, d % 2, :],
                                               ALU.max, ALU.add).then_inc(v_q, 1)
                    v.tensor_scalar(spw[:], cacc[:], 1.0, -1.0, ALU.add, ALU.add).then_inc(v_w1, 1)
                if slot == 14:
                    need(dve, g_s, 1, kk, 1)
                    need(dve, v_q, DT, kk, DT)
                    v.scalar_tensor_tensor(dtb[:, par, :, :].rearrange("p a b -> p (a b)"), dtb[:, par, :, :].rearrange("p a b -> p (a b)"),
                                           ln_one[:, 0:1], spw[:].rearrange("p a b -> p (a b)"), ALU.subtract, ALU.add).then_inc(v_u, 1)
                    need(dve, v_u, 2, kk, 1)
                    v.tensor_tensor(ub[:, par, :, :], dtb[:, par, :, :], xin[:, par, :, :], ALU.mult).then_inc(v_u, 1)

            def scan(k, par, n, d):
                need(dve, a_da, DT * DS, k, DT * n + d + 1)
                if d == 0:
                    need(dve, g_bu, DS, k, n + 1)
                    need(dve, p_ht, DT * DS, k, TT * (n - 2) + TT)
                init = 0.0 if par == 0 else carry[:, n, d:d + 1]
                v.tensor_tensor_scan(hbuf[:, n % 2, d, :], DA[d % 2][:], dbu[:, n % 2, d, :], init,
                                     ALU.mult, ALU.add).then_inc(v_scan, 1)

            def stt(k, par, n, t):
                need(dve, p_ht, DT * DS, k, TT * n + t + 1)
                cs = ctok[:, par, t, n:n + 1]
                if n == 0:
                    need(dve, p_y, DT, k - 2, DT)
                    i = v.tensor_scalar(acc[:, par, t, :], TP[t % 2][:], cs, None, ALU.mult)
                else:
                    need(dve, v_stt, DT * DS, k, TT * (n - 1) + t + 1)
                    i = v.scalar_tensor_tensor(acc[:, par, t, :], TP[t % 2][:], cs, acc[:, par, t, :], ALU.mult, ALU.add)
                i.then_inc(v_stt, 1)

            def save(k, n):
                need(dve, v_scan, DT * DS, k, DT * n + DT)
                v.tensor_copy(carry[:, n, :], hbuf[:, n % 2, :, T - 1:T].rearrange("p a b -> p (a b)")).then_inc(v_carry, 1)

            def b_yb(kk, par):
                need(dve, s_wout, 16, kk, 32 if par == 0 else 16)
                need(dve, p_out, KT, kk - 1, KT)
                for d in range(DT):
                    need(dve, p_y, DT, kk, d + 1)
                    v.scalar_tensor_tensor(yb[:, d, :], xin[:, par, d, :], dskip[:, d:d + 1], F[d % 2][:],
                                           ALU.mult, ALU.add).then_inc(v_yb, 1)

            def b_xo(kk):
                need(dve, s_xres, 16, kk, 16)
                for c in range(KT):
                    need(dve, p_out, KT, kk, c + 1)
                    v.tensor_tensor(xo[:, c, :], xo[:, c, :], F[c][:], ALU.add).then_inc(v_xo, 1)

            def step(k, par, first=False, last=False):
                for n in range(DS):
                    for d in range(DT):
                        if n == 0 and d == 0 and par == 1:
                            need(dve, v_carry, DS // 2, k, DS // 2)
                        scan(k, par, n, d)
                        if n >= 1:
                            stt(k, par, n - 1, d)
                        elif not first:
                            stt(k - 1, 1 - par, DS - 1, d)
                    if par == 0:
                        save(k, n)
                    if not first:
                        if n == 1: b_yb(k - 1, 1 - par)
                        if n == 4: b_xo(k - 1)
                    if not last:
                        front(n, k + 1, 1 - par)

            for s in range(DS):
                front(s, 0, 0)
            step(0, 0, first=True)
            with dve.Fori(0, IMAGES - 1) as j:
                step(2 * j + 1, 1)
                step(2 * j + 2, 0)
            step(CHUNKS - 1, 1, last=True)
            for t in range(TT):
                stt(CHUNKS - 1, 1, DS - 1, t)
            b_yb(CHUNKS - 1, 1)
            b_xo(CHUNKS - 1)

        @block.gpsimd
        def _(pool):
            tt = nc.gpsimd.tensor_tensor

            def rounding(kk, par):
                need(pool, v_w1, 1, kk, 1)
                tt(spw[:], cacc[:], spw[:], ALU.subtract).then_inc(g_s, 1)

            def bu(k, par, n):
                if n == 0:
                    need(pool, v_u, 2, k, 2)
                need(pool, a_bbc, DS, k, n + 1)
                need(pool, v_scan, DT * DS, k, DT * (n - 2) + DT)
                tt(dbu[:, n % 2, :, :], ub[:, par, :, :], bbc[:, n % 2, None, :].to_broadcast([P, DT, T]), ALU.mult).then_inc(g_bu, 1)

            def gate(kk, par):
                need(pool, v_yb, DT, kk, DT)
                tt(yb[:], yb[:], sz[:, par, :, :], ALU.mult).then_inc(g_g, 1)

            def step(k, par, first=False, last=False):
                for n in range(DS):
                    bu(k, par, n)
                    if not first and n == 2:
                        gate(k - 1, 1 - par)
                    if not last and n == 14:
                        rounding(k + 1, 1 - par)

            rounding(0, 0)
            step(0, 0, first=True)
            with pool.Fori(0, IMAGES - 1) as j:
                step(2 * j + 1, 1)
                step(2 * j + 2, 0)
            step(CHUNKS - 1, 1, last=True)
            gate(CHUNKS - 1, 1)
def gate_and_norm(nc, state, w, out):
    HS = C // 4
    SL = N // 512
    ctx = ExitStack()
    with ctx:
        def sb(n, s):
            return ctx.enter_context(nc.sbuf_tensor("c_" + n, s, F32))

        def sem(n):
            return ctx.enter_context(nc.semaphore("c_" + n))

        y = sb("y", [P, B, KT, N])
        res = sb("res", [P, 4, KT, N])
        w1 = sb("w1", [P, KT, HS])
        w2 = sb("w2", [HS, C])
        b1 = sb("b1", [HS, 1])
        vec = sb("vec", [P, 3, KT])
        gsum = sb("gsum", [P, KT, B])
        hid = sb("hid", [HS, B])
        gate = sb("gate", [P, KT, B])
        stats = sb("stats", [P, KT, B * SL, 6])
        agg = sb("agg", [P, KT, 2])
        tmp = sb("tmp", [P, 6, KT])
        pz = ctx.enter_context(nc.psum_tensor("c_pz", [P, 64], F32))

        s_w, s_st = sem("weights"), sem("store_done")
        s_x = [sem("x%d" % b) for b in range(B)]
        s_r = [sem("res%d" % b) for b in range(4)]
        v_sum, p_h, a_h, p_g, a_g, v_y, v_bn, v_agg, v_tmp, a_tmp, v_out = (sem(n) for n in (
            "sum", "hid_ps", "hid", "gate_ps", "gate", "y", "bn", "agg", "tmp", "lnexp", "out"))
        st_v = state.rearrange("i (k p) n -> i p k n", p=P)
        out_v = out.rearrange("b (k p) n -> b p k n", p=P)
        block = ctx.enter_context(nc.Block())

        @block.sync
        def _(sp):
            for b in range(B):
                sp.dma_start(y[:, b], st_v[IMAGES + b]).then_inc(s_x[b], 16)
            for dst, name in ((w1[:], "w1"), (w2[:], "w2"), (b1[:], "b1"), (vec[:], "vec")):
                sp.dma_start(dst, w[name]).then_inc(s_w, 16)
            for b in range(B):
                if b >= 4:
                    sp.wait_ge(v_y, KT * (b - 3))
                sp.dma_start(res[:, b % 4], st_v[b]).then_inc(s_r[b % 4], 16)
            for b in range(B):
                sp.wait_ge(v_out, KT * (b + 1))
                sp.dma_start(out_v[b], y[:, b]).then_inc(s_st, 16)
            sp.wait_ge(s_st, 16 * B)

        @block.tensor
        def _(pe):
            pe.wait_ge(s_w, 64)
            pe.wait_ge(v_sum, B * KT)
            for c in range(KT):
                i = nc.tensor.matmul(pz[0:HS, 0:B], w1[:, c, :], gsum[:, c, :], start=(c == 0), stop=(c == KT - 1))
            i.then_inc(p_h, 1)
            pe.wait_ge(a_h, 1)
            for c in range(KT):
                i = nc.tensor.matmul(pz[:, 16 + c * B:16 + (c + 1) * B], w2[:, c * P:(c + 1) * P], hid[:], start=True, stop=True)
            i.then_inc(p_g, 1)

        @block.scalar
        def _(act):
            av = nc.scalar.activation
            act.wait_ge(p_h, 1)
            av(hid[:], pz[0:HS, 0:B], ACT.Relu, scale=1.0 / N, bias=b1[:, 0:1]).then_inc(a_h, 1)
            act.wait_ge(p_g, 1)
            for c in range(KT):
                av(gate[:, c, :], pz[:, 16 + c * B:16 + (c + 1) * B], ACT.Sigmoid, bias=vec[:, 0, c:c + 1]).then_inc(a_g, 1)
            act.wait_ge(v_tmp, 1)
            av(tmp[:, 1, :], tmp[:, 0, :], ACT.Ln).then_inc(a_tmp, 1)
            act.wait_ge(a_tmp, 1)
            av(tmp[:, 2, :], tmp[:, 1, :], ACT.Exp, scale=-0.5).then_inc(a_tmp, 1)

        def stats_of(dve, b):
            for c in range(KT):
                dve.wait_ge(v_y, KT * b + c + 1)
                for s in range(SL):
                    nc.vector.bn_stats(stats[:, c, b * SL + s, :], y[:, b, c, s * 512:(s + 1) * 512]).then_inc(v_bn, 1)

        @block.vector
        def _(dve):
            v = nc.vector
            for b in range(B):
                dve.wait_ge(s_x[b], 16)
                for c in range(KT):
                    v.reduce_sum(gsum[:, c, b:b + 1], y[:, b, c, :], mybir.AxisListType.X).then_inc(v_sum, 1)
            dve.wait_ge(a_g, KT)
            for b in range(B):
                dve.wait_ge(s_r[b % 4], 16 * (b // 4 + 1))
                for c in range(KT):
                    v.scalar_tensor_tensor(y[:, b, c, :], y[:, b, c, :], gate[:, c, b:b + 1], res[:, b % 4, c, :],
                                           ALU.mult, ALU.add).then_inc(v_y, 1)
                if b:
                    stats_of(dve, b - 1)
            stats_of(dve, B - 1)
            dve.wait_ge(v_bn, B * KT * SL)
            for c in range(KT):
                v.bn_aggr(agg[:, c, :], stats[:, c, :, :].rearrange("p a b -> p (a b)")).then_inc(v_agg, 1)
            dve.wait_ge(v_agg, KT)
            n = [0]

            def link(i):
                n[0] += 1
                i.then_inc(v_tmp, 1)
                dve.wait_ge(v_tmp, n[0])
            link(v.tensor_scalar(tmp[:, 0, :], agg[:, :, 1], LN_EPS, None, ALU.add))
            dve.wait_ge(a_tmp, 2)
            link(v.tensor_tensor(tmp[:, 3, :], tmp[:, 2, :], tmp[:, 2, :], ALU.mult))
            link(v.scalar_tensor_tensor(tmp[:, 1, :], tmp[:, 3, :], -0.5, tmp[:, 0, :], ALU.mult, ALU.mult))
            link(v.scalar_tensor_tensor(tmp[:, 3, :], tmp[:, 1, :], 1.5, tmp[:, 2, :], ALU.add, ALU.mult))
            link(v.tensor_tensor(tmp[:, 4, :], tmp[:, 3, :], vec[:, 1, :], ALU.mult))
            link(v.tensor_tensor(tmp[:, 5, :], tmp[:, 4, :], agg[:, :, 0], ALU.mult))
            link(v.tensor_tensor(tmp[:, 5, :], vec[:, 2, :], tmp[:, 5, :], ALU.subtract))
            for b in range(B):
                for c in range(KT):
                    v.tensor_scalar(y[:, b, c, :], y[:, b, c, :], tmp[:, 4, c:c + 1], tmp[:, 5, c:c + 1],
                                    ALU.mult, ALU.add).then_inc(v_out, 1)


def constants():
    select = np.zeros((DS, DS, P), np.float32)
    for n in range(DS):
        select[n, n, :] = 1.0
    return {
        "ident": np.eye(P, dtype=np.float32),
        "ones_c": np.full((P, P), 1.0 / C, np.float32),
        "ones": np.ones((P, P), np.float32),
        "select": select.reshape(DS, DS * P),
    }


def chan(a, tiles):
    a = a.reshape(a.shape[0], tiles, P, -1)
    return np.ascontiguousarray(a.transpose(0, 2, 1, 3))


def mamba_weights(inp):
    g = {k[len("L1_conv_"):]: np.asarray(v) for k, v in inp.items() if k.startswith("L1_conv_")}
    xw = g["x_proj_w"].transpose(0, 2, 1)
    xw_t = chan(xw, DT)
    small = np.concatenate([
        chan(g["conv_w"], DT).reshape(NL, P, -1), chan(g["conv_b"], DT).reshape(NL, P, -1),
        chan(g["A_log"], DT).reshape(NL, P, -1), chan(g["ln_w"], KT).reshape(NL, P, -1),
        chan(g["ln_b"], KT).reshape(NL, P, -1)], axis=2)
    return {
        "iw": chan(g["in_proj_w"].transpose(0, 2, 1), KT),
        "xw_dt": np.ascontiguousarray(xw_t[..., 0:DTR]),
        "xw_b": np.ascontiguousarray(xw_t[..., DTR:DTR + DS]),
        "xw_c": np.ascontiguousarray(xw_t[..., DTR + DS:]),
        "small": np.ascontiguousarray(small),
        "dw": np.ascontiguousarray(np.concatenate([g["dt_proj_w"].transpose(0, 2, 1), g["dt_proj_b"][:, None, :]], axis=1)),
        "ow": chan(g["out_proj_w"].transpose(0, 2, 1), DT),
        "dskip": chan(g["D"], DT).reshape(NL, P, DT),
    }


def patch_basis():
    yy, xx = np.meshgrid(np.arange(8), np.arange(8), indexing="ij")
    basis, weight, picks = [], [], []
    for kx in range(5):
        for ky in range(8):
            edge = kx in (0, 4)
            if edge and ky > 4:
                continue
            phase = (2 * np.pi / 8) * ((ky * yy + kx * xx) % 8)
            keys = {(ky, kx), ((8 - ky) % 8, kx)} if edge else {(ky, kx)}
            for f in ((np.cos,) if edge and ky in (0, 4) else (np.cos, np.sin)):
                basis.append(f(phase).reshape(64))
                weight.append((1.0 if edge else 2.0) / 64)
                picks.append(keys)
    return np.array(basis), np.array(weight), picks


def fft_constants():
    basis, weight, picks = patch_basis()
    dft = np.zeros((P, P), np.float32)
    idft = np.zeros((P, P), np.float32)
    for patch in range(2):
        tok = (np.arange(8)[:, None] * 16 + patch * 8 + np.arange(8)[None, :]).reshape(64)
        fr = patch * 64 + np.arange(64)
        dft[np.ix_(tok, fr)] = basis.T
        idft[np.ix_(fr, tok)] = basis * weight[:, None]
    fsel = np.zeros((40, P), np.float32)
    for f, keys in enumerate(picks):
        for ky, kx in keys:
            fsel[ky * 5 + kx, [f, 64 + f]] = 1.0
    return {"dft": dft, "idft": idft, "fsel": fsel}


def rows(a, tiles):
    return np.ascontiguousarray(a.reshape(tiles, P, -1).transpose(1, 0, 2))


def conv_weights(inp):
    g = {k[len("L0_conv_"):]: np.asarray(v) for k, v in inp.items() if k.startswith("L0_conv_")}
    heads = np.arange(NH)[:, None] * (2 * KD + HD)
    order = np.concatenate([(heads + np.arange(KD)).reshape(-1), (heads + KD + np.arange(KD)).reshape(-1),
                            (heads + 2 * KD + np.arange(HD)).reshape(-1)])
    par = [np.concatenate([g["qkv_" + s][order], g["pe_" + s], g["proj_" + s]]) for s in "gbmv"]
    bn = np.stack(par)
    vec = np.stack([g[k].reshape(C) for k in ("norm1_w", "norm1_b", "norm2_w", "norm2_b", "gamma1", "gamma2")])
    return {
        "qkv": rows(g["qkv_w"][order].T, KT),
        "proj": rows(g["proj_w"].T, KT),
        "pi": rows(g["pi_w"].T, KT),
        "po": rows(g["po_w"].T, HT),
        "bn": np.ascontiguousarray(bn.reshape(4, 8, P).transpose(2, 0, 1)),
        "vec": np.ascontiguousarray(vec.reshape(6, KT, P).transpose(2, 0, 1)),
        "pe": rows(g["pe_w"].reshape(C, 9), KT),
        "dw": rows(g["dw_w"].reshape(2 * HID, 9), 2 * HT),
        "fftp": np.ascontiguousarray(g["fft_p"].reshape(C, 40).T),
    }


def gate_weights(inp):
    g = {k[len("L1_conv_"):]: np.asarray(v) for k, v in inp.items() if k.startswith("L1_conv_")}
    vec = np.stack([g["se_b2"], g["bn_w"], g["bn_b"]])
    return {
        "w1": rows(g["se_w1"].T, KT),
        "w2": np.ascontiguousarray(g["se_w2"].T),
        "b1": g["se_b1"].reshape(C // 4, 1),
        "vec": np.ascontiguousarray(vec.reshape(3, KT, P).transpose(2, 0, 1)),
    }


def build(nc, args):
    state = nc.dram_tensor("state", (IMAGES + B, C, N), F32, kind="Internal").ap()
    conv_block(nc, args["x"], state, args["conv"], args["const"])
    mamba_layers(nc, state, args["mamba"], args["const"])
    gate_and_norm(nc, state, args["gate"], args["out"])


def kernel(**inputs):
    import concourse.bacc as _bacc
    from concourse.bass_utils import run_bass_kernel_spmd as _run

    nc = _bacc.Bacc("TRN2", target_bir_lowering=False, num_devices=1)
    arrays = {}

    def dram(name, a):
        a = np.ascontiguousarray(a)
        arrays[name] = a
        return nc.dram_tensor(name, a.shape, F32, kind="ExternalInput").ap()

    args = {"x": dram("x", np.asarray(inputs["x"]).reshape(B, C, N))}
    for group, parts in (("conv", conv_weights(inputs)), ("mamba", mamba_weights(inputs)), ("gate", gate_weights(inputs)),
                         ("const", {**constants(), **fft_constants()})):
        args[group] = {k: dram(group + "_" + k, v) for k, v in parts.items()}
    out = nc.dram_tensor("out", (B, C, H, W), F32, kind="ExternalOutput").ap()
    args["out"] = out.rearrange("b c h w -> b c (h w)")
    build(nc, args)
    r = _run(nc, [arrays], core_ids=[0])
    return r.results[0]["out"]
```

```python
from contextlib import ExitStack

import numpy as np
import concourse.bass as bass
from concourse import mybir

P = 128
F32 = mybir.dt.float32
ALU = mybir.AluOpType
ACT = mybir.ActivationFunctionType

B, C, H, W = 8, 256, 32, 32
N = H * W
KT = C // P
NL, DS, DI, DTR, TAPS = 4, 16, 512, 16, 4
DT = DI // P
T = 512
TT = T // P
HALVES = N // T
IMAGES = NL * B
CHUNKS = IMAGES * HALVES
RING = 4
DAB = 3
BROW = 32
SMALL = DT * TAPS + DT + DT * DS + 2 * KT
O_CW, O_CB = 0, DT * TAPS
O_AL = O_CB + DT
O_LW = O_AL + DT * DS
O_LB = O_LW + KT
LN_EPS = 1e-5


def need(eng, sem, per, k, n):
    v = per * k + n
    if isinstance(v, int) and v <= 0:
        return
    eng.wait_ge(sem, v)


NH, KD, HD = 4, 32, 64
SCALE = KD ** -0.5
HID = 2 * C
HT = HID // P
NT = N // P
PW = W + 2
PS_ = 8
RMS_EPS = 1e-6
BN_EPS = 1e-5
UNITS = NT * NH


def conv_block(nc, x_in, state, w, consts):
    ctx = ExitStack()
    with ctx:
        def sb(n, s):
            return ctx.enter_context(nc.sbuf_tensor("a_" + n, s, F32))

        def sem(n):
            return ctx.enter_context(nc.semaphore("a_" + n))

        ident = sb("ident", [P, P])
        ones_c = sb("ones_c", [P, P])
        ones = sb("ones", [P, P])
        dft = sb("dft", [P, P])
        idft = sb("idft", [P, P])
        fsel = sb("fsel", [40, P])
        fftp = sb("fftp", [40, C])
        filt = sb("filt", [P, C])
        wqkv = sb("wqkv", [P, KT, 4 * P])
        wproj = sb("wproj", [P, KT, C])
        wpi = sb("wpi", [P, KT, 2 * HID])
        wpo = sb("wpo", [P, HT, C])
        bn = sb("bn", [P, 4, 8])
        bns = sb("bns", [P, 6, 8])
        vec = sb("vec", [P, 6, KT])
        pew = sb("pew", [P, KT, 9])
        dww = sb("dww", [P, 2 * HT, 9])
        x = sb("x", [P, KT, N])
        xn = sb("xn", [P, KT, N])
        sq = sb("sq", [P, KT, N])
        lnv = sb("lnv", [P, 5, NT])
        dg = sb("dg", [P, NT, P])
        qk = sb("qk", [P, 2, N])
        vpad = sb("vpad", [P, KT, PW, PW])
        vt = sb("vt", [P, NT, C])
        cv = sb("cv", [P, KT, N])
        prob = sb("prob", [P, 2, N])
        probt = sb("probt", [P, 2, N])
        nmx = sb("nmx", [P, 2, UNITS])
        rsum = sb("rsum", [P, 2, UNITS])
        otok = sb("otok", [P, 2, C])
        x1 = sb("x1", [P, KT, N])
        hpad = sb("hpad", [P, 2, PW, PW])
        hcv = sb("hcv", [P, 2, N])
        gl = sb("gl", [P, N])
        g = sb("g", [P, HT, N])
        pt = sb("pt", [P, 4, C])
        zf = sb("zf", [P, 4, C])

        def pair(n):
            return ctx.enter_context(nc.psum_tensor("a_" + n, [P, N], F32))
        PP = [pair("p0"), pair("p1"), pair("p2"), pair("p3")]

        s_w, s_x, s_st = sem("weights"), sem("x_loaded"), sem("store_done")
        p_var, p_bc, p_qkv, p_vt, p_s, p_t, p_av, p_ot, p_pj, p_pi, p_po, p_dft, p_idft, p_filt = (sem("pe_" + n) for n in (
            "var", "bc", "qkv", "vt", "s", "t", "av", "ot", "pj", "pi", "po", "dft", "idft", "filt"))
        a_sq, a_rs, a_qkv, a_cv0, a_exp, a_pt, a_pj, a_pad, a_h0, a_gl, a_po, a_bn, a_vt, a_vc = (sem("act_" + n) for n in (
            "sq", "rs", "qkv", "cv0", "exp", "probt", "pj", "pad", "h0", "gelu", "po", "bn", "vt", "vc"))
        v_rs, v_dg, v_xh, v_xn, v_max, v_pt, v_on, v_o, v_cv, v_x1, v_h, v_g, v_zf, v_x2, v_bn, v_filt, v_zero, v_rc = (
            sem("dve_" + n) for n in (
                "rs", "dg", "xh", "xn", "max", "probt", "otok", "o", "cv", "x1", "h", "g", "zf", "x2", "bn", "filt", "zero", "rsum"))

        N_W = 17
        x_v = x_in.rearrange("b (k p) n -> b p k n", p=P)
        st_v = state.rearrange("i (k p) n -> i p k n", p=P)

        def inner(pad, t):
            return pad[:, t, 1:1 + H, 1:1 + W]

        def image(a):
            return a.rearrange("p (r c) -> p r c", c=W)

        block = ctx.enter_context(nc.Block())

        @block.sync
        def _(sp):
            for dst, name in ((ident[:], "ident"), (ones_c[:], "ones_c"), (ones[:], "ones"), (dft[:], "dft"), (idft[:], "idft"),
                              (fsel[:], "fsel")):
                sp.dma_start(dst, consts[name]).then_inc(s_w, 16)
            for dst, name in ((fftp[:], "fftp"), (wqkv[:], "qkv"), (wproj[:], "proj"), (wpi[:], "pi"), (wpo[:], "po"),
                              (bn[:], "bn"), (vec[:], "vec"), (pew[:], "pe"), (dww[:], "dw")):
                sp.dma_start(dst, w[name]).then_inc(s_w, 16)

            def image_io(b):
                need(sp, s_st, 16, b, 0)
                need(sp, v_x1, KT, b - 1, KT)
                sp.dma_start(x[:], x_v[b]).then_inc(s_x, 16)
                need(sp, v_x2, 4, b, 4)
                sp.dma_start(st_v[b], x1[:]).then_inc(s_st, 16)

            image_io(0)
            with sp.Fori(1, B) as b:
                image_io(b)
            sp.wait_ge(s_st, 16 * B)

        def norm_pe(pe, b, src, which, free0, free1):
            need(pe, a_sq, 2, b, which + 1)
            free0()
            for t in range(NT):
                for c in range(KT):
                    i = nc.tensor.matmul(PP[0][:, t:t + 1], sq[:, c, t * P:(t + 1) * P], ones_c[:, 0:1],
                                         start=(c == 0), stop=(c == KT - 1))
            i.then_inc(p_var, 1)
            need(pe, v_dg, 2, b, which + 1)
            free1()
            for hf in range(2):
                i = nc.tensor.matmul(PP[1][:, hf * 512:(hf + 1) * 512], ones[:],
                                     dg[:, hf * 4:(hf + 1) * 4, :].rearrange("p a b -> p (a b)"), start=True, stop=True)
            i.then_inc(p_bc, 1)

        @block.tensor
        def _(pe):
            mm = nc.tensor.matmul
            tr = nc.tensor.transpose
            pe.wait_ge(s_w, 16 * (N_W - 2))
            mm(PP[3][:, 0:C], fsel[:], fftp[:], start=True, stop=True).then_inc(p_filt, 1)

            def dense(dst, wt, src, o, tiles=KT):
                for hf in range(2):
                    for c in range(tiles):
                        i = mm(dst[:, hf * 512:(hf + 1) * 512], wt[:, c, o:o + P], src[:, c, hf * 512:(hf + 1) * 512],
                               start=(c == 0), stop=(c == tiles - 1))
                return i

            def one(b):
                norm_pe(pe, b, x, 0, lambda: need(pe, a_po, 2, b - 1, 2), lambda: need(pe, v_zf, 2, b - 1, 2))
                need(pe, v_xn, 2, b, 1)
                for i in range(4):
                    if i >= 2:
                        need(pe, a_qkv, 4, b, i - 1)
                    dense(PP[i % 2], wqkv, xn, i * P).then_inc(p_qkv, 1)
                need(pe, a_qkv, 4, b, 4)
                need(pe, a_vc, 2, b, 2)
                for hf in range(2):
                    for m in range(4):
                        mt = hf * 4 + m
                        for c in range(KT):
                            i = tr(PP[hf][:, m * C + c * P:m * C + (c + 1) * P], sq[:, c, mt * P:(mt + 1) * P], ident[:])
                    i.then_inc(p_vt, 1)

                def scores(u):
                    nt, h = u // NH, u % NH
                    if u >= 2:
                        need(pe, a_exp, UNITS, b, u - 1)
                    else:
                        need(pe, a_vt, 2, b, u + 1)
                    r = slice(h * KD, (h + 1) * KD)
                    for hf in range(2):
                        i = mm(PP[u % 2][:, hf * 512:(hf + 1) * 512], qk[r, 0, nt * P:(nt + 1) * P],
                               qk[r, 1, hf * 512:(hf + 1) * 512], start=True, stop=True, tile_position=(h * KD, 0))
                    i.then_inc(p_s, 1)

                def turn(u):
                    need(pe, a_exp, UNITS, b, u + 1)
                    need(pe, a_pt, UNITS, b, u)
                    need(pe, v_pt, UNITS, b, u)
                    for m in range(NT):
                        i = tr(PP[2][:, m * P:(m + 1) * P], prob[:, u % 2, m * P:(m + 1) * P], ident[:])
                    i.then_inc(p_t, 1)

                def values(u):
                    nt, h = u // NH, u % NH
                    bank = PP[3][:, (nt % 2) * 512:(nt % 2) * 512 + 512]
                    need(pe, a_pt, UNITS, b, u + 1)
                    need(pe, v_pt, UNITS, b, u + 1)
                    if h == 0:
                        need(pe, v_o, NT, b, nt - 1)
                        if nt < 2:
                            need(pe, v_x2, 4, b - 1, 4)
                            if isinstance(b, int) and b == 0:
                                need(pe, v_filt, 1, 0, 1)
                    for m in range(NT):
                        i = mm(bank[:, h * HD:(h + 1) * HD], probt[:, u % 2, m * P:(m + 1) * P],
                               vt[:, m, h * HD:(h + 1) * HD], start=(m == 0), stop=(m == NT - 1))
                    i.then_inc(p_av, 1)

                def back(nt):
                    need(pe, v_on, NT, b, nt + 1)
                    bank = PP[3][:, (nt % 2) * 512:(nt % 2) * 512 + 512]
                    for c in range(KT):
                        i = tr(bank[:, C + c * P:C + (c + 1) * P], otok[:, nt % 2, c * P:(c + 1) * P], ident[:])
                    i.then_inc(p_ot, 1)

                for u in range(UNITS + 3):
                    if u < UNITS:
                        scores(u)
                    if 0 <= u - 1 < UNITS:
                        turn(u - 1)
                    if 0 <= u - 2 < UNITS:
                        values(u - 2)
                    if u >= 6 and (u - 6) % NH == 0 and (u - 6) // NH < NT - 1:
                        back((u - 6) // NH)
                back(NT - 1)
                need(pe, v_o, NT, b, NT)
                need(pe, a_exp, UNITS, b, UNITS)
                for c in range(KT):
                    dense(PP[c], wproj, cv, c * P).then_inc(p_pj, 1)
                norm_pe(pe, b, x1, 1, lambda: need(pe, a_pj, KT, b, KT), lambda: None)
                need(pe, v_xn, 2, b, 2)
                for j in range(HT):
                    for q in range(2):
                        if j:
                            need(pe, a_pad, 2 * HT, b, 2 * (j - 1) + q + 1)
                        dense(PP[q], wpi, xn, (q * HT + j) * P).then_inc(p_pi, 1)
                need(pe, v_g, HT, b, HT)
                for i2 in range(2):
                    need(pe, a_pad, 2 * HT, b, 2 * HT)
                    if i2:
                        need(pe, a_po, 2, b, 1)
                    for t in range(4):
                        for j in range(HT):
                            tile = i2 * 4 + t
                            i = mm(PP[0][:, t * C:(t + 1) * C], g[:, j, tile * P:(tile + 1) * P], wpo[:, j, :], start=(j == 0), stop=(j == HT - 1))
                    i.then_inc(p_po, 1)
                    need(pe, a_po, 2, b, i2 + 1)
                    if i2:
                        need(pe, v_zf, 2, b, 1)
                    for hf in range(2):
                        i = mm(PP[1][:, hf * 512:(hf + 1) * 512], dft[:], pt[:, hf * 2:hf * 2 + 2, :].rearrange("p a b -> p (a b)"),
                               start=True, stop=True)
                    i.then_inc(p_dft, 1)
                    need(pe, v_zf, 2, b, i2 + 1)
                    if i2:
                        need(pe, v_x2, 4, b, 2)
                    for c in range(KT):
                        bank = image(PP[3][:, c * 512:(c + 1) * 512])
                        for t in range(4):
                            r0 = (t // 2) * PS_
                            i = mm(bank[:, r0:r0 + PS_, (t % 2) * 16:(t % 2) * 16 + 16], zf[:, t, c * P:(c + 1) * P], idft[:],
                                   start=True, stop=True)
                    i.then_inc(p_idft, 1)

            one(0)
            with pe.Fori(1, B) as b:
                one(b)

        def norm_act(act, b, src, which):
            av = nc.scalar.activation
            need(act, p_var, 2, b, which)
            av(sq[:], src[:], ACT.Square).then_inc(a_sq, 1)
            need(act, v_rs, 8, b, 4 * which + 1)
            av(lnv[:, 1, :], lnv[:, 0, :], ACT.Ln).then_inc(a_rs, 1)
            need(act, a_rs, 4, b, 2 * which + 1)
            av(lnv[:, 2, :], lnv[:, 1, :], ACT.Exp, scale=-0.5).then_inc(a_rs, 1)

        @block.scalar
        def _(act):
            av = nc.scalar.activation
            act.wait_ge(v_bn, 1)
            av(bns[:, 1, :], bns[:, 0, :], ACT.Ln).then_inc(a_bn, 1)
            act.wait_ge(a_bn, 1)
            av(bns[:, 2, :], bns[:, 1, :], ACT.Exp, scale=-0.5).then_inc(a_bn, 1)

            def one(b):
                need(act, s_x, 16, b, 16)
                norm_act(act, b, x, 0)
                need(act, v_bn, 8, 0, 8) if isinstance(b, int) and b == 0 else None
                need(act, p_av, UNITS, b - 1, UNITS)
                for i in range(4):
                    need(act, p_qkv, 4, b, i + 1)
                    src = PP[i % 2][:]
                    if i < 2:
                        av(qk[:, i, :], src, ACT.Identity, scale=bns[:, 4, i:i + 1], bias=bns[:, 5, i:i + 1]).then_inc(a_qkv, 1)
                    else:
                        if i == 2:
                            need(act, v_cv, 16, b - 1, 16)
                            need(act, v_zero, 1, 0, 1)
                        av(sq[:, i - 2, :], src, ACT.Identity, scale=bns[:, 4, i:i + 1], bias=bns[:, 5, i:i + 1]).then_inc(a_vc, 1)
                        av(inner(vpad, i - 2), image(src), ACT.Identity, scale=bns[:, 4, i:i + 1], bias=bns[:, 5, i:i + 1]).then_inc(a_qkv, 1)
                need(act, p_pj, KT, b - 1, KT)
                for c in range(KT):
                    need(act, a_qkv, 4, b, c + 3)
                    av(image(cv[:, c, :]), vpad[:, c, 0:H, 0:W], ACT.Identity, scale=pew[:, c, 0:1],
                       bias=bns[:, 5, 4 + c:5 + c]).then_inc(a_cv0, 1)
                for hf in range(2):
                    need(act, p_vt, 2, b, hf + 1)
                    av(vt[:, hf * 4:(hf + 1) * 4, :], PP[hf][:].rearrange("p (a b) -> p a b", b=C), ACT.Copy).then_inc(a_vt, 1)
                for u in range(UNITS + 1):
                    if u < UNITS:
                        need(act, v_max, 2 * UNITS, b, 2 * u + 2)
                        need(act, p_t, UNITS, b, u - 1)
                        av(prob[:, u % 2, :], PP[u % 2][:], ACT.Exp, scale=SCALE, bias=nmx[:, 1, u:u + 1],
                           accum_out=rsum[:, 0, u:u + 1]).then_inc(a_exp, 1)
                    if u >= 1:
                        need(act, p_t, UNITS, b, u)
                        need(act, p_av, UNITS, b, u - 2)
                        av(probt[:, (u - 1) % 2, 0:512], PP[2][:, 0:512], ACT.Copy).then_inc(a_pt, 1)
                for c in range(KT):
                    need(act, p_pj, KT, b, c + 1)
                    need(act, s_st, 16, b, 0)
                    av(x1[:, c, :], PP[c][:], ACT.Identity, scale=bns[:, 4, 6 + c:7 + c], bias=bns[:, 5, 6 + c:7 + c]).then_inc(a_pj, 1)
                need(act, v_x1, KT, b, KT)
                norm_act(act, b, x1, 1)
                for j in range(HT + 1):
                    if j < HT:
                        for q in range(2):
                            need(act, p_pi, 2 * HT, b, 2 * j + q + 1)
                            need(act, v_h, 16 * HT, b, 16 * (j - 1) + 8 * (q + 1))
                            if j == 0 and q == 0:
                                need(act, v_zero, 1, 0, 2)
                            av(inner(hpad, q), image(PP[q][:]), ACT.Copy).then_inc(a_pad, 1)
                            need(act, a_pad, 2 * HT, b, 2 * j + q + 1)
                            need(act, v_g, HT, b, j)
                            if q == 0:
                                need(act, a_gl, HT, b, j)
                            av(image(hcv[:, q, :]), hpad[:, q, 0:H, 0:W], ACT.Copy, scale=dww[:, q * HT + j, 0:1]).then_inc(a_h0, 1)
                        need(act, v_h, 16 * HT, b, 16 * j + 8)
                        need(act, v_g, HT, b, j)
                        av(gl[:], hcv[:, 0, :], ACT.Gelu).then_inc(a_gl, 1)
                for i2 in range(2):
                    need(act, p_po, 2, b, i2 + 1)
                    need(act, p_dft, 2, b, i2)
                    av(pt[:], PP[0][:].rearrange("p (a b) -> p a b", b=C), ACT.Copy).then_inc(a_po, 1)

            one(0)
            with act.Fori(1, B) as b:
                one(b)

        def norm_dve(dve, b, src, which):
            v = nc.vector
            r = 8
            o = 4 * which
            need(dve, p_var, 2, b, which + 1)
            need(dve, v_dg, 2, b, which)
            v.tensor_scalar(lnv[:, 0, :], PP[0][:, 0:NT], RMS_EPS, None, ALU.add).then_inc(v_rs, 1)
            need(dve, a_rs, 4, b, 2 * which + 2)
            v.tensor_tensor(lnv[:, 3, :], lnv[:, 2, :], lnv[:, 2, :], ALU.mult).then_inc(v_rs, 1)
            need(dve, v_rs, r, b, o + 2)
            v.scalar_tensor_tensor(lnv[:, 4, :], lnv[:, 3, :], -0.5, lnv[:, 0, :], ALU.mult, ALU.mult).then_inc(v_rs, 1)
            need(dve, v_rs, r, b, o + 3)
            v.scalar_tensor_tensor(lnv[:, 1, :], lnv[:, 4, :], 1.5, lnv[:, 2, :], ALU.add, ALU.mult).then_inc(v_rs, 1)
            need(dve, v_rs, r, b, o + 4)
            need(dve, p_bc, 2, b, which)
            for t in range(NT):
                i = v.tensor_scalar(dg[:, t, :], ident[:], lnv[:, 1, t:t + 1], None, ALU.mult)
            i.then_inc(v_dg, 1)
            need(dve, p_bc, 2, b, which + 1)
            if which == 0:
                need(dve, p_pi, 2 * HT, b - 1, 2 * HT)
            else:
                need(dve, p_qkv, 4, b, 4)
            for c in range(KT):
                v.tensor_tensor(xn[:, c, :], src[:, c, :], PP[1][:], ALU.mult).then_inc(v_xh, 1)
            for c in range(KT):
                need(dve, v_xh, 4, b, 2 * which + c + 1)
                i = v.tensor_scalar(xn[:, c, :], xn[:, c, :], vec[:, 2 * which, c:c + 1], vec[:, 2 * which + 1, c:c + 1],
                                    ALU.mult, ALU.add)
            i.then_inc(v_xn, 1)

        @block.vector
        def _(dve):
            v = nc.vector
            v.memset(vpad[:], 0.0).then_inc(v_zero, 1)
            v.memset(hpad[:], 0.0).then_inc(v_zero, 1)
            dve.wait_ge(s_w, 16 * (N_W - 2))
            n_bn = [0]

            def link(i):
                n_bn[0] += 1
                i.then_inc(v_bn, 1)
                dve.wait_ge(v_bn, n_bn[0])
            link(v.tensor_scalar(bns[:, 0, :], bn[:, 3, :], BN_EPS, None, ALU.add))
            dve.wait_ge(a_bn, 2)
            link(v.tensor_tensor(bns[:, 3, :], bns[:, 2, :], bns[:, 2, :], ALU.mult))
            link(v.scalar_tensor_tensor(bns[:, 1, :], bns[:, 3, :], -0.5, bns[:, 0, :], ALU.mult, ALU.mult))
            link(v.scalar_tensor_tensor(bns[:, 3, :], bns[:, 1, :], 1.5, bns[:, 2, :], ALU.add, ALU.mult))
            link(v.tensor_tensor(bns[:, 4, :], bns[:, 3, :], bn[:, 0, :], ALU.mult))
            link(v.tensor_tensor(bns[:, 5, :], bns[:, 4, :], bn[:, 2, :], ALU.mult))
            link(v.tensor_tensor(bns[:, 5, :], bn[:, 1, :], bns[:, 5, :], ALU.subtract))
            for c in range(KT):
                v.tensor_scalar(pew[:, c, :], pew[:, c, :], bns[:, 4, 4 + c:5 + c], None, ALU.mult)
            for r in (4, 5):
                v.tensor_tensor(bns[:, r, 6:8], bns[:, r, 6:8], vec[:, 4, :], ALU.mult)
            link(v.memset(nmx[:], 0.0))
            dve.wait_ge(p_filt, 1)
            v.tensor_copy(filt[:], PP[3][:, 0:C]).then_inc(v_filt, 1)
            dve.wait_ge(v_filt, 1)

            def pe_tap(b, k):
                c, tap = k % 2, k // 2 + 1
                if tap == 1:
                    need(dve, a_cv0, KT, b, c + 1)
                else:
                    need(dve, v_cv, 16, b, k - 1)
                dy, dx = tap // 3, tap % 3
                v.scalar_tensor_tensor(image(cv[:, c, :]), vpad[:, c, dy:dy + H, dx:dx + W], pew[:, c, tap:tap + 1],
                                       image(cv[:, c, :]), ALU.mult, ALU.add).then_inc(v_cv, 1)

            def one(b):
                need(dve, s_x, 16, b, 16)
                norm_dve(dve, b, x, 0)
                for u in range(UNITS + 3):
                    if u < UNITS:
                        need(dve, p_s, UNITS, b, u + 1)
                        v.tensor_reduce(nmx[:, 0, u:u + 1], PP[u % 2][:], mybir.AxisListType.X, ALU.max, negate=True).then_inc(v_max, 1)
                        need(dve, v_max, 2 * UNITS, b, 2 * u + 1)
                        v.tensor_scalar(nmx[:, 1, u:u + 1], nmx[:, 0, u:u + 1], SCALE, None, ALU.mult).then_inc(v_max, 1)
                    if 1 <= u <= UNITS:
                        need(dve, p_t, UNITS, b, u)
                        need(dve, p_av, UNITS, b, u - 2)
                        v.tensor_copy(probt[:, (u - 1) % 2, 512:1024], PP[2][:, 512:1024]).then_inc(v_pt, 1)
                    if u < 8:
                        pe_tap(b, 2 * u)
                        pe_tap(b, 2 * u + 1)
                    if u >= 5 and (u - 5) % NH == 0 and (u - 5) // NH < NT:
                        onorm(b, (u - 5) // NH)
                    if u >= 7 and (u - 7) % NH == 0 and (u - 7) // NH < NT - 1:
                        oadd(b, (u - 7) // NH)
                oadd(b, NT - 1)
                for c in range(KT):
                    need(dve, a_pj, KT, b, c + 1)
                    v.tensor_tensor(x1[:, c, :], x1[:, c, :], x[:, c, :], ALU.add).then_inc(v_x1, 1)
                need(dve, v_x1, KT, b, KT)
                norm_dve(dve, b, x1, 1)
                for j in range(HT):
                    for q in range(2):
                        for tap in range(1, 9):
                            if tap == 1:
                                need(dve, a_h0, 2 * HT, b, 2 * j + q + 1)
                            else:
                                need(dve, v_h, 16 * HT, b, 16 * j + 8 * q + tap - 1)
                            dy, dx = tap // 3, tap % 3
                            v.scalar_tensor_tensor(image(hcv[:, q, :]), hpad[:, q, dy:dy + H, dx:dx + W],
                                                   dww[:, q * HT + j, tap:tap + 1], image(hcv[:, q, :]),
                                                   ALU.mult, ALU.add).then_inc(v_h, 1)
                    need(dve, a_gl, HT, b, j + 1)
                    need(dve, v_h, 16 * HT, b, 16 * j + 16)
                    need(dve, p_po, 2, b - 1, 2)
                    for cb in range(2):
                        gv = g[:, j, :].rearrange("p (rb cb r c) -> p cb rb r c", rb=4, cb=2, r=PS_)[:, cb]
                        tok = lambda a: a.rearrange("p (rb r cb c) -> p cb rb r c", rb=4, r=PS_, cb=2)[:, cb]
                        i = v.tensor_tensor(gv, tok(gl[:]), tok(hcv[:, 1, :]), ALU.mult)
                    i.then_inc(v_g, 1)
                for i2 in range(2):
                    need(dve, p_dft, 2, b, i2 + 1)
                    need(dve, p_idft, 2, b, i2)
                    v.tensor_tensor(zf[:], PP[1][:].rearrange("p (a b) -> p a b", b=C),
                                    filt[:, None, :].to_broadcast([P, 4, C]), ALU.mult).then_inc(v_zf, 1)
                    need(dve, p_idft, 2, b, i2 + 1)
                    for c in range(KT):
                        o = i2 * 512
                        v.scalar_tensor_tensor(x1[:, c, o:o + 512], PP[3][:, c * 512:(c + 1) * 512], vec[:, 5, c:c + 1],
                                               x1[:, c, o:o + 512], ALU.mult, ALU.add).then_inc(v_x2, 1)

            def onorm(b, nt):
                need(dve, p_av, UNITS, b, NH * (nt + 1))
                need(dve, a_exp, UNITS, b, NH * (nt + 1))
                need(dve, p_ot, NT, b, nt - 1)
                us = slice(NH * nt, NH * (nt + 1))
                v.reciprocal(rsum[:, 1, us], rsum[:, 0, us]).then_inc(v_rc, 1)
                need(dve, v_rc, NT, b, nt + 1)
                bank = PP[3][:, (nt % 2) * 512:(nt % 2) * 512 + C].rearrange("p (h d) -> p h d", d=HD)
                v.tensor_tensor(otok[:, nt % 2, :].rearrange("p (h d) -> p h d", d=HD), bank,
                                rsum[:, 1, us, None].to_broadcast([P, NH, HD]), ALU.mult).then_inc(v_on, 1)

            def oadd(b, nt):
                need(dve, p_ot, NT, b, nt + 1)
                if nt == 0:
                    need(dve, v_cv, 16, b, 16)
                o = (nt % 2) * 512 + C
                v.tensor_tensor(cv[:, :, nt * P:(nt + 1) * P], PP[3][:, o:o + C].rearrange("p (a b) -> p a b", b=P),
                                cv[:, :, nt * P:(nt + 1) * P], ALU.add).then_inc(v_o, 1)

            one(0)
            with dve.Fori(1, B) as b:
                one(b)
def mamba_layers(nc, state, w, consts):
    ctx = ExitStack()
    with ctx:
        def sb(n, s):
            return ctx.enter_context(nc.sbuf_tensor("m_" + n, s, F32))

        def sem(n):
            return ctx.enter_context(nc.semaphore("m_" + n))

        ident = sb("ident", [P, P])
        ones_c = sb("ones_c", [P, P])
        ones = sb("ones", [P, P])
        dtw = sb("dtw", [DTR + 1, DI])
        iw = sb("iw", [P, KT, 2 * DI])
        xw = sb("xw", [P, DT, BROW + DS])
        xwc = sb("xwc", [P, DT, DS])
        ow = sb("ow", [P, DT, C])
        dskip = sb("dskip", [P, DT])
        small = sb("small", [P, SMALL])
        aexp = sb("aexp", [P, DT * DS])
        amat = sb("amat", [P, DT * DS])
        x_sb = sb("x_sb", [P, KT, T])
        xo = sb("xo", [P, KT, T])
        xc = sb("xc", [P, KT, T])
        sq = sb("sq", [P, KT, T])
        lnv = sb("lnv", [P, 5, TT])
        dg = sb("dg", [P, TT, P])
        xpre = sb("xpre", [P, DT, TAPS - 1 + T])
        cacc = sb("cacc", [P, DT, T])
        xin = sb("xin", [P, 2, DT, T])
        sz = sb("sz", [P, 2, DT, T])
        dtb = sb("dtb", [P, 2, DT, T])
        ub = sb("ub", [P, 2, DT, T])
        spw = sb("spw", [P, DT, T])
        yb = sb("yb", [P, DT, T])
        acc = sb("acc", [P, 2, TT, DI])
        hbuf = sb("hbuf", [P, 2, DT, T])
        dbu = sb("dbu", [P, 2, DT, T])
        bbc = sb("bbc", [P, RING, T])
        pr = sb("pr", [P, 2, T])
        ctok = sb("ctok", [P, 2, TT, DS])
        carry = sb("carry", [P, DS, DT])
        ln_one = sb("ln_one", [P, 1])

        def bank(n):
            return ctx.enter_context(nc.psum_tensor("m_" + n, [P, 512], F32))
        F = [bank("f0"), bank("f1")]
        G = bank("g")
        TP = [bank("t0"), bank("t1")]
        DA = [bank("d%d" % i) for i in range(DAB)]
        brow = nc.dram_tensor("b_rows", (2, DS, T), F32, kind="Internal").ap()

        s_const, s_x, s_win, s_wout, s_xres, s_store = (sem(n) for n in (
            "const", "x_loaded", "win_loaded", "wout_loaded", "xres_loaded", "store_done"))
        s_init = sem("init")
        s_brow = sem("b_rows_stored")
        s_row = [sem("b_row_loaded%d" % r) for r in range(RING)]
        p_mean, p_var, p_rb, p_ix, p_iz, p_proj, p_ctok, p_dt, p_ht, p_y, p_out = (sem("pe_" + n) for n in (
            "mean", "var", "rstd", "ix", "iz", "proj", "ctok", "dt", "ht", "y", "out"))
        a_sq, a_rs, a_xn, a_pre, a_tap, a_z, a_xin, a_sz, a_proj, a_dtx, a_abs, a_e, a_l, a_da, a_amat = (
            sem("act_" + n) for n in (
                "sq", "rs", "xn", "pre", "tap", "z", "xin", "sz", "proj", "dtx", "abs", "e", "ln", "da", "amat"))
        v_xc, v_rs, v_dg, v_xh, v_conv, v_tail, v_ctok, v_w1, v_scan, v_stt, v_carry, v_yb, v_xo, v_dt = (
            sem("dve_" + n) for n in (
                "xc", "rs", "dg", "xh", "conv", "tail", "ctok", "w1", "scan", "stt", "carry", "yb", "xo", "dt"))
        g_w, g_u, g_bu, g_g = sem("pool_rounding"), sem("pool_u"), sem("pool_bu"), sem("pool_gate")

        state_v = state.rearrange("i (k p) n -> i p k n", p=P)
        N_WIN = 5
        N_CONST = 3

        def half(par):
            return slice(par * T, (par + 1) * T)

        block = ctx.enter_context(nc.Block())

        @block.sync
        def _(sp):
            sp.dma_start(ident[:], consts["ident"]).then_inc(s_const, 16)
            sp.dma_start(ones_c[:], consts["ones_c"]).then_inc(s_const, 16)
            sp.dma_start(ones[:], consts["ones"]).then_inc(s_const, 16)
            sp.wait_ge(s_init, 2)

            def load_in_weights(kk, im):
                lay = im // B
                need(sp, p_ctok, 1, kk - 1, 1)
                need(sp, v_conv, 12, kk - 1, 12)
                for dst, src in ((iw[:], w["iw"]), (xw[:, :, 0:DTR], w["xw_dt"]), (xw[:, :, BROW:BROW + DS], w["xw_b"]),
                                 (xwc[:], w["xw_c"]), (small[:], w["small"])):
                    sp.dma_start(dst, src[lay]).then_inc(s_win, 16)
                sp.dma_start(dtw[:], w["dw"][lay]).then_inc(s_win, 16)

            def load_x(kk, im, par):
                need(sp, v_xc, KT, kk - 1, KT)
                sp.dma_start(x_sb[:], state_v[im][:, :, half(par)]).then_inc(s_x, 16)

            def load_out_weights(kk, im):
                lay = im // B
                need(sp, p_out, KT, kk - 1, KT)
                need(sp, v_yb, DT, kk - 1, DT)
                sp.dma_start(ow[:], w["ow"][lay]).then_inc(s_wout, 16)
                sp.dma_start(dskip[:], w["dskip"][lay]).then_inc(s_wout, 16)

            def residual(kk, im, par):
                need(sp, s_store, 16, kk - 1, 16)
                sp.dma_start(xo[:], state_v[im][:, :, half(par)]).then_inc(s_xres, 16)

            def store(kk, im, par):
                need(sp, v_xo, KT, kk, KT)
                sp.dma_start(state_v[im + B][:, :, half(par)], xo[:]).then_inc(s_store, 16)

            def keep_rows(kk, par):
                need(sp, a_proj, 2, kk, 2)
                for r in (0, DS // 2):
                    sp.dma_start(brow[par][r:r + DS // 2, :], pr[BROW + r:BROW + r + DS // 2, par, :]).then_inc(s_brow, 16)

            def row(k, par, n):
                need(sp, g_bu, DS, k, n - RING + 1)
                if n == 0:
                    need(sp, s_brow, 32, k, 32)
                sp.dma_start(bbc[:, n % RING, :], brow[par][n:n + 1, :].to_broadcast([P, T])).then_inc(s_row[n % RING], 16)

            def step(k, im, par, first=False, last=False, last2=False):
                pk = (k - 1, im if par == 1 else im - 1, 1 - par)
                for n in range(DS):
                    if not first and n == 1:
                        residual(*pk)
                    if not last and not last2 and n == 2:
                        load_x(k + 2, im + 1, par)
                    if not first and n == 15:
                        store(*pk)
                    if par == 0 and n == 14:
                        load_out_weights(k, im)
                    if not last and n == 12:
                        keep_rows(k + 1, 1 - par)
                    if n + 2 < DS:
                        row(k, par, n + 2)
                    elif not last:
                        row(k + 1, 1 - par, n + 2 - DS)
                    if par == 0 and not last2 and n == 14:
                        load_in_weights(k + 2, im + 1)

            load_in_weights(0, 0)
            load_x(0, 0, 0)
            load_x(1, 0, 1)
            keep_rows(0, 0)
            row(0, 0, 0)
            row(0, 0, 1)
            step(0, 0, 0, first=True)
            step(1, 0, 1)
            with sp.Fori(1, IMAGES - 1) as j:
                step(2 * j, j, 0)
                step(2 * j + 1, j, 1)
            step(CHUNKS - 2, IMAGES - 1, 0, last2=True)
            step(CHUNKS - 1, IMAGES - 1, 1, last=True)
            residual(CHUNKS - 1, IMAGES - 1, 1)
            store(CHUNKS - 1, IMAGES - 1, 1)
            sp.wait_ge(s_store, 16 * CHUNKS)

        def at(slot, quarter):
            return 4 * slot + quarter


        @block.tensor
        def _(pe):
            mm = nc.tensor.matmul
            pe.wait_ge(s_const, 16 * N_CONST)

            def f_mean(kk, par, c):
                if c == 0:
                    need(pe, s_x, 16, kk, 16)
                    need(pe, v_ctok, 1, kk - 1, 1)
                i = mm(F[0][:], ones_c[:], x_sb[:, c, :], start=(c == 0), stop=(c == KT - 1))
                if c == KT - 1:
                    i.then_inc(p_mean, 1)

            def f_var(kk, par):
                need(pe, a_sq, 1, kk, 1)
                need(pe, a_dtx, DT, kk - 1, 4)
                for t in range(TT):
                    for c in range(KT):
                        i = mm(F[1][:, t:t + 1], sq[:, c, t * P:(t + 1) * P], ones_c[:, 0:1],
                               start=(c == 0), stop=(c == KT - 1))
                i.then_inc(p_var, 1)

            def f_rstd(kk, par):
                need(pe, v_dg, 1, kk, 1)
                mm(F[0][:], ones[:], dg[:].rearrange("p a b -> p (a b)"), start=True, stop=True).then_inc(p_rb, 1)

            def f_in(kk, par, piece):
                which, d, c = piece // (DT * KT), piece // KT % DT, piece % KT
                if piece == 0:
                    need(pe, a_xn, KT, kk, KT)
                    need(pe, s_win, 48, kk, 96 if par == 0 else 48)
                if c == 0:
                    if which == 0 and d >= 2:
                        need(pe, a_tap, DT, kk, d - 1)
                    if which == 1 and d < 2:
                        need(pe, a_tap, DT, kk, d + 3)
                    if which == 1 and d >= 2:
                        need(pe, a_z, DT, kk, d - 1)
                o = which * DI + d * P
                i = mm(F[(d + 1) % 2][:], iw[:, c, o:o + P], xc[:, c, :], start=(c == 0), stop=(c == KT - 1))
                if c == KT - 1:
                    i.then_inc(p_ix if which == 0 else p_iz, 1)

            def f_proj(kk, par, d):
                if d == 0:
                    need(pe, a_z, DT, kk, 3)
                need(pe, a_xin, 2, kk, d // 2 + 1)
                i = mm(F[1][0:BROW + DS, :], xw[:, d, :], xin[:, par, d, :], start=(d == 0), stop=(d == DT - 1))
                if d == DT - 1:
                    i.then_inc(p_proj, 1)

            def f_dt(kk, par, d):
                if d == 0:
                    need(pe, a_z, DT, kk, 4)
                    need(pe, a_proj, 2, kk, 2)
                if d >= 2:
                    need(pe, a_dtx, DT, kk, d - 1)
                mm(F[d % 2][:], dtw[:, d * P:(d + 1) * P], pr[0:DTR + 1, par, :],
                   start=True, stop=True).then_inc(p_dt, 1)

            def f_ctok(kk, par, t):
                if t == 0:
                    need(pe, a_dtx, DT, kk, 3)
                for d in range(DT):
                    i = mm(F[0][:, t * DS:(t + 1) * DS], xin[:, par, d, t * P:(t + 1) * P], xwc[:, d, :],
                           start=(d == 0), stop=(d == DT - 1))
                if t == TT - 1:
                    i.then_inc(p_ctok, 1)

            def ht(k, n, t):
                if t == 0:
                    need(pe, v_scan, DT * DS, k, DT * n + DT)
                need(pe, v_stt, DT * DS, k, TT * n + t - 1)
                for d in range(DT):
                    i = nc.tensor.transpose(TP[t % 2][:, d * P:(d + 1) * P], hbuf[:, n % 2, d, t * P:(t + 1) * P], ident[:])
                i.then_inc(p_ht, 1)

            def b_y(kk, par, d):
                if d == 0:
                    need(pe, v_stt, DT * DS, kk, DT * DS)
                    need(pe, v_xo, KT, kk - 1, KT)
                need(pe, v_yb, DT, kk, d)
                for t in range(TT):
                    i = nc.tensor.transpose(G[:, t * P:(t + 1) * P], acc[:, par, t, d * P:(d + 1) * P], ident[:])
                i.then_inc(p_y, 1)

            def b_out(kk, par, c, d):
                if c == 0:
                    need(pe, g_g, DT, kk, d + 1)
                    if d == 0:
                        need(pe, s_wout, 16, kk, 32 if par == 0 else 16)
                elif d == 0:
                    need(pe, v_xo, KT, kk, c)
                i = mm(G[:], ow[:, d, c * P:(c + 1) * P], yb[:, d, :], start=(d == 0), stop=(d == DT - 1))
                if d == DT - 1:
                    i.then_inc(p_out, 1)

            def front(quarter, kk, par):
                def piece(first, count):
                    i = quarter - first
                    return i if 0 <= i < count else None
                if (i := piece(at(0, 0), KT)) is not None: f_mean(kk, par, i)
                if quarter == at(1, 2): f_var(kk, par)
                if quarter == at(3, 0): f_rstd(kk, par)
                if (i := piece(at(4, 2), 2 * DT * KT)) is not None: f_in(kk, par, i)
                if (i := piece(at(8, 3), DT)) is not None: f_proj(kk, par, i)
                if quarter == at(10, 1): f_dt(kk, par, 0)
                if quarter == at(10, 2): f_dt(kk, par, 1)
                if quarter == at(11, 0): f_dt(kk, par, 2)
                if quarter == at(11, 1): f_dt(kk, par, 3)
                if (i := piece(at(11, 3), TT)) is not None: f_ctok(kk, par, i)

            def back(quarter, kk, par):
                def piece(first, count):
                    i = quarter - first
                    return i if 0 <= i < count else None
                if quarter == at(1, 1): b_y(kk, par, 0)
                if quarter in (at(2, 0), at(2, 2), at(3, 0)): b_y(kk, par, (quarter - at(1, 2)) // 2)
                if (i := piece(at(9, 3), DT)) is not None: b_out(kk, par, 0, i)
                if (i := piece(at(12, 3), DT)) is not None: b_out(kk, par, 1, i)

            def step(k, par, first=False, last=False):
                for n in range(DS):
                    for q in range(TT):
                        if n >= 1:
                            ht(k, n - 1, q)
                        elif not first:
                            ht(k - 1, DS - 1, q)
                        if not last:
                            front(at(n, q), k + 1, 1 - par)
                        if not first:
                            back(at(n, q), k - 1, 1 - par)

            for s in range(DS):
                for q in range(TT):
                    front(at(s, q), 0, 0)
            step(0, 0, first=True)
            step(1, 1)
            with pe.Fori(1, IMAGES - 1) as j:
                step(2 * j, 0)
                step(2 * j + 1, 1)
            step(CHUNKS - 2, 0)
            step(CHUNKS - 1, 1, last=True)
            for q in range(TT):
                ht(CHUNKS - 1, DS - 1, q)
            for d in range(DT):
                b_y(CHUNKS - 1, 1, d)
            for c in range(KT):
                for d in range(DT):
                    b_out(CHUNKS - 1, 1, c, d)

        @block.scalar
        def _(act):
            av = nc.scalar.activation
            last_use = [max(g for g in range(DT * DS) if g % DAB == b) for b in range(DAB)]

            def pre(kk, par, d):
                if d == 0:
                    need(act, v_tail, 1, kk, 1)
                need(act, p_ix, DT, kk, d + 1)
                av(xpre[:, d, TAPS - 1:], F[(d + 1) % 2][:], ACT.Copy).then_inc(a_pre, 1)
                if d == 0:
                    need(act, g_w, 2, kk - 1, 2)
                    need(act, a_l, 1, kk - 1, 1)
                cw = O_CW + d * TAPS + TAPS - 1
                av(cacc[:, d, :], F[(d + 1) % 2][:], ACT.Identity, scale=small[:, cw:cw + 1],
                   bias=small[:, O_CB + d:O_CB + d + 1]).then_inc(a_tap, 1)

            def zcopy(kk, par, d):
                if d == 0:
                    need(act, g_g, DT, kk - 2, DT)
                need(act, p_iz, DT, kk, d + 1)
                av(sz[:, par, d, :], F[(d + 1) % 2][:], ACT.Copy).then_inc(a_z, 1)

            def dtcopy(kk, par, d):
                need(act, p_dt, DT, kk, d + 1)
                av(dtb[:, par, d, :], F[d % 2][:], ACT.Copy).then_inc(a_dtx, 1)

            def front(slot, q, kk, par):
                if (slot, q) == (1, 0):
                    need(act, v_xc, KT, kk, KT)
                    av(sq[:], xc[:], ACT.Square).then_inc(a_sq, 1)
                if (slot, q) == (2, 1):
                    need(act, v_rs, 4, kk, 1)
                    av(lnv[:, 1, :], lnv[:, 0, :], ACT.Ln).then_inc(a_rs, 1)
                    need(act, a_rs, 2, kk, 1)
                    av(lnv[:, 2, :], lnv[:, 1, :], ACT.Exp, scale=-0.5).then_inc(a_rs, 1)
                if (slot, q) == (4, 0):
                    need(act, s_win, 48, kk, 96 if par == 0 else 48)
                    for c in range(KT):
                        need(act, v_xh, KT, kk, c + 1)
                        av(xc[:, c, :], xc[:, c, :], ACT.Identity, scale=small[:, O_LW + c:O_LW + c + 1],
                           bias=small[:, O_LB + c:O_LB + c + 1]).then_inc(a_xn, 1)
                if slot in (5, 6) and q in (0, 2): pre(kk, par, 2 * (slot - 5) + q // 2)
                if slot in (7, 8) and q in (0, 2): zcopy(kk, par, 2 * (slot - 7) + q // 2)
                if (slot, q) in ((7, 1), (8, 1)):
                    r = slot - 7
                    need(act, v_conv, 12, kk, 6 * r + 6)
                    if r == 0:
                        need(act, v_yb, DT, kk - 2, DT)
                        need(act, g_u, 1, kk - 2, 1)
                    av(xin[:, par, 2 * r:2 * r + 2, :], cacc[:, 2 * r:2 * r + 2, :], ACT.Silu).then_inc(a_xin, 1)
                if (slot, q) == (9, 3):
                    need(act, p_proj, 1, kk, 1)
                    av(pr[0:DTR, par, :], F[1][0:DTR, :], ACT.Copy).then_inc(a_proj, 1)
                    av(pr[BROW:BROW + DS, par, :], F[1][BROW:BROW + DS, :], ACT.Copy).then_inc(a_proj, 1)
                if (slot, q) == (10, 2): dtcopy(kk, par, 0)
                if (slot, q) == (10, 3): dtcopy(kk, par, 1)
                if (slot, q) == (11, 1): dtcopy(kk, par, 2)
                if (slot, q) == (11, 2): dtcopy(kk, par, 3)
                if (slot, q) == (11, 3):
                    need(act, a_dtx, DT, kk, DT)
                    need(act, v_dt, 2, kk - 1, 1)
                    av(spw[:], dtb[:, par, :, :], ACT.Abs).then_inc(a_abs, 1)
                if (slot, q) == (12, 1):
                    need(act, a_abs, 1, kk, 1)
                    av(cacc[:], spw[:], ACT.Exp, scale=-1.0).then_inc(a_e, 1)
                if (slot, q) == (12, 3):
                    need(act, a_e, 1, kk, 1)
                    av(spw[:], cacc[:], ACT.Ln, bias=1.0).then_inc(a_l, 1)
                if (slot, q) == (14, 1):
                    need(act, a_z, DT, kk, DT)
                    av(sz[:, par, :, :], sz[:, par, :, :], ACT.Silu).then_inc(a_sz, 1)
                if (slot, q) == (15, 0) and par == 0:
                    need(act, s_win, 48, kk, 96)
                    av(aexp[:], small[:, O_AL:O_AL + DT * DS], ACT.Exp).then_inc(a_amat, 1)

            def decay(k, par, n, d):
                if n == 0 and d == 0:
                    if par == 0:
                        need(act, a_amat, 1, k, 1)
                        need(act, a_da, DT * DS, k - 1, DT * DS)
                        av(amat[:], aexp[:], ACT.Copy, scale=-1.0).then_inc(a_amat, 1)
                        need(act, a_amat, 1, k, 2)
                    need(act, v_dt, 2, k, 2)
                g = DT * n + d
                need(act, v_scan, DT * DS, k, g - DAB + 1 if g >= DAB else last_use[g] + 1 - DT * DS)
                av(DA[g % DAB][:], dtb[:, par, d, :], ACT.Exp, scale=amat[:, d * DS + n:d * DS + n + 1]).then_inc(a_da, 1)

            def step(k, par, first=False, last=False):
                for n in range(DS):
                    for q in range(DT):
                        decay(k, par, n, q)
                        if not last:
                            front(n, q, k + 1, 1 - par)

            act.wait_ge(s_init, 3)
            av(ln_one[:], ln_one[:], ACT.Ln, bias=1.0).then_inc(s_init, 1)
            for s in range(DS):
                for q in range(DT):
                    front(s, q, 0, 0)
            step(0, 0, first=True)
            step(1, 1)
            with act.Fori(1, IMAGES - 1) as j:
                step(2 * j, 0)
                step(2 * j + 1, 1)
            step(CHUNKS - 2, 0)
            step(CHUNKS - 1, 1, last=True)

        @block.vector
        def _(dve):
            v = nc.vector
            v.memset(xw[:], 0.0).then_inc(s_init, 1)
            v.memset(pr[:], 1.0).then_inc(s_init, 1)
            v.memset(ln_one[:], 0.0).then_inc(s_init, 1)
            v.memset(xpre[:, :, 0:TAPS - 1], 0.0).then_inc(v_tail, 1)
            dve.wait_ge(s_const, 16 * N_CONST)

            def conv(kk, i):
                d, tap = i // (TAPS - 1), i % (TAPS - 1)
                if tap == 0:
                    need(dve, a_tap, DT, kk, d + 1)
                else:
                    need(dve, v_conv, 12, kk, i)
                s = TAPS - 2 - tap
                cw = O_CW + d * TAPS + s
                v.scalar_tensor_tensor(cacc[:, d, :], xpre[:, d, s:s + T], small[:, cw:cw + 1], cacc[:, d, :],
                                       ALU.mult, ALU.add).then_inc(v_conv, 1)

            def front(slot, q, kk, par):
                if (slot, q) == (0, 2):
                    need(dve, p_mean, 1, kk, 1)
                    need(dve, p_iz, DT, kk - 1, DT)
                    for c in range(KT):
                        v.tensor_tensor(xc[:, c, :], x_sb[:, c, :], F[0][:], ALU.subtract).then_inc(v_xc, 1)
                if (slot, q) == (1, 3):
                    need(dve, p_var, 1, kk, 1)
                    need(dve, v_dg, 1, kk - 1, 1)
                    v.tensor_scalar(lnv[:, 0, :], F[1][:, 0:TT], LN_EPS, None, ALU.add).then_inc(v_rs, 1)
                if (slot, q) == (2, 2):
                    need(dve, a_rs, 2, kk, 2)
                    v.tensor_tensor(lnv[:, 3, :], lnv[:, 2, :], lnv[:, 2, :], ALU.mult).then_inc(v_rs, 1)
                    need(dve, v_rs, 4, kk, 2)
                    v.scalar_tensor_tensor(lnv[:, 4, :], lnv[:, 3, :], -0.5, lnv[:, 0, :], ALU.mult, ALU.mult).then_inc(v_rs, 1)
                    need(dve, v_rs, 4, kk, 3)
                    v.scalar_tensor_tensor(lnv[:, 1, :], lnv[:, 4, :], 1.5, lnv[:, 2, :], ALU.add, ALU.mult).then_inc(v_rs, 1)
                    need(dve, v_rs, 4, kk, 4)
                    need(dve, p_rb, 1, kk - 1, 1)
                    for t in range(TT):
                        i = v.tensor_scalar(dg[:, t, :], ident[:], lnv[:, 1, t:t + 1], None, ALU.mult)
                    i.then_inc(v_dg, 1)
                if (slot, q) == (3, 2):
                    need(dve, p_rb, 1, kk, 1)
                    need(dve, a_sq, 1, kk, 1)
                    for c in range(KT):
                        v.tensor_tensor(xc[:, c, :], xc[:, c, :], F[0][:], ALU.mult).then_inc(v_xh, 1)
                if (slot, q) == (5, 1):
                    need(dve, v_tail, 1, kk, 1)
                if at(5, 1) <= at(slot, q) < at(5, 1) + 12:
                    conv(kk, at(slot, q) - at(5, 1))
                if (slot, q) == (8, 2):
                    need(dve, v_conv, 12, kk, 12)
                    if par == 0:
                        v.tensor_copy(xpre[:, :, 0:TAPS - 1], xpre[:, :, T:T + TAPS - 1]).then_inc(v_tail, 1)
                    else:
                        v.memset(xpre[:, :, 0:TAPS - 1], 0.0).then_inc(v_tail, 1)
                if (slot, q) == (12, 3):
                    need(dve, p_ctok, 1, kk, 1)
                    v.tensor_copy(ctok[:, par, :, :], F[0][:, 0:TT * DS].rearrange("p (a b) -> p a b", b=DS)).then_inc(v_ctok, 1)
                if (slot, q) == (12, 2):
                    need(dve, a_e, 1, kk, 1)
                    need(dve, g_bu, DS, kk - 2, DS)
                    v.tensor_scalar(ub[:, par, :, :], cacc[:], 1.0, -1.0, ALU.add, ALU.add).then_inc(v_w1, 1)
                if (slot, q) == (13, 2):
                    need(dve, a_l, 1, kk, 1)
                    flat = dtb[:, par, :, :].rearrange("p a b -> p (a b)")
                    v.scalar_tensor_tensor(flat, flat, 0.0, spw[:].rearrange("p a b -> p (a b)"), ALU.max, ALU.add).then_inc(v_dt, 1)
                if (slot, q) == (14, 2):
                    need(dve, v_dt, 2, kk, 1)
                    need(dve, g_w, 2, kk, 2)
                    flat = dtb[:, par, :, :].rearrange("p a b -> p (a b)")
                    v.scalar_tensor_tensor(flat, flat, ln_one[:, 0:1], ub[:, par, :, :].rearrange("p a b -> p (a b)"),
                                           ALU.subtract, ALU.add).then_inc(v_dt, 1)

            def scan(k, par, n, d):
                need(dve, a_da, DT * DS, k, DT * n + d + 1)
                if d == 0:
                    need(dve, g_bu, DS, k, n + 1)
                    need(dve, p_ht, DT * DS, k, TT * (n - 2) + TT)
                init = 0.0 if par == 0 else carry[:, n, d:d + 1]
                v.tensor_tensor_scan(hbuf[:, n % 2, d, :], DA[(DT * n + d) % DAB][:], dbu[:, n % 2, d, :], init,
                                     ALU.mult, ALU.add).then_inc(v_scan, 1)

            def stt(k, par, n, t):
                need(dve, p_ht, DT * DS, k, TT * n + t + 1)
                cs = ctok[:, par, t, n:n + 1]
                if n == 0:
                    need(dve, p_y, DT, k - 2, DT)
                    i = v.tensor_scalar(acc[:, par, t, :], TP[t % 2][:], cs, None, ALU.mult)
                else:
                    need(dve, v_stt, DT * DS, k, TT * (n - 1) + t + 1)
                    i = v.scalar_tensor_tensor(acc[:, par, t, :], TP[t % 2][:], cs, acc[:, par, t, :], ALU.mult, ALU.add)
                i.then_inc(v_stt, 1)

            def save(k, n):
                need(dve, v_scan, DT * DS, k, DT * n + DT)
                v.tensor_copy(carry[:, n, :], hbuf[:, n % 2, :, T - 1:T].rearrange("p a b -> p (a b)")).then_inc(v_carry, 1)

            def b_yb(kk, par, d):
                if d == 0:
                    need(dve, s_wout, 16, kk, 32 if par == 0 else 16)
                    need(dve, p_out, KT, kk - 1, KT)
                need(dve, p_y, DT, kk, d + 1)
                v.scalar_tensor_tensor(yb[:, d, :], xin[:, par, d, :], dskip[:, d:d + 1], G[:],
                                       ALU.mult, ALU.add).then_inc(v_yb, 1)

            def b_xo(kk, c):
                if c == 0:
                    need(dve, s_xres, 16, kk, 16)
                need(dve, p_out, KT, kk, c + 1)
                v.tensor_tensor(xo[:, c, :], xo[:, c, :], G[:], ALU.add).then_inc(v_xo, 1)

            def back(slot, q, kk, par):
                quarter = at(slot, q)
                if quarter in (at(1, 3), at(2, 1), at(2, 3), at(3, 1)): b_yb(kk, par, (quarter - at(1, 3)) // 2)
                if (slot, q) == (11, 0): b_xo(kk, 0)
                if (slot, q) == (14, 0): b_xo(kk, 1)

            def step(k, par, first=False, last=False):
                for n in range(DS):
                    for q in range(DT):
                        if n == 0 and q == 0 and par == 1:
                            need(dve, v_carry, DS // 2, k, DS // 2)
                        if n == 0 and not first and q < TT - 2:
                            if q == 0:
                                stt(k - 1, 1 - par, DS - 1, 0)
                            stt(k - 1, 1 - par, DS - 1, q + 1)
                        scan(k, par, n, q)
                        if n >= 1:
                            stt(k, par, n - 1, q)
                        elif not first and q == TT - 2:
                            stt(k - 1, 1 - par, DS - 1, TT - 1)
                        if not first:
                            back(n, q, k - 1, 1 - par)
                        if not last:
                            front(n, q, k + 1, 1 - par)
                    if par == 0:
                        save(k, n)

            for s in range(DS):
                for q in range(DT):
                    front(s, q, 0, 0)
            step(0, 0, first=True)
            step(1, 1)
            with dve.Fori(1, IMAGES - 1) as j:
                step(2 * j, 0)
                step(2 * j + 1, 1)
            step(CHUNKS - 2, 0)
            step(CHUNKS - 1, 1, last=True)
            for t in range(TT):
                stt(CHUNKS - 1, 1, DS - 1, t)
            for d in range(DT):
                b_yb(CHUNKS - 1, 1, d)
            for c in range(KT):
                b_xo(CHUNKS - 1, c)

        @block.gpsimd
        def _(pool):
            tt = nc.gpsimd.tensor_tensor

            def rounding(kk, par, r):
                need(pool, v_w1, 1, kk, 1)
                t2 = slice(2 * r, 2 * r + 2)
                tt(ub[:, par, t2, :], cacc[:, t2, :], ub[:, par, t2, :], ALU.subtract).then_inc(g_w, 1)

            def dt_x(kk, par):
                need(pool, v_dt, 2, kk, 2)
                tt(ub[:, par, :, :], dtb[:, par, :, :], xin[:, par, :, :], ALU.mult).then_inc(g_u, 1)

            def bu(k, par, n):
                if n == 0:
                    need(pool, g_u, 1, k, 1)
                need(pool, s_row[n % RING], 16 * DS // RING, k, 16 * (n // RING + 1))
                need(pool, v_scan, DT * DS, k, DT * (n - 2) + DT)
                tt(dbu[:, n % 2, :, :], ub[:, par, :, :], bbc[:, n % RING, None, :].to_broadcast([P, DT, T]), ALU.mult).then_inc(g_bu, 1)

            def gate(kk, par, d):
                need(pool, v_yb, DT, kk, DT)
                need(pool, a_sz, 1, kk, 1)
                tt(yb[:, d, :], yb[:, d, :], sz[:, par, d, :], ALU.mult).then_inc(g_g, 1)

            def step(k, par, first=False, last=False):
                for n in range(DS):
                    bu(k, par, n)
                    if not first and 4 <= n < 4 + DT:
                        gate(k - 1, 1 - par, n - 4)
                    if not last and n in (13, 14):
                        rounding(k + 1, 1 - par, n - 13)
                    if not last and n == 15:
                        dt_x(k + 1, 1 - par)

            rounding(0, 0, 0)
            rounding(0, 0, 1)
            dt_x(0, 0)
            step(0, 0, first=True)
            step(1, 1)
            with pool.Fori(1, IMAGES - 1) as j:
                step(2 * j, 0)
                step(2 * j + 1, 1)
            step(CHUNKS - 2, 0)
            step(CHUNKS - 1, 1, last=True)
            for d in range(DT):
                gate(CHUNKS - 1, 1, d)
def gate_and_norm(nc, state, w, out):
    HS = C // 4
    SL = N // 512
    ctx = ExitStack()
    with ctx:
        def sb(n, s):
            return ctx.enter_context(nc.sbuf_tensor("c_" + n, s, F32))

        def sem(n):
            return ctx.enter_context(nc.semaphore("c_" + n))

        y = sb("y", [P, B, KT, N])
        res = sb("res", [P, 4, KT, N])
        w1 = sb("w1", [P, KT, HS])
        w2 = sb("w2", [HS, C])
        b1 = sb("b1", [HS, 1])
        vec = sb("vec", [P, 3, KT])
        gsum = sb("gsum", [P, KT, B])
        hid = sb("hid", [HS, B])
        gate = sb("gate", [P, KT, B])
        stats = sb("stats", [P, KT, B * SL, 6])
        agg = sb("agg", [P, KT, 2])
        tmp = sb("tmp", [P, 6, KT])
        pz = ctx.enter_context(nc.psum_tensor("c_pz", [P, 64], F32))

        s_w, s_st = sem("weights"), sem("store_done")
        s_x = [sem("x%d" % b) for b in range(B)]
        s_r = [sem("res%d" % b) for b in range(4)]
        v_sum, p_h, a_h, p_g, a_g, v_y, v_bn, v_agg, v_tmp, a_tmp, v_out = (sem(n) for n in (
            "sum", "hid_ps", "hid", "gate_ps", "gate", "y", "bn", "agg", "tmp", "lnexp", "out"))
        st_v = state.rearrange("i (k p) n -> i p k n", p=P)
        out_v = out.rearrange("b (k p) n -> b p k n", p=P)
        block = ctx.enter_context(nc.Block())

        @block.sync
        def _(sp):
            for b in range(B):
                sp.dma_start(y[:, b], st_v[IMAGES + b]).then_inc(s_x[b], 16)
            for dst, name in ((w1[:], "w1"), (w2[:], "w2"), (b1[:], "b1"), (vec[:], "vec")):
                sp.dma_start(dst, w[name]).then_inc(s_w, 16)
            for b in range(B):
                if b >= 4:
                    sp.wait_ge(v_y, KT * (b - 3))
                sp.dma_start(res[:, b % 4], st_v[b]).then_inc(s_r[b % 4], 16)
            for b in range(B):
                sp.wait_ge(v_out, KT * (b + 1))
                sp.dma_start(out_v[b], y[:, b]).then_inc(s_st, 16)
            sp.wait_ge(s_st, 16 * B)

        @block.tensor
        def _(pe):
            pe.wait_ge(s_w, 64)
            pe.wait_ge(v_sum, B * KT)
            for c in range(KT):
                i = nc.tensor.matmul(pz[0:HS, 0:B], w1[:, c, :], gsum[:, c, :], start=(c == 0), stop=(c == KT - 1))
            i.then_inc(p_h, 1)
            pe.wait_ge(a_h, 1)
            for c in range(KT):
                i = nc.tensor.matmul(pz[:, 16 + c * B:16 + (c + 1) * B], w2[:, c * P:(c + 1) * P], hid[:], start=True, stop=True)
            i.then_inc(p_g, 1)

        @block.scalar
        def _(act):
            av = nc.scalar.activation
            act.wait_ge(p_h, 1)
            av(hid[:], pz[0:HS, 0:B], ACT.Relu, scale=1.0 / N, bias=b1[:, 0:1]).then_inc(a_h, 1)
            act.wait_ge(p_g, 1)
            for c in range(KT):
                av(gate[:, c, :], pz[:, 16 + c * B:16 + (c + 1) * B], ACT.Sigmoid, bias=vec[:, 0, c:c + 1]).then_inc(a_g, 1)
            act.wait_ge(v_tmp, 1)
            av(tmp[:, 1, :], tmp[:, 0, :], ACT.Ln).then_inc(a_tmp, 1)
            act.wait_ge(a_tmp, 1)
            av(tmp[:, 2, :], tmp[:, 1, :], ACT.Exp, scale=-0.5).then_inc(a_tmp, 1)

        def stats_of(dve, b):
            for c in range(KT):
                dve.wait_ge(v_y, KT * b + c + 1)
                for s in range(SL):
                    nc.vector.bn_stats(stats[:, c, b * SL + s, :], y[:, b, c, s * 512:(s + 1) * 512]).then_inc(v_bn, 1)

        @block.vector
        def _(dve):
            v = nc.vector
            for b in range(B):
                dve.wait_ge(s_x[b], 16)
                for c in range(KT):
                    v.reduce_sum(gsum[:, c, b:b + 1], y[:, b, c, :], mybir.AxisListType.X).then_inc(v_sum, 1)
            dve.wait_ge(a_g, KT)
            for b in range(B):
                dve.wait_ge(s_r[b % 4], 16 * (b // 4 + 1))
                for c in range(KT):
                    v.scalar_tensor_tensor(y[:, b, c, :], y[:, b, c, :], gate[:, c, b:b + 1], res[:, b % 4, c, :],
                                           ALU.mult, ALU.add).then_inc(v_y, 1)
                if b:
                    stats_of(dve, b - 1)
            stats_of(dve, B - 1)
            dve.wait_ge(v_bn, B * KT * SL)
            for c in range(KT):
                v.bn_aggr(agg[:, c, :], stats[:, c, :, :].rearrange("p a b -> p (a b)")).then_inc(v_agg, 1)
            dve.wait_ge(v_agg, KT)
            n = [0]

            def link(i):
                n[0] += 1
                i.then_inc(v_tmp, 1)
                dve.wait_ge(v_tmp, n[0])
            link(v.tensor_scalar(tmp[:, 0, :], agg[:, :, 1], LN_EPS, None, ALU.add))
            dve.wait_ge(a_tmp, 2)
            link(v.tensor_tensor(tmp[:, 3, :], tmp[:, 2, :], tmp[:, 2, :], ALU.mult))
            link(v.scalar_tensor_tensor(tmp[:, 1, :], tmp[:, 3, :], -0.5, tmp[:, 0, :], ALU.mult, ALU.mult))
            link(v.scalar_tensor_tensor(tmp[:, 3, :], tmp[:, 1, :], 1.5, tmp[:, 2, :], ALU.add, ALU.mult))
            link(v.tensor_tensor(tmp[:, 4, :], tmp[:, 3, :], vec[:, 1, :], ALU.mult))
            link(v.tensor_tensor(tmp[:, 5, :], tmp[:, 4, :], agg[:, :, 0], ALU.mult))
            link(v.tensor_tensor(tmp[:, 5, :], vec[:, 2, :], tmp[:, 5, :], ALU.subtract))
            for b in range(B):
                for c in range(KT):
                    v.tensor_scalar(y[:, b, c, :], y[:, b, c, :], tmp[:, 4, c:c + 1], tmp[:, 5, c:c + 1],
                                    ALU.mult, ALU.add).then_inc(v_out, 1)


def constants():
    return {
        "ident": np.eye(P, dtype=np.float32),
        "ones_c": np.full((P, P), 1.0 / C, np.float32),
        "ones": np.ones((P, P), np.float32),
    }


def chan(a, tiles):
    a = a.reshape(a.shape[0], tiles, P, -1)
    return np.ascontiguousarray(a.transpose(0, 2, 1, 3))


def mamba_weights(inp):
    g = {k[len("L1_conv_"):]: np.asarray(v) for k, v in inp.items() if k.startswith("L1_conv_")}
    xw = g["x_proj_w"].transpose(0, 2, 1)
    xw_t = chan(xw, DT)
    small = np.concatenate([
        chan(g["conv_w"], DT).reshape(NL, P, -1), chan(g["conv_b"], DT).reshape(NL, P, -1),
        chan(g["A_log"], DT).reshape(NL, P, -1), chan(g["ln_w"], KT).reshape(NL, P, -1),
        chan(g["ln_b"], KT).reshape(NL, P, -1)], axis=2)
    return {
        "iw": chan(g["in_proj_w"].transpose(0, 2, 1), KT),
        "xw_dt": np.ascontiguousarray(xw_t[..., 0:DTR]),
        "xw_b": np.ascontiguousarray(xw_t[..., DTR:DTR + DS]),
        "xw_c": np.ascontiguousarray(xw_t[..., DTR + DS:]),
        "small": np.ascontiguousarray(small),
        "dw": np.ascontiguousarray(np.concatenate([g["dt_proj_w"].transpose(0, 2, 1), g["dt_proj_b"][:, None, :]], axis=1)),
        "ow": chan(g["out_proj_w"].transpose(0, 2, 1), DT),
        "dskip": chan(g["D"], DT).reshape(NL, P, DT),
    }


def patch_basis():
    yy, xx = np.meshgrid(np.arange(8), np.arange(8), indexing="ij")
    basis, weight, picks = [], [], []
    for kx in range(5):
        for ky in range(8):
            edge = kx in (0, 4)
            if edge and ky > 4:
                continue
            phase = (2 * np.pi / 8) * ((ky * yy + kx * xx) % 8)
            keys = {(ky, kx), ((8 - ky) % 8, kx)} if edge else {(ky, kx)}
            for f in ((np.cos,) if edge and ky in (0, 4) else (np.cos, np.sin)):
                basis.append(f(phase).reshape(64))
                weight.append((1.0 if edge else 2.0) / 64)
                picks.append(keys)
    return np.array(basis), np.array(weight), picks


def fft_constants():
    basis, weight, picks = patch_basis()
    dft = np.zeros((P, P), np.float32)
    idft = np.zeros((P, P), np.float32)
    for patch in range(2):
        tok = (np.arange(8)[:, None] * 16 + patch * 8 + np.arange(8)[None, :]).reshape(64)
        fr = patch * 64 + np.arange(64)
        dft[np.ix_(tok, fr)] = basis.T
        idft[np.ix_(fr, tok)] = basis * weight[:, None]
    fsel = np.zeros((40, P), np.float32)
    for f, keys in enumerate(picks):
        for ky, kx in keys:
            fsel[ky * 5 + kx, [f, 64 + f]] = 1.0
    return {"dft": dft, "idft": idft, "fsel": fsel}


def rows(a, tiles):
    return np.ascontiguousarray(a.reshape(tiles, P, -1).transpose(1, 0, 2))


def conv_weights(inp):
    g = {k[len("L0_conv_"):]: np.asarray(v) for k, v in inp.items() if k.startswith("L0_conv_")}
    heads = np.arange(NH)[:, None] * (2 * KD + HD)
    order = np.concatenate([(heads + np.arange(KD)).reshape(-1), (heads + KD + np.arange(KD)).reshape(-1),
                            (heads + 2 * KD + np.arange(HD)).reshape(-1)])
    par = [np.concatenate([g["qkv_" + s][order], g["pe_" + s], g["proj_" + s]]) for s in "gbmv"]
    bn = np.stack(par)
    vec = np.stack([g[k].reshape(C) for k in ("norm1_w", "norm1_b", "norm2_w", "norm2_b", "gamma1", "gamma2")])
    return {
        "qkv": rows(g["qkv_w"][order].T, KT),
        "proj": rows(g["proj_w"].T, KT),
        "pi": rows(g["pi_w"].T, KT),
        "po": rows(g["po_w"].T, HT),
        "bn": np.ascontiguousarray(bn.reshape(4, 8, P).transpose(2, 0, 1)),
        "vec": np.ascontiguousarray(vec.reshape(6, KT, P).transpose(2, 0, 1)),
        "pe": rows(g["pe_w"].reshape(C, 9), KT),
        "dw": rows(g["dw_w"].reshape(2 * HID, 9), 2 * HT),
        "fftp": np.ascontiguousarray(g["fft_p"].reshape(C, 40).T),
    }


def gate_weights(inp):
    g = {k[len("L1_conv_"):]: np.asarray(v) for k, v in inp.items() if k.startswith("L1_conv_")}
    vec = np.stack([g["se_b2"], g["bn_w"], g["bn_b"]])
    return {
        "w1": rows(g["se_w1"].T, KT),
        "w2": np.ascontiguousarray(g["se_w2"].T),
        "b1": g["se_b1"].reshape(C // 4, 1),
        "vec": np.ascontiguousarray(vec.reshape(3, KT, P).transpose(2, 0, 1)),
    }


def build(nc, args):
    state = nc.dram_tensor("state", (IMAGES + B, C, N), F32, kind="Internal").ap()
    conv_block(nc, args["x"], state, args["conv"], args["const"])
    mamba_layers(nc, state, args["mamba"], args["const"])
    gate_and_norm(nc, state, args["gate"], args["out"])


def kernel(**inputs):
    import concourse.bacc as _bacc
    from concourse.bass_utils import run_bass_kernel_spmd as _run

    nc = _bacc.Bacc("TRN2", target_bir_lowering=False, num_devices=1)
    arrays = {}

    def dram(name, a):
        a = np.ascontiguousarray(a)
        arrays[name] = a
        return nc.dram_tensor(name, a.shape, F32, kind="ExternalInput").ap()

    args = {"x": dram("x", np.asarray(inputs["x"]).reshape(B, C, N))}
    for group, parts in (("conv", conv_weights(inputs)), ("mamba", mamba_weights(inputs)), ("gate", gate_weights(inputs)),
                         ("const", {**constants(), **fft_constants()})):
        args[group] = {k: dram(group + "_" + k, v) for k, v in parts.items()}
    out = nc.dram_tensor("out", (B, C, H, W), F32, kind="ExternalOutput").ap()
    args["out"] = out.rearrange("b c h w -> b c (h w)")
    build(nc, args)
    r = _run(nc, [arrays], core_ids=[0])
    return r.results[0]["out"]
```

```python
from contextlib import ExitStack

import numpy as np
import concourse.bass as bass
from concourse import mybir

P = 128
F32 = mybir.dt.float32
ALU = mybir.AluOpType
ACT = mybir.ActivationFunctionType

B, C, H, W = 8, 256, 32, 32
N = H * W
KT = C // P
NL, DS, DI, DTR, TAPS = 4, 16, 512, 16, 4
DT = DI // P
T = 512
TT = T // P
HALVES = N // T
IMAGES = NL * B
CHUNKS = IMAGES * HALVES
RING = 4
STT = TT * (DS - 1)
DAB = 3
BROW = 32
SMALL = DT * TAPS + DT + DT * DS + 2 * KT
O_CW, O_CB = 0, DT * TAPS
O_AL = O_CB + DT
O_LW = O_AL + DT * DS
O_LB = O_LW + KT
LN_EPS = 1e-5


def need(eng, sem, per, k, n):
    v = per * k + n
    if isinstance(v, int) and v <= 0:
        return
    eng.wait_ge(sem, v)


NH, KD, HD = 4, 32, 64
SCALE = KD ** -0.5
HID = 2 * C
HT = HID // P
NT = N // P
PW = W + 2
PS_ = 8
RMS_EPS = 1e-6
BN_EPS = 1e-5
HK = 2 * HT
UNITS = NT * NH


def conv_block(nc, x_in, state, w, consts):
    ctx = ExitStack()
    with ctx:
        def sb(n, s):
            return ctx.enter_context(nc.sbuf_tensor("a_" + n, s, F32))

        def sem(n):
            return ctx.enter_context(nc.semaphore("a_" + n))

        ident = sb("ident", [P, P])
        ones_c = sb("ones_c", [P, P])
        ones = sb("ones", [P, P])
        dft = sb("dft", [P, P])
        idft = sb("idft", [P, P])
        fsel = sb("fsel", [40, P])
        fftp = sb("fftp", [40, C])
        filt = sb("filt", [P, C])
        wqkv = sb("wqkv", [P, KT, 4 * P])
        wproj = sb("wproj", [P, KT, C])
        wpi = sb("wpi", [P, KT, 2 * HID])
        wpo = sb("wpo", [P, HT, C])
        bn = sb("bn", [P, 4, 8])
        bns = sb("bns", [P, 6, 8])
        vec = sb("vec", [P, 6, KT])
        pew = sb("pew", [P, KT, 9])
        dww = sb("dww", [P, 2 * HT, 9])
        xb = sb("xb", [P, 2, KT, N])
        xn = sb("xn", [P, KT, N])
        sq = sb("sq", [P, KT, N])
        lnv = sb("lnv", [P, 5, NT])
        dg = sb("dg", [P, NT, P])
        qh = sb("qh", [P, NH, N])
        kh = sb("kh", [P, N])
        vpad = sb("vpad", [P, KT, PW, PW])
        vt = sb("vt", [P, NT, C])
        cv = sb("cv", [P, KT, N])
        prob = sb("prob", [P, 2, N])
        probt = sb("probt", [P, 2, N])
        pt = prob[:, 0, :].rearrange("p (a b) -> p a b", b=C)
        zf = probt[:, 0, :].rearrange("p (a b) -> p a b", b=C)
        nmx = sb("nmx", [P, 2, UNITS])
        rsum = sb("rsum", [P, 2, UNITS])
        otok = sb("otok", [P, 2, C])
        hpad = sb("hpad", [P, HK, PW, PW])
        hcv = sb("hcv", [P, 2, N])
        gl = sb("gl", [P, N])
        g = sb("g", [P, HT, N])

        def pair(n):
            return ctx.enter_context(nc.psum_tensor("a_" + n, [P, N], F32))
        PP = [pair("p0"), pair("p1"), pair("p2"), pair("p3")]

        s_w, s_x, s_st = sem("weights"), sem("x_loaded"), sem("store_done")
        p_var, p_bc, p_qkv, p_vt, p_s, p_t, p_av, p_ot, p_pj, p_pi, p_po, p_dft, p_idft, p_filt = (sem("pe_" + n) for n in (
            "var", "bc", "qkv", "vt", "s", "t", "av", "ot", "pj", "pi", "po", "dft", "idft", "filt"))
        a_sq, a_rs, a_qkv, a_cv0, a_exp, a_pt, a_pj, a_pad, a_h0, a_gl, a_po, a_bn, a_vt, a_vc = (sem("act_" + n) for n in (
            "sq", "rs", "qkv", "cv0", "exp", "probt", "pj", "pad", "h0", "gelu", "po", "bn", "vt", "vc"))
        v_rs, v_dg, v_xh, v_xn, v_max, v_nmx, v_on, v_o, v_cv, v_x1, v_h, v_zf, v_x2, v_bn, v_filt, v_zero, v_rc = (
            sem("dve_" + n) for n in (
                "rs", "dg", "xh", "xn", "max", "neg_max", "otok", "o", "cv", "x1", "h", "zf", "x2", "bn", "filt", "zero", "rsum"))
        g_g = sem("pool_g")

        N_W = 15
        x_v = x_in.rearrange("b (k p) n -> b p k n", p=P)
        st_v = state.rearrange("i (k p) n -> i p k n", p=P)

        def inner(pad, t):
            return pad[:, t, 1:1 + H, 1:1 + W]

        def image(a):
            return a.rearrange("p (r c) -> p r c", c=W)

        def at(unit, piece):
            return 2 * unit + piece

        def images(eng, one, tail):
            one(0, 0)
            one(1, 1)
            with eng.Fori(1, B // 2 - 1) as j:
                one(2 * j, 0)
                one(2 * j + 1, 1)
            one(B - 2, 0)
            one(B - 1, 1)
            tail(B - 1, 1)

        def is_first(b):
            return isinstance(b, int) and b == 0

        def is_last(b):
            return isinstance(b, int) and b == B - 1

        block = ctx.enter_context(nc.Block())

        @block.sync
        def _(sp):
            def load(b, par):
                need(sp, s_st, 16, b - 2, 16)
                sp.dma_start(xb[:, par], x_v[b]).then_inc(s_x, 16)

            def store(b, par):
                need(sp, v_x2, 4, b, 4)
                sp.dma_start(st_v[b], xb[:, par]).then_inc(s_st, 16)

            load(0, 0)
            for dst, name in ((ident[:], "ident"), (ones_c[:], "ones_c"), (ones[:], "ones"), (dft[:], "dft"), (idft[:], "idft"),
                              (fsel[:], "fsel")):
                sp.dma_start(dst, consts[name]).then_inc(s_w, 16)
            for dst, name in ((fftp[:], "fftp"), (wqkv[:], "qkv"), (wproj[:], "proj"), (wpi[:], "pi"), (wpo[:], "po"),
                              (bn[:], "bn"), (vec[:], "vec"), (pew[:], "pe"), (dww[:], "dw")):
                sp.dma_start(dst, w[name]).then_inc(s_w, 16)
            sp.wait_ge(s_x, 16)
            load(1, 1)
            with sp.Fori(0, B // 2 - 1) as j:
                for par in range(2):
                    store(2 * j + par, par)
                    load(2 * j + par + 2, par)
            store(B - 2, 0)
            store(B - 1, 1)
            sp.wait_ge(s_st, 16 * B)

        @block.tensor
        def _(pe):
            mm = nc.tensor.matmul
            tr = nc.tensor.transpose
            pe.wait_ge(s_w, 16 * N_W)
            mm(PP[3][:, 0:C], fsel[:], fftp[:], start=True, stop=True).then_inc(p_filt, 1)

            def dense(dst, wt, src, o, tiles=KT):
                for hf in range(2):
                    for c in range(tiles):
                        i = mm(dst[:, hf * 512:(hf + 1) * 512], wt[:, c, o:o + P], src[:, c, hf * 512:(hf + 1) * 512],
                               start=(c == 0), stop=(c == tiles - 1))
                return i

            def norm_var(b, which):
                need(pe, a_sq, 2, b, which + 1)
                if which == 1:
                    need(pe, a_pt, UNITS, b, UNITS)
                else:
                    need(pe, v_xh, 4, b - 1, 4)
                for t in range(NT):
                    for c in range(KT):
                        i = mm(PP[2][:, t:t + 1], sq[:, c, t * P:(t + 1) * P], ones_c[:, 0:1],
                               start=(c == 0), stop=(c == KT - 1))
                i.then_inc(p_var, 1)

            def norm_bc(b, which):
                need(pe, v_dg, 2, b, which + 1)
                for hf in range(2):
                    i = mm(PP[2][:, hf * 512:(hf + 1) * 512], ones[:],
                           dg[:, hf * 4:(hf + 1) * 4, :].rearrange("p a b -> p (a b)"), start=True, stop=True)
                i.then_inc(p_bc, 1)

            def scores(b, u):
                nt, h = u // NH, u % NH
                if u >= 2:
                    need(pe, a_exp, UNITS, b, u - 1)
                else:
                    need(pe, a_vt, 2, b, u + 1)
                for hf in range(2):
                    i = mm(PP[u % 2][:, hf * 512:(hf + 1) * 512], qh[:, h, nt * P:(nt + 1) * P],
                           kh[:, hf * 512:(hf + 1) * 512], start=True, stop=True)
                i.then_inc(p_s, 1)

            def turn(b, u):
                need(pe, a_exp, UNITS, b, u + 1)
                if u >= 1:
                    need(pe, a_pt, UNITS, b, u)
                for m in range(NT):
                    i = tr(PP[2][:, m * P:(m + 1) * P], prob[:, u % 2, m * P:(m + 1) * P], ident[:])
                i.then_inc(p_t, 1)

            def values(b, u):
                nt, h = u // NH, u % NH
                bank = PP[3][:, (nt % 2) * 512:(nt % 2) * 512 + 512]
                need(pe, a_pt, UNITS, b, u + 1)
                if h == 0:
                    if nt >= 1:
                        need(pe, v_o, NT, b, nt - 1)
                    if nt < 2:
                        need(pe, v_x2, 4, b - 2, 4)
                        if is_first(b):
                            pe.wait_ge(v_filt, 1)
                for m in range(NT):
                    i = mm(bank[:, h * HD:(h + 1) * HD], probt[:, u % 2, m * P:(m + 1) * P],
                           vt[:, m, h * HD:(h + 1) * HD], start=(m == 0), stop=(m == NT - 1))
                i.then_inc(p_av, 1)

            def back(b, nt):
                need(pe, v_on, NT, b, nt + 1)
                bank = PP[3][:, (nt % 2) * 512:(nt % 2) * 512 + 512]
                for c in range(KT):
                    i = tr(bank[:, C + c * P:C + (c + 1) * P], otok[:, nt % 2, c * P:(c + 1) * P], ident[:])
                i.then_inc(p_ot, 1)

            def out_and_dft(e, i2, bank_free):
                if i2 == 0:
                    need(pe, g_g, HT, e, HT)
                    bank_free()
                else:
                    need(pe, a_po, 2, e, 1)
                for t in range(4):
                    for j in range(HT):
                        tile = i2 * 4 + t
                        i = mm(PP[0][:, t * C:(t + 1) * C], g[:, j, tile * P:(tile + 1) * P], wpo[:, j, :],
                               start=(j == 0), stop=(j == HT - 1))
                i.then_inc(p_po, 1)
                need(pe, a_po, 2, e, i2 + 1)
                if i2:
                    need(pe, v_zf, 2, e, 1)
                for hf in range(2):
                    i = mm(PP[1][:, hf * 512:(hf + 1) * 512], dft[:], prob[:, 0, hf * 512:(hf + 1) * 512],
                           start=True, stop=True)
                i.then_inc(p_dft, 1)

            def inverse(e, i2):
                need(pe, v_zf, 2, e, i2 + 1)
                if i2:
                    need(pe, v_x2, 4, e, 2)
                for c in range(KT):
                    bank = image(PP[3][:, c * 512:(c + 1) * 512])
                    for t in range(4):
                        r0 = (t // 2) * PS_
                        i = mm(bank[:, r0:r0 + PS_, (t % 2) * 16:(t % 2) * 16 + 16], zf[:, t, c * P:(c + 1) * P], idft[:],
                               start=True, stop=True)
                i.then_inc(p_idft, 1)

            def one(b, par):
                edffn = not is_first(b)
                need(pe, v_xn, 2, b, 1)
                for i in range(4):
                    if i >= 2:
                        need(pe, a_qkv, 4, b, i - 1)
                    else:
                        need(pe, a_pad, HK, b - 1, HK - 1 + i)
                    dense(PP[i % 2], wqkv, cv, i * P).then_inc(p_qkv, 1)
                need(pe, a_qkv, 4, b, 4)
                need(pe, a_vc, 2, b, 2)
                for hf in range(2):
                    for m in range(4):
                        mt = hf * 4 + m
                        for c in range(KT):
                            i = tr(PP[hf][:, m * C + c * P:m * C + (c + 1) * P], sq[:, c, mt * P:(mt + 1) * P], ident[:])
                    i.then_inc(p_vt, 1)
                for u in range(UNITS + 3):
                    if u < UNITS:
                        scores(b, u)
                    if 0 <= u - 1 < UNITS:
                        turn(b, u - 1)
                    if 0 <= u - 2 < UNITS:
                        values(b, u - 2)
                    if u >= 6 and (u - 6) % NH == 0 and (u - 6) // NH < NT - 1:
                        back(b, (u - 6) // NH)
                back(b, NT - 1)
                need(pe, v_o, NT, b, NT)
                need(pe, a_exp, UNITS, b, UNITS)
                for c in range(KT):
                    dense(PP[c], wproj, cv, c * P).then_inc(p_pj, 1)
                if edffn:
                    out_and_dft(b - 1, 0, lambda: need(pe, a_pj, KT, b, KT))
                norm_var(b, 1)
                if edffn:
                    inverse(b - 1, 0)
                    out_and_dft(b - 1, 1, None)
                norm_bc(b, 1)
                if edffn:
                    inverse(b - 1, 1)
                need(pe, v_xn, 2, b, 2)
                if not edffn:
                    need(pe, a_pj, KT, b, KT)
                for k in range(HK):
                    if k >= 2:
                        need(pe, a_pad, HK, b, k - 1)
                    dense(PP[k % 2], wpi, xn, ((k % 2) * HT + k // 2) * P).then_inc(p_pi, 1)
                    if k == 5 and not is_last(b):
                        norm_var(b + 1, 0)
                if not is_last(b):
                    norm_bc(b + 1, 0)

            def tail(e, par):
                for i2 in range(2):
                    out_and_dft(e, i2, lambda: need(pe, a_pad, HK, e, HK))
                    inverse(e, i2)

            norm_var(0, 0)
            norm_bc(0, 0)
            images(pe, one, tail)

        @block.scalar
        def _(act):
            av = nc.scalar.activation
            act.wait_ge(v_bn, 1)
            av(bns[:, 1, :], bns[:, 0, :], ACT.Ln).then_inc(a_bn, 1)
            act.wait_ge(a_bn, 1)
            av(bns[:, 2, :], bns[:, 1, :], ACT.Exp, scale=-0.5).then_inc(a_bn, 1)

            def norm_sq(b, par, which):
                if which == 0:
                    need(act, s_x, 16, b, 16)
                    need(act, p_var, 2, b - 1, 2)
                else:
                    need(act, v_x1, KT, b, KT)
                av(sq[:], xb[:, par], ACT.Square).then_inc(a_sq, 1)

            def norm_rs(b, which):
                need(act, v_rs, 8, b, 4 * which + 1)
                av(lnv[:, 1, :], lnv[:, 0, :], ACT.Ln).then_inc(a_rs, 1)
                need(act, a_rs, 4, b, 2 * which + 1)
                av(lnv[:, 2, :], lnv[:, 1, :], ACT.Exp, scale=-0.5).then_inc(a_rs, 1)

            def tap0(e, k):
                j, q = k // 2, k % 2
                need(act, a_pad, HK, e, k + 1)
                if q == 0:
                    need(act, a_gl, HT, e, j)
                else:
                    need(act, g_g, HT, e, j)
                av(image(hcv[:, q, :]), hpad[:, k, 0:H, 0:W], ACT.Copy, scale=dww[:, q * HT + j, 0:1]).then_inc(a_h0, 1)

            def gelu(e, j):
                need(act, v_h, 8 * HK, e, 16 * j + 8)
                need(act, g_g, HT, e, j)
                av(gl[:], hcv[:, 0, :], ACT.Gelu).then_inc(a_gl, 1)

            def conv(e, u):
                if u % 8 == 4:
                    gelu(e, u // 8)
                if u % 4 == 3 and u < UNITS - 1:
                    tap0(e, u // 4 + 1)

            def out_copy(e, i2):
                need(act, p_po, 2, e, i2 + 1)
                need(act, p_dft, 2, e, i2)
                av(pt, PP[0][:].rearrange("p (a b) -> p a b", b=C), ACT.Copy).then_inc(a_po, 1)

            def one(b, par):
                edffn = not is_first(b)
                if is_first(b):
                    act.wait_ge(v_bn, 8)
                for i in range(4):
                    need(act, p_qkv, 4, b, i + 1)
                    src = PP[i % 2][:]
                    if i == 0:
                        if is_first(b):
                            act.wait_ge(v_zero, 3)
                        for h in range(NH):
                            r = slice(h * KD, (h + 1) * KD)
                            o = av(qh[r, h, :], PP[0][r, :], ACT.Identity, scale=bns[r, 4, 0:1], bias=bns[r, 5, 0:1])
                        o.then_inc(a_qkv, 1)
                    elif i == 1:
                        av(kh[:], src, ACT.Identity, scale=bns[:, 4, 1:2], bias=bns[:, 5, 1:2]).then_inc(a_qkv, 1)
                    else:
                        if i == 2:
                            need(act, v_cv, 16, b - 1, 16)
                            if is_first(b):
                                act.wait_ge(v_zero, 1)
                        av(sq[:, i - 2, :], src, ACT.Identity, scale=bns[:, 4, i:i + 1], bias=bns[:, 5, i:i + 1]).then_inc(a_vc, 1)
                        av(inner(vpad, i - 2), image(src), ACT.Identity, scale=bns[:, 4, i:i + 1], bias=bns[:, 5, i:i + 1]).then_inc(a_qkv, 1)
                for hf in range(2):
                    need(act, p_vt, 2, b, hf + 1)
                    av(vt[:, hf * 4:(hf + 1) * 4, :], PP[hf][:].rearrange("p (a b) -> p a b", b=C), ACT.Copy).then_inc(a_vt, 1)
                for c in range(KT):
                    need(act, a_qkv, 4, b, c + 3)
                    av(image(cv[:, c, :]), vpad[:, c, 0:H, 0:W], ACT.Identity, scale=pew[:, c, 0:1],
                       bias=bns[:, 5, 4 + c:5 + c]).then_inc(a_cv0, 1)
                if edffn:
                    tap0(b - 1, 0)
                for u in range(UNITS + 1):
                    if u < UNITS:
                        need(act, v_nmx, UNITS, b, u + 1)
                        if u >= 2:
                            need(act, p_t, UNITS, b, u - 1)
                        av(prob[:, u % 2, :], PP[u % 2][:], ACT.Exp, scale=SCALE, bias=nmx[:, 1, u:u + 1],
                           accum_out=rsum[:, 0, u:u + 1]).then_inc(a_exp, 1)
                    if u >= 1:
                        need(act, p_t, UNITS, b, u)
                        if u >= 3:
                            need(act, p_av, UNITS, b, u - 2)
                        av(probt[:, (u - 1) % 2, :], PP[2][:], ACT.Copy).then_inc(a_pt, 1)
                    if edffn and u < UNITS:
                        conv(b - 1, u)
                for c in range(KT):
                    need(act, p_pj, KT, b, c + 1)
                    av(sq[:, c, :], PP[c][:], ACT.Identity, scale=bns[:, 4, 6 + c:7 + c], bias=bns[:, 5, 6 + c:7 + c]).then_inc(a_pj, 1)
                norm_sq(b, par, 1)
                if edffn:
                    out_copy(b - 1, 0)
                norm_rs(b, 1)
                if edffn:
                    out_copy(b - 1, 1)
                for k in range(HK):
                    need(act, p_pi, HK, b, k + 1)
                    need(act, v_h, 8 * HK, b - 1, 8 * k + 8)
                    if is_first(b) and k == 0:
                        act.wait_ge(v_zero, 2)
                    av(inner(hpad, k), image(PP[k % 2][:]), ACT.Copy).then_inc(a_pad, 1)
                    if not is_last(b):
                        if k == 4:
                            norm_sq(b + 1, 1 - par, 0)
                        if k == 6:
                            norm_rs(b + 1, 0)

            def tail(e, par):
                tap0(e, 0)
                for u in range(UNITS):
                    conv(e, u)
                for i2 in range(2):
                    out_copy(e, i2)

            norm_sq(0, 0, 0)
            norm_rs(0, 0)
            images(act, one, tail)

        @block.vector
        def _(dve):
            v = nc.vector
            v.memset(vpad[:], 0.0).then_inc(v_zero, 1)
            v.memset(hpad[:], 0.0).then_inc(v_zero, 1)
            v.memset(qh[:], 0.0).then_inc(v_zero, 1)
            dve.wait_ge(s_w, 16 * N_W)
            n_bn = [0]

            def link(i):
                n_bn[0] += 1
                i.then_inc(v_bn, 1)
                dve.wait_ge(v_bn, n_bn[0])
            link(v.tensor_scalar(bns[:, 0, :], bn[:, 3, :], BN_EPS, None, ALU.add))
            dve.wait_ge(a_bn, 2)
            link(v.tensor_tensor(bns[:, 3, :], bns[:, 2, :], bns[:, 2, :], ALU.mult))
            link(v.scalar_tensor_tensor(bns[:, 1, :], bns[:, 3, :], -0.5, bns[:, 0, :], ALU.mult, ALU.mult))
            link(v.scalar_tensor_tensor(bns[:, 3, :], bns[:, 1, :], 1.5, bns[:, 2, :], ALU.add, ALU.mult))
            link(v.tensor_tensor(bns[:, 4, :], bns[:, 3, :], bn[:, 0, :], ALU.mult))
            link(v.tensor_tensor(bns[:, 5, :], bns[:, 4, :], bn[:, 2, :], ALU.mult))
            link(v.tensor_tensor(bns[:, 5, :], bn[:, 1, :], bns[:, 5, :], ALU.subtract))
            for c in range(KT):
                v.tensor_scalar(pew[:, c, :], pew[:, c, :], bns[:, 4, 4 + c:5 + c], None, ALU.mult)
            for r in (4, 5):
                v.tensor_tensor(bns[:, r, 6:8], bns[:, r, 6:8], vec[:, 4, :], ALU.mult)
            link(v.memset(nmx[:], 0.0))
            dve.wait_ge(p_filt, 1)
            v.tensor_copy(filt[:], PP[3][:, 0:C]).then_inc(v_filt, 1)
            dve.wait_ge(v_filt, 1)

            def norm_dg(b, which):
                r = 8
                o = 4 * which
                need(dve, p_var, 2, b, which + 1)
                v.tensor_scalar(lnv[:, 0, :], PP[2][:, 0:NT], RMS_EPS, None, ALU.add).then_inc(v_rs, 1)
                need(dve, a_rs, 4, b, 2 * which + 2)
                v.tensor_tensor(lnv[:, 3, :], lnv[:, 2, :], lnv[:, 2, :], ALU.mult).then_inc(v_rs, 1)
                need(dve, v_rs, r, b, o + 2)
                v.scalar_tensor_tensor(lnv[:, 4, :], lnv[:, 3, :], -0.5, lnv[:, 0, :], ALU.mult, ALU.mult).then_inc(v_rs, 1)
                need(dve, v_rs, r, b, o + 3)
                v.scalar_tensor_tensor(lnv[:, 1, :], lnv[:, 4, :], 1.5, lnv[:, 2, :], ALU.add, ALU.mult).then_inc(v_rs, 1)
                need(dve, v_rs, r, b, o + 4)
                if not (is_first(b) and which == 0):
                    need(dve, p_bc, 2, b, which)
                for t in range(NT):
                    i = v.tensor_scalar(dg[:, t, :], ident[:], lnv[:, 1, t:t + 1], None, ALU.mult)
                i.then_inc(v_dg, 1)

            def norm_xn(b, par, which):
                dst = cv if which == 0 else xn
                need(dve, p_bc, 2, b, which + 1)
                if which == 0:
                    need(dve, p_pj, KT, b - 1, KT)
                else:
                    need(dve, p_pi, HK, b - 1, HK)
                for c in range(KT):
                    v.tensor_tensor(dst[:, c, :], xb[:, par, c, :], PP[2][:], ALU.mult).then_inc(v_xh, 1)
                for c in range(KT):
                    need(dve, v_xh, 4, b, 2 * which + c + 1)
                    i = v.tensor_scalar(dst[:, c, :], dst[:, c, :], vec[:, 2 * which, c:c + 1], vec[:, 2 * which + 1, c:c + 1],
                                        ALU.mult, ALU.add)
                i.then_inc(v_xn, 1)

            def pe_tap(b, k):
                c, tap = k % 2, k // 2 + 1
                if tap == 1:
                    need(dve, a_cv0, KT, b, c + 1)
                else:
                    need(dve, v_cv, 16, b, k - 1)
                dy, dx = tap // 3, tap % 3
                v.scalar_tensor_tensor(image(cv[:, c, :]), vpad[:, c, dy:dy + H, dx:dx + W], pew[:, c, tap:tap + 1],
                                       image(cv[:, c, :]), ALU.mult, ALU.add).then_inc(v_cv, 1)

            def conv(e, i):
                k, tap = i // 8, i % 8 + 1
                j, q = k // 2, k % 2
                if tap == 1:
                    need(dve, a_h0, HK, e, k + 1)
                else:
                    need(dve, v_h, 8 * HK, e, i)
                dy, dx = tap // 3, tap % 3
                v.scalar_tensor_tensor(image(hcv[:, q, :]), hpad[:, k, dy:dy + H, dx:dx + W],
                                       dww[:, q * HT + j, tap:tap + 1], image(hcv[:, q, :]),
                                       ALU.mult, ALU.add).then_inc(v_h, 1)

            def onorm(b, nt):
                need(dve, p_av, UNITS, b, NH * (nt + 1))
                need(dve, a_exp, UNITS, b, NH * (nt + 1))
                if nt >= 2:
                    need(dve, p_ot, NT, b, nt - 1)
                us = slice(NH * nt, NH * (nt + 1))
                v.reciprocal(rsum[:, 1, us], rsum[:, 0, us]).then_inc(v_rc, 1)
                need(dve, v_rc, NT, b, nt + 1)
                bank = PP[3][:, (nt % 2) * 512:(nt % 2) * 512 + C].rearrange("p (h d) -> p h d", d=HD)
                v.tensor_tensor(otok[:, nt % 2, :].rearrange("p (h d) -> p h d", d=HD), bank,
                                rsum[:, 1, us, None].to_broadcast([P, NH, HD]), ALU.mult).then_inc(v_on, 1)

            def oadd(b, nt):
                need(dve, p_ot, NT, b, nt + 1)
                if nt == 0:
                    need(dve, v_cv, 16, b, 16)
                o = (nt % 2) * 512 + C
                v.tensor_tensor(cv[:, :, nt * P:(nt + 1) * P], PP[3][:, o:o + C].rearrange("p (a b) -> p a b", b=P),
                                cv[:, :, nt * P:(nt + 1) * P], ALU.add).then_inc(v_o, 1)

            def filtered(e, i2):
                need(dve, p_dft, 2, e, i2 + 1)
                if i2:
                    need(dve, p_idft, 2, e, i2)
                else:
                    need(dve, p_idft, 2, e - 1, 2)
                v.tensor_tensor(zf, PP[1][:].rearrange("p (a b) -> p a b", b=C),
                                filt[:, None, :].to_broadcast([P, 4, C]), ALU.mult).then_inc(v_zf, 1)

            def add_edffn(e, par, i2):
                need(dve, p_idft, 2, e, i2 + 1)
                for c in range(KT):
                    o = i2 * 512
                    v.scalar_tensor_tensor(xb[:, par, c, o:o + 512], PP[3][:, c * 512:(c + 1) * 512], vec[:, 5, c:c + 1],
                                           xb[:, par, c, o:o + 512], ALU.mult, ALU.add).then_inc(v_x2, 1)

            def one(b, par):
                edffn = not is_first(b)
                for u in range(UNITS + 3):
                    if u < UNITS:
                        need(dve, p_s, UNITS, b, u + 1)
                        v.tensor_reduce(nmx[:, 0, u:u + 1], PP[u % 2][:], mybir.AxisListType.X, ALU.max, negate=True).then_inc(v_max, 1)
                        need(dve, v_max, UNITS, b, u + 1)
                        v.tensor_scalar(nmx[:, 1, u:u + 1], nmx[:, 0, u:u + 1], SCALE, None, ALU.mult).then_inc(v_nmx, 1)
                    if u < 8:
                        pe_tap(b, 2 * u)
                        pe_tap(b, 2 * u + 1)
                    if u >= 5 and (u - 5) % NH == 0 and (u - 5) // NH < NT:
                        onorm(b, (u - 5) // NH)
                    if u >= 7 and (u - 7) % NH == 0 and (u - 7) // NH < NT - 1:
                        oadd(b, (u - 7) // NH)
                    if edffn and u < UNITS:
                        conv(b - 1, at(u, 0))
                        conv(b - 1, at(u, 1))
                oadd(b, NT - 1)
                for c in range(KT):
                    need(dve, a_pj, KT, b, c + 1)
                    v.tensor_tensor(xb[:, par, c, :], xb[:, par, c, :], sq[:, c, :], ALU.add).then_inc(v_x1, 1)
                if edffn:
                    filtered(b - 1, 0)
                norm_dg(b, 1)
                if edffn:
                    add_edffn(b - 1, 1 - par, 0)
                    filtered(b - 1, 1)
                norm_xn(b, par, 1)
                if edffn:
                    add_edffn(b - 1, 1 - par, 1)
                if not is_last(b):
                    norm_dg(b + 1, 0)
                    norm_xn(b + 1, 1 - par, 0)

            def tail(e, par):
                for i in range(8 * HK):
                    conv(e, i)
                for i2 in range(2):
                    filtered(e, i2)
                    add_edffn(e, par, i2)

            dve.wait_ge(s_x, 16)
            norm_dg(0, 0)
            norm_xn(0, 0, 0)
            images(dve, one, tail)

        @block.gpsimd
        def _(pool):
            def gate(e, j):
                need(pool, a_gl, HT, e, j + 1)
                need(pool, v_h, 8 * HK, e, 16 * j + 16)
                need(pool, p_po, 2, e - 1, 2)
                for cb in range(2):
                    gv = g[:, j, :].rearrange("p (rb cb r c) -> p cb rb r c", rb=4, cb=2, r=PS_)[:, cb]
                    tok = lambda a: a.rearrange("p (rb r cb c) -> p cb rb r c", rb=4, r=PS_, cb=2)[:, cb]
                    i = nc.gpsimd.tensor_tensor(gv, tok(gl[:]), tok(hcv[:, 1, :]), ALU.mult)
                i.then_inc(g_g, 1)

            def one(b, par):
                if not is_first(b):
                    for j in range(HT):
                        gate(b - 1, j)

            def tail(e, par):
                for j in range(HT):
                    gate(e, j)

            images(pool, one, tail)
def mamba_layers(nc, state, w, consts):
    ctx = ExitStack()
    with ctx:
        def sb(n, s):
            return ctx.enter_context(nc.sbuf_tensor("m_" + n, s, F32))

        def sem(n):
            return ctx.enter_context(nc.semaphore("m_" + n))

        ident = sb("ident", [P, P])
        ones_c = sb("ones_c", [P, P])
        dtw = sb("dtw", [DTR + 1, DI])
        iw = sb("iw", [P, KT, 2 * DI])
        xw = sb("xw", [P, DT, BROW + DS])
        xwc = sb("xwc", [P, DT, DS])
        ow = sb("ow", [P, DT, C])
        dskip = sb("dskip", [P, DT])
        small = sb("small", [P, SMALL])
        aexp = sb("aexp", [P, DT * DS])
        amat = sb("amat", [P, DT * DS])
        x_sb = sb("x_sb", [P, KT, T])
        xo = sb("xo", [P, KT, T])
        xc = sb("xc", [P, KT, T])
        sq = sb("sq", [P, KT, T])
        rs = sb("rs", [P, 2, T])
        xpre = sb("xpre", [P, DT, TAPS - 1 + T])
        cacc = sb("cacc", [P, DT, T])
        tapw = sb("tapw", [P, DT * TAPS, P])
        xin = sb("xin", [P, 2, DT, T])
        sz = sb("sz", [P, 2, DT, T])
        dtb = sb("dtb", [P, 2, DT, T])
        ub = sb("ub", [P, 2, DT, T])
        spw = sb("spw", [P, DT, T])
        yb = sb("yb", [P, DT, T])
        acc = sb("acc", [P, 2, TT, DI])
        hbuf = sb("hbuf", [P, 2, DT, T])
        dbu = sb("dbu", [P, 2, DT, T])
        bbc = sb("bbc", [P, RING, T])
        pr = sb("pr", [P, 2, T])
        ctok = sb("ctok", [P, 2, TT, DS])
        carry = sb("carry", [P, DS, DT])
        eps = sb("eps", [P, 1])
        ln_one = sb("ln_one", [P, 1])

        def bank(n):
            return ctx.enter_context(nc.psum_tensor("m_" + n, [P, 512], F32))
        F = [bank("f0"), bank("f1")]
        G = bank("g")
        TP = [bank("t0"), bank("t1")]
        DA = [bank("d%d" % i) for i in range(DAB)]
        brow = nc.dram_tensor("b_rows", (2, DS, T), F32, kind="Internal").ap()

        s_const, s_x, s_win, s_wout, s_xres, s_store = (sem(n) for n in (
            "const", "x_loaded", "win_loaded", "wout_loaded", "xres_loaded", "store_done"))
        s_init = sem("init")
        s_brow = sem("b_rows_stored")
        s_row = [sem("b_row_loaded%d" % r) for r in range(RING)]
        p_mean, p_var, p_ix, p_conv, p_iz, p_proj, p_ctok, p_dt, p_ht, p_y, p_out = (sem("pe_" + n) for n in (
            "mean", "var", "ix", "conv", "iz", "proj", "ctok", "dt", "ht", "y", "out"))
        a_sq, a_rs, a_xn, a_pre, a_tapw, a_tap, a_z, a_xin, a_sz, a_proj, a_dtx, a_abs, a_e, a_l, a_da, a_acc, a_amat = (
            sem("act_" + n) for n in (
                "sq", "rs", "xn", "pre", "tap_weights", "tap", "z", "xin", "sz", "proj", "dtx", "abs", "e", "ln", "da", "acc", "amat"))
        v_xc, v_rs, v_xh, v_tail, v_ctok, v_w1, v_scan, v_stt, v_carry, v_yb, v_xo, v_dt = (
            sem("dve_" + n) for n in (
                "xc", "rs", "xh", "tail", "ctok", "w1", "scan", "stt", "carry", "yb", "xo", "dt"))
        g_w, g_u, g_bu, g_g = sem("pool_rounding"), sem("pool_u"), sem("pool_bu"), sem("pool_gate")

        state_v = state.rearrange("i (k p) n -> i p k n", p=P)
        N_WIN = 5
        N_CONST = 2

        def half(par):
            return slice(par * T, (par + 1) * T)

        block = ctx.enter_context(nc.Block())

        @block.sync
        def _(sp):
            sp.dma_start(ident[:], consts["ident"]).then_inc(s_const, 16)
            sp.dma_start(ones_c[:], consts["ones_c"]).then_inc(s_const, 16)
            sp.wait_ge(s_init, 2)

            def load_in_weights(kk, im):
                lay = im // B
                need(sp, p_ctok, 1, kk - 1, 1)
                need(sp, p_iz, DT, kk - 1, DT)
                for dst, src in ((iw[:], w["iw"]), (xw[:, :, 0:DTR], w["xw_dt"]), (xw[:, :, BROW:BROW + DS], w["xw_b"]),
                                 (xwc[:], w["xw_c"]), (small[:], w["small"])):
                    sp.dma_start(dst, src[lay]).then_inc(s_win, 16)
                sp.dma_start(dtw[:], w["dw"][lay]).then_inc(s_win, 16)

            def load_x(kk, im, par):
                need(sp, v_xc, KT, kk - 1, KT)
                sp.dma_start(x_sb[:], state_v[im][:, :, half(par)]).then_inc(s_x, 16)

            def load_out_weights(kk, im):
                lay = im // B
                need(sp, p_out, KT, kk - 1, KT)
                need(sp, v_yb, DT, kk - 1, DT)
                sp.dma_start(ow[:], w["ow"][lay]).then_inc(s_wout, 16)
                sp.dma_start(dskip[:], w["dskip"][lay]).then_inc(s_wout, 16)

            def residual(kk, im, par):
                need(sp, s_store, 16, kk - 1, 16)
                sp.dma_start(xo[:], state_v[im][:, :, half(par)]).then_inc(s_xres, 16)

            def store(kk, im, par):
                need(sp, v_xo, KT, kk, KT)
                sp.dma_start(state_v[im + B][:, :, half(par)], xo[:]).then_inc(s_store, 16)

            def keep_rows(kk, par):
                need(sp, a_proj, 2, kk, 2)
                for r in (0, DS // 2):
                    sp.dma_start(brow[par][r:r + DS // 2, :], pr[BROW + r:BROW + r + DS // 2, par, :]).then_inc(s_brow, 16)

            def row(k, par, n):
                need(sp, g_bu, DS, k, n - RING + 1)
                if n == 0:
                    need(sp, s_brow, 32, k, 32)
                sp.dma_start(bbc[:, n % RING, :], brow[par][n:n + 1, :].to_broadcast([P, T])).then_inc(s_row[n % RING], 16)

            def step(k, im, par, first=False, last=False, last2=False):
                pk = (k - 1, im if par == 1 else im - 1, 1 - par)
                for n in range(DS):
                    if not first and n == 1:
                        residual(*pk)
                    if not last and not last2 and n == 2:
                        load_x(k + 2, im + 1, par)
                    if not first and n == 15:
                        store(*pk)
                    if par == 0 and n == 14:
                        load_out_weights(k, im)
                    if not last and n == 12:
                        keep_rows(k + 1, 1 - par)
                    if n + 2 < DS:
                        row(k, par, n + 2)
                    elif not last:
                        row(k + 1, 1 - par, n + 2 - DS)
                    if par == 0 and not last2 and n == 14:
                        load_in_weights(k + 2, im + 1)

            load_in_weights(0, 0)
            load_x(0, 0, 0)
            load_x(1, 0, 1)
            keep_rows(0, 0)
            row(0, 0, 0)
            row(0, 0, 1)
            step(0, 0, 0, first=True)
            step(1, 0, 1)
            with sp.Fori(1, IMAGES - 1) as j:
                step(2 * j, j, 0)
                step(2 * j + 1, j, 1)
            step(CHUNKS - 2, IMAGES - 1, 0, last2=True)
            step(CHUNKS - 1, IMAGES - 1, 1, last=True)
            residual(CHUNKS - 1, IMAGES - 1, 1)
            store(CHUNKS - 1, IMAGES - 1, 1)
            sp.wait_ge(s_store, 16 * CHUNKS)

        def at(slot, quarter):
            return 4 * slot + quarter


        @block.tensor
        def _(pe):
            mm = nc.tensor.matmul
            pe.wait_ge(s_const, 16 * N_CONST)

            def f_mean(kk, par, c):
                if c == 0:
                    need(pe, s_x, 16, kk, 16)
                    need(pe, a_z, DT, kk - 1, 4)
                i = mm(F[0][:], ones_c[:], x_sb[:, c, :], start=(c == 0), stop=(c == KT - 1))
                if c == KT - 1:
                    i.then_inc(p_mean, 1)

            def f_var(kk, par, c):
                if c == 0:
                    need(pe, a_sq, 1, kk, 1)
                    need(pe, a_z, DT, kk - 1, 3)
                i = mm(F[1][:], ones_c[:], sq[:, c, :], start=(c == 0), stop=(c == KT - 1))
                if c == KT - 1:
                    i.then_inc(p_var, 1)

            def f_in(kk, par, piece):
                which, d, c = piece // (DT * KT), piece // KT % DT, piece % KT
                if piece == 0:
                    need(pe, a_xn, KT, kk, KT)
                    need(pe, s_win, 48, kk, 96 if par == 0 else 48)
                if c == 0:
                    if which == 0 and d >= 2:
                        need(pe, a_pre, DT, kk, d - 1)
                    if which == 1 and d == 0:
                        need(pe, a_dtx, DT, kk, 4)
                    if which == 1 and d == 1:
                        need(pe, v_ctok, 1, kk, 1)
                    if which == 1 and d >= 2:
                        need(pe, a_z, DT, kk, d - 1)
                o = which * DI + d * P
                i = mm(F[(d + 1) % 2][:], iw[:, c, o:o + P], xc[:, c, :], start=(c == 0), stop=(c == KT - 1))
                if c == KT - 1:
                    i.then_inc(p_ix if which == 0 else p_iz, 1)

            def f_conv(kk, par, d, tap):
                if tap == 0:
                    if d < 2:
                        need(pe, a_pre, DT, kk, d + 3)
                        if par == 0:
                            need(pe, a_tapw, DT // 2, kk, DT)
                    else:
                        need(pe, a_tap, DT, kk, d - 1)
                i = mm(F[(d + 1) % 2][:], tapw[:, d * TAPS + tap, :], xpre[:, d, tap:tap + T],
                       start=(tap == 0), stop=(tap == TAPS - 1))
                if tap == TAPS - 1:
                    i.then_inc(p_conv, 1)

            def f_proj(kk, par, d):
                if d == 0:
                    need(pe, a_tap, DT, kk, 3)
                need(pe, a_xin, 2, kk, d // 2 + 1)
                i = mm(F[1][0:BROW + DS, :], xw[:, d, :], xin[:, par, d, :], start=(d == 0), stop=(d == DT - 1))
                if d == DT - 1:
                    i.then_inc(p_proj, 1)

            def f_dt(kk, par, d):
                if d == 0:
                    need(pe, a_tap, DT, kk, 4)
                    need(pe, a_proj, 2, kk, 2)
                if d >= 2:
                    need(pe, a_dtx, DT, kk, d - 1)
                mm(F[d % 2][:], dtw[:, d * P:(d + 1) * P], pr[0:DTR + 1, par, :],
                   start=True, stop=True).then_inc(p_dt, 1)

            def f_ctok(kk, par, t):
                if t == 0:
                    need(pe, a_dtx, DT, kk, 3)
                for d in range(DT):
                    i = mm(F[0][:, t * DS:(t + 1) * DS], xin[:, par, d, t * P:(t + 1) * P], xwc[:, d, :],
                           start=(d == 0), stop=(d == DT - 1))
                if t == TT - 1:
                    i.then_inc(p_ctok, 1)

            def ht(k, n, t):
                if t == 0:
                    need(pe, v_scan, DT * DS, k, DT * n + DT)
                if n == 0 and t < 2:
                    need(pe, v_stt, STT, k - 1, STT - 1 + t)
                elif n == 0 or (n == 1 and t < 2):
                    need(pe, a_acc, TT, k, TT * n + t - 1)
                else:
                    need(pe, v_stt, STT, k, TT * (n - 1) + t - 1)
                for d in range(DT):
                    i = nc.tensor.transpose(TP[t % 2][:, d * P:(d + 1) * P], hbuf[:, n % 2, d, t * P:(t + 1) * P], ident[:])
                i.then_inc(p_ht, 1)

            def b_y(kk, par, d):
                if d == 0:
                    need(pe, v_stt, STT, kk, STT)
                    need(pe, v_xo, KT, kk - 1, KT)
                need(pe, v_yb, DT, kk, d)
                for t in range(TT):
                    i = nc.tensor.transpose(G[:, t * P:(t + 1) * P], acc[:, par, t, d * P:(d + 1) * P], ident[:])
                i.then_inc(p_y, 1)

            def b_out(kk, par, c, d):
                if c == 0:
                    need(pe, g_g, DT, kk, d + 1)
                    if d == 0:
                        need(pe, s_wout, 16, kk, 32 if par == 0 else 16)
                elif d == 0:
                    need(pe, v_xo, KT, kk, c)
                i = mm(G[:], ow[:, d, c * P:(c + 1) * P], yb[:, d, :], start=(d == 0), stop=(d == DT - 1))
                if d == DT - 1:
                    i.then_inc(p_out, 1)

            def front(quarter, kk, par):
                def piece(first, count):
                    i = quarter - first
                    return i if 0 <= i < count else None
                if (i := piece(at(0, 0), KT)) is not None: f_mean(kk, par, i)
                if quarter in (6, 7): f_var(kk, par, quarter - 6)
                if (i := piece(14, DT * KT)) is not None: f_in(kk, par, i)
                if 22 <= quarter < 34:
                    d, r = (quarter - 22) // 3, (quarter - 22) % 3
                    for tap in ((0,), (1,), (2, 3))[r]:
                        f_conv(kk, par, d, tap)
                if quarter in (34, 35, 38, 39): f_proj(kk, par, (34, 35, 38, 39).index(quarter))
                if quarter in (42, 43, 46, 47): f_dt(kk, par, (42, 43, 46, 47).index(quarter))
                if quarter in (48, 49):
                    for t in (2 * (quarter - 48), 2 * (quarter - 48) + 1):
                        f_ctok(kk, par, t)
                z_at = (51, 52, 53, 54, 56, 57, 58, 59)
                if quarter in z_at: f_in(kk, par, DT * KT + z_at.index(quarter))

            def back(quarter, kk, par):
                if quarter == at(1, 1): b_y(kk, par, 0)
                if quarter in (at(2, 0), at(2, 2), at(3, 0)): b_y(kk, par, (quarter - at(1, 2)) // 2)
                if quarter in (36, 37, 40, 41): b_out(kk, par, 0, (36, 37, 40, 41).index(quarter))
                if quarter in (44, 45, 50, 55): b_out(kk, par, 1, (44, 45, 50, 55).index(quarter))

            def step(k, par, first=False, last=False):
                for n in range(DS):
                    for q in range(TT):
                        if n >= 1:
                            ht(k, n - 1, q)
                        elif not first:
                            ht(k - 1, DS - 1, q)
                        if not last:
                            front(at(n, q), k + 1, 1 - par)
                        if not first:
                            back(at(n, q), k - 1, 1 - par)

            for s in range(DS):
                for q in range(TT):
                    front(at(s, q), 0, 0)
            step(0, 0, first=True)
            step(1, 1)
            with pe.Fori(1, IMAGES - 1) as j:
                step(2 * j, 0)
                step(2 * j + 1, 1)
            step(CHUNKS - 2, 0)
            step(CHUNKS - 1, 1, last=True)
            for q in range(TT):
                ht(CHUNKS - 1, DS - 1, q)
            for d in range(DT):
                b_y(CHUNKS - 1, 1, d)
            for c in range(KT):
                for d in range(DT):
                    b_out(CHUNKS - 1, 1, c, d)

        @block.scalar
        def _(act):
            av = nc.scalar.activation
            last_use = [max(g for g in range(DT * DS) if g % DAB == b) for b in range(DAB)]

            def pre(kk, par, d):
                if d == 0:
                    need(act, v_tail, 1, kk, 1)
                need(act, p_ix, DT, kk, d + 1)
                av(xpre[:, d, TAPS - 1:], F[(d + 1) % 2][:], ACT.Copy).then_inc(a_pre, 1)

            def build_taps(kk, d):
                if d == 0:
                    need(act, s_win, 48, kk, 96)
                    need(act, p_conv, DT, kk - 1, DT)
                for tap in range(TAPS):
                    cw = O_CW + d * TAPS + tap
                    i = av(tapw[:, d * TAPS + tap, :], ident[:], ACT.Copy, scale=small[:, cw:cw + 1])
                i.then_inc(a_tapw, 1)

            def conv_out(kk, par, d):
                if d == 0:
                    need(act, g_w, 2, kk - 1, 2)
                    need(act, a_l, 1, kk - 1, 1)
                need(act, p_conv, DT, kk, d + 1)
                av(cacc[:, d, :], F[(d + 1) % 2][:], ACT.Identity, bias=small[:, O_CB + d:O_CB + d + 1]).then_inc(a_tap, 1)

            def zcopy(kk, par, d):
                if d == 0:
                    need(act, g_g, DT, kk - 2, DT)
                need(act, p_iz, DT, kk, d + 1)
                av(sz[:, par, d, :], F[(d + 1) % 2][:], ACT.Copy).then_inc(a_z, 1)

            def dtcopy(kk, par, d):
                need(act, p_dt, DT, kk, d + 1)
                av(dtb[:, par, d, :], F[d % 2][:], ACT.Copy).then_inc(a_dtx, 1)

            def front(slot, q, kk, par):
                quarter = at(slot, q)
                if quarter == 4:
                    need(act, v_xc, KT, kk, KT)
                    av(sq[:], xc[:], ACT.Square).then_inc(a_sq, 1)
                if quarter == 11:
                    need(act, p_var, 1, kk, 1)
                    need(act, v_rs, 2, kk - 1, 2)
                    av(rs[:, 1, :], F[1][:], ACT.Ln, bias=eps[:, 0:1]).then_inc(a_rs, 1)
                    need(act, v_xh, KT, kk - 1, KT)
                    need(act, a_rs, 3, kk, 1)
                    av(rs[:, 0, :], rs[:, 1, :], ACT.Exp, scale=-0.5).then_inc(a_rs, 1)
                    need(act, a_rs, 3, kk, 2)
                    av(rs[:, 1, :], rs[:, 0, :], ACT.Square, scale=0.5 ** 0.5).then_inc(a_rs, 1)
                if quarter == 14:
                    need(act, s_win, 48, kk, 96 if par == 0 else 48)
                    for c in range(KT):
                        need(act, v_xh, KT, kk, c + 1)
                        av(xc[:, c, :], xc[:, c, :], ACT.Identity, scale=small[:, O_LW + c:O_LW + c + 1],
                           bias=small[:, O_LB + c:O_LB + c + 1]).then_inc(a_xn, 1)
                if par == 0 and quarter in (15, 16, 17, 19): build_taps(kk, (15, 16, 17, 19).index(quarter))
                if quarter in (18, 20, 22, 24): pre(kk, par, (quarter - 18) // 2)
                if quarter in (27, 30, 33, 36): conv_out(kk, par, (quarter - 27) // 3)
                if quarter in (31, 37):
                    r = (quarter - 31) // 6
                    need(act, a_tap, DT, kk, 2 * r + 2)
                    if r == 0:
                        need(act, v_yb, DT, kk - 2, DT)
                        need(act, g_u, 1, kk - 2, 1)
                    av(xin[:, par, 2 * r:2 * r + 2, :], cacc[:, 2 * r:2 * r + 2, :], ACT.Silu).then_inc(a_xin, 1)
                if quarter in (45, 46, 48, 49): dtcopy(kk, par, (45, 46, 48, 49).index(quarter))
                if quarter in (55, 57, 60, 62): zcopy(kk, par, (55, 57, 60, 62).index(quarter))
                if quarter == 42:
                    need(act, p_proj, 1, kk, 1)
                    av(pr[0:DTR, par, :], F[1][0:DTR, :], ACT.Copy).then_inc(a_proj, 1)
                    av(pr[BROW:BROW + DS, par, :], F[1][BROW:BROW + DS, :], ACT.Copy).then_inc(a_proj, 1)
                if quarter == 50:
                    need(act, a_dtx, DT, kk, DT)
                    need(act, v_dt, 2, kk - 1, 1)
                    av(spw[:], dtb[:, par, :, :], ACT.Abs).then_inc(a_abs, 1)
                if quarter == 51:
                    need(act, a_abs, 1, kk, 1)
                    av(cacc[:], spw[:], ACT.Exp, scale=-1.0).then_inc(a_e, 1)
                if quarter == 53:
                    need(act, a_e, 1, kk, 1)
                    av(spw[:], cacc[:], ACT.Ln, bias=1.0).then_inc(a_l, 1)
                if quarter == 63:
                    need(act, a_z, DT, kk, DT)
                    av(sz[:, par, :, :], sz[:, par, :, :], ACT.Silu).then_inc(a_sz, 1)
                if quarter == 61 and par == 0:
                    need(act, s_win, 48, kk, 96)
                    av(aexp[:], small[:, O_AL:O_AL + DT * DS], ACT.Exp).then_inc(a_amat, 1)

            def decay(k, par, n, d):
                if n == 0 and d == 0:
                    if par == 0:
                        need(act, a_amat, 1, k, 1)
                        need(act, a_da, DT * DS, k - 1, DT * DS)
                        av(amat[:], aexp[:], ACT.Copy, scale=-1.0).then_inc(a_amat, 1)
                        need(act, a_amat, 1, k, 2)
                    need(act, v_dt, 2, k, 2)
                g = DT * n + d
                need(act, v_scan, DT * DS, k, g - DAB + 1 if g >= DAB else last_use[g] + 1 - DT * DS)
                av(DA[g % DAB][:], dtb[:, par, d, :], ACT.Exp, scale=amat[:, d * DS + n:d * DS + n + 1]).then_inc(a_da, 1)

            def acc0(k, par, t):
                if t == 0:
                    need(act, v_ctok, 1, k, 1)
                    need(act, p_y, DT, k - 2, DT)
                need(act, p_ht, DT * DS, k, t + 1)
                av(acc[:, par, t, :], TP[t % 2][:], ACT.Copy, scale=ctok[:, par, t, 0:1]).then_inc(a_acc, 1)

            def step(k, par, first=False, last=False):
                for n in range(DS):
                    for q in range(DT):
                        decay(k, par, n, q)
                        if 0 <= at(n, q) - at(1, 2) < TT:
                            acc0(k, par, at(n, q) - at(1, 2))
                        if not last:
                            front(n, q, k + 1, 1 - par)

            act.wait_ge(s_init, 4)
            av(ln_one[:], ln_one[:], ACT.Ln, bias=1.0).then_inc(s_init, 1)
            for s in range(DS):
                for q in range(DT):
                    front(s, q, 0, 0)
            step(0, 0, first=True)
            step(1, 1)
            with act.Fori(1, IMAGES - 1) as j:
                step(2 * j, 0)
                step(2 * j + 1, 1)
            step(CHUNKS - 2, 0)
            step(CHUNKS - 1, 1, last=True)

        @block.vector
        def _(dve):
            v = nc.vector
            v.memset(xw[:], 0.0).then_inc(s_init, 1)
            v.memset(pr[:], 1.0).then_inc(s_init, 1)
            v.memset(ln_one[:], 0.0).then_inc(s_init, 1)
            v.memset(eps[:], LN_EPS).then_inc(s_init, 1)
            v.memset(xpre[:, :, 0:TAPS - 1], 0.0).then_inc(v_tail, 1)
            dve.wait_ge(s_const, 16 * N_CONST)

            def front(slot, q, kk, par):
                quarter = at(slot, q)
                if quarter == 2:
                    need(dve, p_mean, 1, kk, 1)
                    need(dve, p_iz, DT, kk - 1, DT)
                    for c in range(KT):
                        v.tensor_tensor(xc[:, c, :], F[0][:], x_sb[:, c, :], ALU.subtract).then_inc(v_xc, 1)
                if quarter == 11:
                    need(dve, a_rs, 3, kk, 3)
                    v.scalar_tensor_tensor(rs[:, 1, :], F[1][:], LN_EPS, rs[:, 1, :], ALU.add, ALU.mult).then_inc(v_rs, 1)
                    need(dve, v_rs, 2, kk, 1)
                    v.scalar_tensor_tensor(F[0][:], rs[:, 1, :], 1.5, rs[:, 0, :], ALU.subtract, ALU.mult).then_inc(v_rs, 1)
                if quarter == 12:
                    need(dve, v_rs, 2, kk, 2)
                    need(dve, a_sq, 1, kk, 1)
                    for c in range(KT):
                        v.tensor_tensor(xc[:, c, :], xc[:, c, :], F[0][:], ALU.mult).then_inc(v_xh, 1)
                if quarter == 35:
                    need(dve, p_conv, DT, kk, DT)
                    need(dve, v_tail, 1, kk, 1)
                    if par == 0:
                        v.tensor_copy(xpre[:, :, 0:TAPS - 1], xpre[:, :, T:T + TAPS - 1]).then_inc(v_tail, 1)
                    else:
                        v.memset(xpre[:, :, 0:TAPS - 1], 0.0).then_inc(v_tail, 1)
                if quarter == 50:
                    need(dve, p_ctok, 1, kk, 1)
                    v.tensor_copy(ctok[:, par, :, :], F[0][:, 0:TT * DS].rearrange("p (a b) -> p a b", b=DS)).then_inc(v_ctok, 1)
                if quarter == 52:
                    need(dve, a_e, 1, kk, 1)
                    need(dve, g_bu, DS, kk - 2, DS)
                    v.tensor_scalar(ub[:, par, :, :], cacc[:], 1.0, -1.0, ALU.add, ALU.add).then_inc(v_w1, 1)
                if quarter == 55:
                    need(dve, a_l, 1, kk, 1)
                    flat = dtb[:, par, :, :].rearrange("p a b -> p (a b)")
                    v.scalar_tensor_tensor(flat, flat, 0.0, spw[:].rearrange("p a b -> p (a b)"), ALU.max, ALU.add).then_inc(v_dt, 1)
                if quarter == 59:
                    need(dve, v_dt, 2, kk, 1)
                    need(dve, g_w, 2, kk, 2)
                    flat = dtb[:, par, :, :].rearrange("p a b -> p (a b)")
                    v.scalar_tensor_tensor(flat, flat, ln_one[:, 0:1], ub[:, par, :, :].rearrange("p a b -> p (a b)"),
                                           ALU.subtract, ALU.add).then_inc(v_dt, 1)

            def scan(k, par, n, d):
                need(dve, a_da, DT * DS, k, DT * n + d + 1)
                if d == 0:
                    need(dve, g_bu, DS, k, n + 1)
                    need(dve, p_ht, DT * DS, k, TT * (n - 2) + TT)
                init = 0.0 if par == 0 else carry[:, n, d:d + 1]
                v.tensor_tensor_scan(hbuf[:, n % 2, d, :], DA[(DT * n + d) % DAB][:], dbu[:, n % 2, d, :], init,
                                     ALU.mult, ALU.add).then_inc(v_scan, 1)

            def stt(k, par, n, t):
                need(dve, p_ht, DT * DS, k, TT * n + t + 1)
                if n == 1:
                    need(dve, a_acc, TT, k, t + 1)
                else:
                    need(dve, v_stt, STT, k, TT * (n - 2) + t + 1)
                v.scalar_tensor_tensor(acc[:, par, t, :], TP[t % 2][:], ctok[:, par, t, n:n + 1], acc[:, par, t, :],
                                       ALU.mult, ALU.add).then_inc(v_stt, 1)

            def save(k, n):
                need(dve, v_scan, DT * DS, k, DT * n + DT)
                v.tensor_copy(carry[:, n, :], hbuf[:, n % 2, :, T - 1:T].rearrange("p a b -> p (a b)")).then_inc(v_carry, 1)

            def b_yb(kk, par, d):
                if d == 0:
                    need(dve, s_wout, 16, kk, 32 if par == 0 else 16)
                    need(dve, p_out, KT, kk - 1, KT)
                need(dve, p_y, DT, kk, d + 1)
                v.scalar_tensor_tensor(yb[:, d, :], xin[:, par, d, :], dskip[:, d:d + 1], G[:],
                                       ALU.mult, ALU.add).then_inc(v_yb, 1)

            def b_xo(kk, c):
                if c == 0:
                    need(dve, s_xres, 16, kk, 16)
                need(dve, p_out, KT, kk, c + 1)
                v.tensor_tensor(xo[:, c, :], xo[:, c, :], G[:], ALU.add).then_inc(v_xo, 1)

            def back(slot, q, kk, par):
                quarter = at(slot, q)
                if quarter in (at(1, 3), at(2, 1), at(2, 3), at(3, 1)): b_yb(kk, par, (quarter - at(1, 3)) // 2)
                if quarter == 42: b_xo(kk, 0)
                if quarter == 57: b_xo(kk, 1)

            def step(k, par, first=False, last=False):
                for n in range(DS):
                    for q in range(DT):
                        if n == 0 and q == 0 and par == 1:
                            need(dve, v_carry, DS // 2, k, DS // 2)
                        if n == 0 and not first and q < TT - 2:
                            if q == 0:
                                stt(k - 1, 1 - par, DS - 1, 0)
                            stt(k - 1, 1 - par, DS - 1, q + 1)
                        scan(k, par, n, q)
                        if n >= 2:
                            stt(k, par, n - 1, q)
                        elif n == 0 and not first and q == TT - 2:
                            stt(k - 1, 1 - par, DS - 1, TT - 1)
                        if not first:
                            back(n, q, k - 1, 1 - par)
                        if not last:
                            front(n, q, k + 1, 1 - par)
                    if par == 0:
                        save(k, n)

            for s in range(DS):
                for q in range(DT):
                    front(s, q, 0, 0)
            step(0, 0, first=True)
            step(1, 1)
            with dve.Fori(1, IMAGES - 1) as j:
                step(2 * j, 0)
                step(2 * j + 1, 1)
            step(CHUNKS - 2, 0)
            step(CHUNKS - 1, 1, last=True)
            for t in range(TT):
                stt(CHUNKS - 1, 1, DS - 1, t)
            for d in range(DT):
                b_yb(CHUNKS - 1, 1, d)
            for c in range(KT):
                b_xo(CHUNKS - 1, c)

        @block.gpsimd
        def _(pool):
            tt = nc.gpsimd.tensor_tensor

            def rounding(kk, par, r):
                need(pool, v_w1, 1, kk, 1)
                t2 = slice(2 * r, 2 * r + 2)
                tt(ub[:, par, t2, :], cacc[:, t2, :], ub[:, par, t2, :], ALU.subtract).then_inc(g_w, 1)

            def dt_x(kk, par):
                need(pool, v_dt, 2, kk, 2)
                tt(ub[:, par, :, :], dtb[:, par, :, :], xin[:, par, :, :], ALU.mult).then_inc(g_u, 1)

            def bu(k, par, n):
                if n == 0:
                    need(pool, g_u, 1, k, 1)
                need(pool, s_row[n % RING], 16 * DS // RING, k, 16 * (n // RING + 1))
                need(pool, v_scan, DT * DS, k, DT * (n - 2) + DT)
                tt(dbu[:, n % 2, :, :], ub[:, par, :, :], bbc[:, n % RING, None, :].to_broadcast([P, DT, T]), ALU.mult).then_inc(g_bu, 1)

            def gate(kk, par, d):
                need(pool, v_yb, DT, kk, DT)
                need(pool, a_sz, 1, kk, 1)
                tt(yb[:, d, :], yb[:, d, :], sz[:, par, d, :], ALU.mult).then_inc(g_g, 1)

            def step(k, par, first=False, last=False):
                for n in range(DS):
                    bu(k, par, n)
                    if not first and 4 <= n < 4 + DT:
                        gate(k - 1, 1 - par, n - 4)
                    if not last and n in (13, 14):
                        rounding(k + 1, 1 - par, n - 13)
                    if not last and n == 15:
                        dt_x(k + 1, 1 - par)

            rounding(0, 0, 0)
            rounding(0, 0, 1)
            dt_x(0, 0)
            step(0, 0, first=True)
            step(1, 1)
            with pool.Fori(1, IMAGES - 1) as j:
                step(2 * j, 0)
                step(2 * j + 1, 1)
            step(CHUNKS - 2, 0)
            step(CHUNKS - 1, 1, last=True)
            for d in range(DT):
                gate(CHUNKS - 1, 1, d)
def gate_and_norm(nc, state, w, out):
    HS = C // 4
    SL = N // 512
    ctx = ExitStack()
    with ctx:
        def sb(n, s):
            return ctx.enter_context(nc.sbuf_tensor("c_" + n, s, F32))

        def sem(n):
            return ctx.enter_context(nc.semaphore("c_" + n))

        y = sb("y", [P, B, KT, N])
        res = sb("res", [P, 4, KT, N])
        w1 = sb("w1", [P, KT, HS])
        w2 = sb("w2", [HS, C])
        b1 = sb("b1", [HS, 1])
        vec = sb("vec", [P, 3, KT])
        gsum = sb("gsum", [P, KT, B])
        hid = sb("hid", [HS, B])
        gate = sb("gate", [P, KT, B])
        stats = sb("stats", [P, KT, B * SL, 6])
        agg = sb("agg", [P, KT, 2])
        tmp = sb("tmp", [P, 6, KT])
        pz = ctx.enter_context(nc.psum_tensor("c_pz", [P, 64], F32))

        s_w, s_st = sem("weights"), sem("store_done")
        s_x = [sem("x%d" % b) for b in range(B)]
        s_r = [sem("res%d" % b) for b in range(4)]
        v_sum, p_h, a_h, p_g, a_g, v_y, v_bn, v_agg, v_tmp, a_tmp, v_out = (sem(n) for n in (
            "sum", "hid_ps", "hid", "gate_ps", "gate", "y", "bn", "agg", "tmp", "lnexp", "out"))
        st_v = state.rearrange("i (k p) n -> i p k n", p=P)
        out_v = out.rearrange("b (k p) n -> b p k n", p=P)
        block = ctx.enter_context(nc.Block())

        @block.sync
        def _(sp):
            for b in range(B):
                sp.dma_start(y[:, b], st_v[IMAGES + b]).then_inc(s_x[b], 16)
            for dst, name in ((w1[:], "w1"), (w2[:], "w2"), (b1[:], "b1"), (vec[:], "vec")):
                sp.dma_start(dst, w[name]).then_inc(s_w, 16)
            for b in range(B):
                if b >= 4:
                    sp.wait_ge(v_y, KT * (b - 3))
                sp.dma_start(res[:, b % 4], st_v[b]).then_inc(s_r[b % 4], 16)
            for b in range(B):
                sp.wait_ge(v_out, KT * (b + 1))
                sp.dma_start(out_v[b], y[:, b]).then_inc(s_st, 16)
            sp.wait_ge(s_st, 16 * B)

        @block.tensor
        def _(pe):
            pe.wait_ge(s_w, 64)
            pe.wait_ge(v_sum, B * KT)
            for c in range(KT):
                i = nc.tensor.matmul(pz[0:HS, 0:B], w1[:, c, :], gsum[:, c, :], start=(c == 0), stop=(c == KT - 1))
            i.then_inc(p_h, 1)
            pe.wait_ge(a_h, 1)
            for c in range(KT):
                i = nc.tensor.matmul(pz[:, 16 + c * B:16 + (c + 1) * B], w2[:, c * P:(c + 1) * P], hid[:], start=True, stop=True)
            i.then_inc(p_g, 1)

        @block.scalar
        def _(act):
            av = nc.scalar.activation
            act.wait_ge(p_h, 1)
            av(hid[:], pz[0:HS, 0:B], ACT.Relu, scale=1.0 / N, bias=b1[:, 0:1]).then_inc(a_h, 1)
            act.wait_ge(p_g, 1)
            for c in range(KT):
                av(gate[:, c, :], pz[:, 16 + c * B:16 + (c + 1) * B], ACT.Sigmoid, bias=vec[:, 0, c:c + 1]).then_inc(a_g, 1)
            act.wait_ge(v_tmp, 1)
            av(tmp[:, 1, :], tmp[:, 0, :], ACT.Ln).then_inc(a_tmp, 1)
            act.wait_ge(a_tmp, 1)
            av(tmp[:, 2, :], tmp[:, 1, :], ACT.Exp, scale=-0.5).then_inc(a_tmp, 1)

        def stats_of(dve, b):
            for c in range(KT):
                dve.wait_ge(v_y, KT * b + c + 1)
                for s in range(SL):
                    nc.vector.bn_stats(stats[:, c, b * SL + s, :], y[:, b, c, s * 512:(s + 1) * 512]).then_inc(v_bn, 1)

        @block.vector
        def _(dve):
            v = nc.vector
            for b in range(B):
                dve.wait_ge(s_x[b], 16)
                for c in range(KT):
                    v.reduce_sum(gsum[:, c, b:b + 1], y[:, b, c, :], mybir.AxisListType.X).then_inc(v_sum, 1)
            dve.wait_ge(a_g, KT)
            for b in range(B):
                dve.wait_ge(s_r[b % 4], 16 * (b // 4 + 1))
                for c in range(KT):
                    v.scalar_tensor_tensor(y[:, b, c, :], y[:, b, c, :], gate[:, c, b:b + 1], res[:, b % 4, c, :],
                                           ALU.mult, ALU.add).then_inc(v_y, 1)
                if b:
                    stats_of(dve, b - 1)
            stats_of(dve, B - 1)
            dve.wait_ge(v_bn, B * KT * SL)
            for c in range(KT):
                v.bn_aggr(agg[:, c, :], stats[:, c, :, :].rearrange("p a b -> p (a b)")).then_inc(v_agg, 1)
            dve.wait_ge(v_agg, KT)
            n = [0]

            def link(i):
                n[0] += 1
                i.then_inc(v_tmp, 1)
                dve.wait_ge(v_tmp, n[0])
            link(v.tensor_scalar(tmp[:, 0, :], agg[:, :, 1], LN_EPS, None, ALU.add))
            dve.wait_ge(a_tmp, 2)
            link(v.tensor_tensor(tmp[:, 3, :], tmp[:, 2, :], tmp[:, 2, :], ALU.mult))
            link(v.scalar_tensor_tensor(tmp[:, 1, :], tmp[:, 3, :], -0.5, tmp[:, 0, :], ALU.mult, ALU.mult))
            link(v.scalar_tensor_tensor(tmp[:, 3, :], tmp[:, 1, :], 1.5, tmp[:, 2, :], ALU.add, ALU.mult))
            link(v.tensor_tensor(tmp[:, 4, :], tmp[:, 3, :], vec[:, 1, :], ALU.mult))
            link(v.tensor_tensor(tmp[:, 5, :], tmp[:, 4, :], agg[:, :, 0], ALU.mult))
            link(v.tensor_tensor(tmp[:, 5, :], vec[:, 2, :], tmp[:, 5, :], ALU.subtract))
            for b in range(B):
                for c in range(KT):
                    v.tensor_scalar(y[:, b, c, :], y[:, b, c, :], tmp[:, 4, c:c + 1], tmp[:, 5, c:c + 1],
                                    ALU.mult, ALU.add).then_inc(v_out, 1)


def constants():
    return {
        "ident": np.eye(P, dtype=np.float32),
        "ones_c": np.full((P, P), 1.0 / C, np.float32),
        "ones": np.ones((P, P), np.float32),
    }


def chan(a, tiles):
    a = a.reshape(a.shape[0], tiles, P, -1)
    return np.ascontiguousarray(a.transpose(0, 2, 1, 3))


def mamba_weights(inp):
    g = {k[len("L1_conv_"):]: np.asarray(v) for k, v in inp.items() if k.startswith("L1_conv_")}
    xw = g["x_proj_w"].transpose(0, 2, 1)
    xw_t = chan(xw, DT)
    small = np.concatenate([
        chan(g["conv_w"], DT).reshape(NL, P, -1), chan(g["conv_b"], DT).reshape(NL, P, -1),
        chan(g["A_log"], DT).reshape(NL, P, -1), chan(g["ln_w"], KT).reshape(NL, P, -1),
        chan(g["ln_b"], KT).reshape(NL, P, -1)], axis=2)
    return {
        "iw": chan(g["in_proj_w"].transpose(0, 2, 1), KT),
        "xw_dt": np.ascontiguousarray(xw_t[..., 0:DTR]),
        "xw_b": np.ascontiguousarray(xw_t[..., DTR:DTR + DS]),
        "xw_c": np.ascontiguousarray(xw_t[..., DTR + DS:]),
        "small": np.ascontiguousarray(small),
        "dw": np.ascontiguousarray(np.concatenate([g["dt_proj_w"].transpose(0, 2, 1), g["dt_proj_b"][:, None, :]], axis=1)),
        "ow": chan(g["out_proj_w"].transpose(0, 2, 1), DT),
        "dskip": chan(g["D"], DT).reshape(NL, P, DT),
    }


def patch_basis():
    yy, xx = np.meshgrid(np.arange(8), np.arange(8), indexing="ij")
    basis, weight, picks = [], [], []
    for kx in range(5):
        for ky in range(8):
            edge = kx in (0, 4)
            if edge and ky > 4:
                continue
            phase = (2 * np.pi / 8) * ((ky * yy + kx * xx) % 8)
            keys = {(ky, kx), ((8 - ky) % 8, kx)} if edge else {(ky, kx)}
            for f in ((np.cos,) if edge and ky in (0, 4) else (np.cos, np.sin)):
                basis.append(f(phase).reshape(64))
                weight.append((1.0 if edge else 2.0) / 64)
                picks.append(keys)
    return np.array(basis), np.array(weight), picks


def fft_constants():
    basis, weight, picks = patch_basis()
    dft = np.zeros((P, P), np.float32)
    idft = np.zeros((P, P), np.float32)
    for patch in range(2):
        tok = (np.arange(8)[:, None] * 16 + patch * 8 + np.arange(8)[None, :]).reshape(64)
        fr = patch * 64 + np.arange(64)
        dft[np.ix_(tok, fr)] = basis.T
        idft[np.ix_(fr, tok)] = basis * weight[:, None]
    fsel = np.zeros((40, P), np.float32)
    for f, keys in enumerate(picks):
        for ky, kx in keys:
            fsel[ky * 5 + kx, [f, 64 + f]] = 1.0
    return {"dft": dft, "idft": idft, "fsel": fsel}


def rows(a, tiles):
    return np.ascontiguousarray(a.reshape(tiles, P, -1).transpose(1, 0, 2))


def conv_weights(inp):
    g = {k[len("L0_conv_"):]: np.asarray(v) for k, v in inp.items() if k.startswith("L0_conv_")}
    heads = np.arange(NH)[:, None] * (2 * KD + HD)
    order = np.concatenate([(heads + np.arange(KD)).reshape(-1), (heads + KD + np.arange(KD)).reshape(-1),
                            (heads + 2 * KD + np.arange(HD)).reshape(-1)])
    par = [np.concatenate([g["qkv_" + s][order], g["pe_" + s], g["proj_" + s]]) for s in "gbmv"]
    bn = np.stack(par)
    vec = np.stack([g[k].reshape(C) for k in ("norm1_w", "norm1_b", "norm2_w", "norm2_b", "gamma1", "gamma2")])
    return {
        "qkv": rows(g["qkv_w"][order].T, KT),
        "proj": rows(g["proj_w"].T, KT),
        "pi": rows(g["pi_w"].T, KT),
        "po": rows(g["po_w"].T, HT),
        "bn": np.ascontiguousarray(bn.reshape(4, 8, P).transpose(2, 0, 1)),
        "vec": np.ascontiguousarray(vec.reshape(6, KT, P).transpose(2, 0, 1)),
        "pe": rows(g["pe_w"].reshape(C, 9), KT),
        "dw": rows(g["dw_w"].reshape(2 * HID, 9), 2 * HT),
        "fftp": np.ascontiguousarray(g["fft_p"].reshape(C, 40).T),
    }


def gate_weights(inp):
    g = {k[len("L1_conv_"):]: np.asarray(v) for k, v in inp.items() if k.startswith("L1_conv_")}
    vec = np.stack([g["se_b2"], g["bn_w"], g["bn_b"]])
    return {
        "w1": rows(g["se_w1"].T, KT),
        "w2": np.ascontiguousarray(g["se_w2"].T),
        "b1": g["se_b1"].reshape(C // 4, 1),
        "vec": np.ascontiguousarray(vec.reshape(3, KT, P).transpose(2, 0, 1)),
    }


def build(nc, args):
    state = nc.dram_tensor("state", (IMAGES + B, C, N), F32, kind="Internal").ap()
    conv_block(nc, args["x"], state, args["conv"], args["const"])
    mamba_layers(nc, state, args["mamba"], args["const"])
    gate_and_norm(nc, state, args["gate"], args["out"])


def kernel(**inputs):
    import concourse.bacc as _bacc
    from concourse.bass_utils import run_bass_kernel_spmd as _run

    nc = _bacc.Bacc("TRN2", target_bir_lowering=False, num_devices=1)
    arrays = {}

    def dram(name, a):
        a = np.ascontiguousarray(a)
        arrays[name] = a
        return nc.dram_tensor(name, a.shape, F32, kind="ExternalInput").ap()

    args = {"x": dram("x", np.asarray(inputs["x"]).reshape(B, C, N))}
    for group, parts in (("conv", conv_weights(inputs)), ("mamba", mamba_weights(inputs)), ("gate", gate_weights(inputs)),
                         ("const", {**constants(), **fft_constants()})):
        args[group] = {k: dram(group + "_" + k, v) for k, v in parts.items()}
    out = nc.dram_tensor("out", (B, C, H, W), F32, kind="ExternalOutput").ap()
    args["out"] = out.rearrange("b c h w -> b c (h w)")
    build(nc, args)
    r = _run(nc, [arrays], core_ids=[0])
    return r.results[0]["out"]
```
